# Optimizing a Trainium2 kernel written in Bass

```python
import numpy as np
import jax
import jax.numpy as jnp

def _softmax(x, axis=-1):
    return jax.nn.softmax(x, axis=axis)

def _gelu(x):
    return jax.nn.gelu(x, approximate=True)

def _silu(x):
    return jax.nn.silu(x)

def _sigmoid(x):
    return jax.nn.sigmoid(x)

def _layernorm(x, axis=-1, eps=1e-05):
    m = jnp.mean(x, axis=axis, keepdims=True)
    v = jnp.var(x, axis=axis, keepdims=True)
    return (x - m) / jnp.sqrt(v + eps)

def _scatter_add(tgt, idx, src, axis=0):
    return tgt.at[idx].add(src)

def _segment_sum(src, seg, n):
    return jax.ops.segment_sum(src, seg, n)
kernel_name = 'mk_adaln_ffn_d4_seqx_r4_0440f0'

def setup_inputs(seed: int=0):
    np.random.seed(seed)
    _w = jnp.asarray

    def _rec_inputs():
        import jax
        import jax.numpy as jnp
        _rk = jax.random.key(seed)
        x = -0.0003929 + 0.9999 * jax.random.normal(jax.random.fold_in(_rk, 1), (64, 64, 256), jnp.float32)
        _lenS = 64 - jax.random.randint(jax.random.fold_in(_rk, 7), (64,), 0, max(1, 64 // 4) + 1, jnp.int32)
        _lenS2 = 64 - jax.random.randint(jax.random.fold_in(_rk, 8), (64,), 0, max(1, 64 // 4) + 1, jnp.int32)
        itok_B_0_7 = jax.random.randint(jax.random.fold_in(_rk, 11), (64,), 0, 8, jnp.int32)
        condB_zX = jax.random.uniform(jax.random.fold_in(_rk, 12), (64,), jnp.float32, 0.0, 0.983423)
        condB_zY = jax.random.uniform(jax.random.fold_in(_rk, 13), (64,), jnp.float32, 0.0, 0.979075)
        condB_zR = jax.random.uniform(jax.random.fold_in(_rk, 14), (64,), jnp.float32, 0.0, 0.9968)
        itok_B_0_30 = jax.random.randint(jax.random.fold_in(_rk, 15), (64,), 0, 31, jnp.int32)
        return (x, itok_B_0_7, condB_zX, condB_zY, condB_zR, itok_B_0_30)
    x, itok_B_0_7, condB_zX, condB_zY, condB_zR, itok_B_0_30 = _rec_inputs()

    def _L0_cond_setup():
        import jax, jax.numpy as jnp
        import numpy as np
        S, O, H = (8, 256, 256)
        B, N = (32, 128)
        key = jax.random.key(seed)
        k1, k2, k3, k4 = jax.random.split(key, 4)
        x = jax.random.normal(k1, (B, N, H), dtype=jnp.float32)
        subject_id = jax.random.randint(k2, (B,), 0, S)
        wbound = jnp.sqrt(2.0 / 6.0) * jnp.sqrt(3.0 / H)
        weight = jax.random.uniform(k3, (S, O, H), minval=-wbound, maxval=wbound, dtype=jnp.float32)
        bbound = 1.0 / jnp.sqrt(H)
        bias = jax.random.uniform(k4, (S, O), minval=-bbound, maxval=bbound, dtype=jnp.float32)
        return {'x': x, 'subject_id': subject_id, 'weight': weight, 'bias': bias}
    _L0_cond_all = _L0_cond_setup()
    _L0_cond_in = {k: v for k, v in _L0_cond_all.items() if k in ('weight', 'bias')}
    del _L0_cond_all

    def _L0_ffn_setup():
        import jax, jax.numpy as jnp
        import numpy as np
        B, S, DIM = (4, 1024, 256)
        BASE_COUPLING = 0.1
        NUM_CYCLES = 3

        def _gelu(x):
            return jax.nn.gelu(x, approximate=False)

        def _coupling_net(h, w1, b1, w2, b2, w3, b3, w4, b4):
            h = _gelu(h @ w1 + b1)
            h = _gelu(h @ w2 + b2)
            h = _gelu(h @ w3 + b3)
            return jax.nn.sigmoid(h @ w4 + b4)

        def _global_net(h, w1, b1, w2, b2, w3, b3):
            h = _gelu(h @ w1 + b1)
            h = _gelu(h @ w2 + b2)
            return jax.nn.sigmoid(h @ w3 + b3)

        def _twist(x):
            o_r, o_i, p_r, p_i = jnp.split(x, 4, axis=-1)
            return jnp.concatenate([p_r, -p_i, -o_r, o_i], axis=-1)
        key = jax.random.key(seed)
        ks = jax.random.split(key, 9)
        d = DIM

        def w(k, fan_in, fan_out):
            return jax.random.normal(k, (fan_in, fan_out), dtype=jnp.float32) / np.sqrt(fan_in).astype(np.float32)
        inp = {'x': jax.random.normal(ks[0], (B, S, d), dtype=jnp.float32)}
        cn_dims = [(d, d), (d, d // 2), (d // 2, d // 4), (d // 4, 1)]
        for i, (a, b) in enumerate(cn_dims):
            inp[f'cn_w{i + 1}'] = w(ks[1 + i], a, b)
            inp[f'cn_b{i + 1}'] = jnp.zeros((b,), dtype=jnp.float32)
        gc_dims = [(d, d // 2), (d // 2, d // 4), (d // 4, 1)]
        for i, (a, b) in enumerate(gc_dims):
            inp[f'gc_w{i + 1}'] = w(ks[5 + i], a, b)
            inp[f'gc_b{i + 1}'] = jnp.zeros((b,), dtype=jnp.float32)
        inp['adaptive_range'] = jnp.full((1,), 0.2, dtype=jnp.float32)
        return inp
    _L0_ffn_all = _L0_ffn_setup()
    _L0_ffn_in = {k: v for k, v in _L0_ffn_all.items() if k in ('cn_w1', 'cn_b1', 'cn_w2', 'cn_b2', 'cn_w3', 'cn_b3', 'cn_w4', 'cn_b4', 'gc_w1', 'gc_b1', 'gc_w2', 'gc_b2', 'gc_w3', 'gc_b3', 'adaptive_range')}
    del _L0_ffn_all

    def _L1_cond_setup():
        import jax, jax.numpy as jnp
        import numpy as np
        key = jax.random.key(seed)
        k1, k2, k3, k4 = jax.random.split(key, 4)
        B, H, W = (64, 256, 256)
        return {'y': jax.random.uniform(k1, (B, H, W), dtype=jnp.float32), 'zX': jax.random.uniform(k2, (B, 1), dtype=jnp.float32), 'zY': jax.random.uniform(k3, (B, 1), dtype=jnp.float32), 'zR': jax.random.uniform(k4, (B, 1), dtype=jnp.float32), 'dx': 1, 'dy': 1}
    _L1_cond_all = _L1_cond_setup()
    _L1_cond_in = {k: v for k, v in _L1_cond_all.items() if k in ()}
    del _L1_cond_all

    def _L1_ffn_setup():
        import jax, jax.numpy as jnp
        import numpy as np

        def _ste(w, w_q):
            return w + jax.lax.stop_gradient(w_q - w)

        def quantize_w8_per(w, axis):
            amax = jnp.clip(jnp.max(jnp.abs(w), axis=axis, keepdims=True), 1e-08, None)
            scale = 127.0 / amax
            w_q = jnp.clip(jnp.round(w * scale), -128.0, 127.0) / scale
            return _ste(w, w_q)

        def quantize_a16(x):
            amax = jnp.clip(jnp.max(jnp.abs(x)), 1e-08, None)
            scale = 32767.0 / amax
            x_q = jnp.clip(jnp.round(x * scale), -32768.0, 32767.0) / scale
            return _ste(x, x_q)
        key = jax.random.key(seed)
        k1, k2, k3 = jax.random.split(key, 3)
        d_model, d_ff = (256, 1024)
        x = jax.random.normal(k1, (4, 512, d_model), dtype=jnp.float32)
        W_in = jax.random.normal(k2, (d_model, d_ff), dtype=jnp.float32) / np.sqrt(d_model)
        b_in = jnp.zeros((d_ff,), dtype=jnp.float32)
        W_out = jax.random.normal(k3, (d_ff, d_model), dtype=jnp.float32) / np.sqrt(d_ff)
        b_out = jnp.zeros((d_model,), dtype=jnp.float32)
        return {'x': x, 'W_in': W_in, 'b_in': b_in, 'W_out': W_out, 'b_out': b_out}
    _L1_ffn_all = _L1_ffn_setup()
    _L1_ffn_in = {k: v for k, v in _L1_ffn_all.items() if k in ('W_in', 'b_in', 'W_out', 'b_out')}
    del _L1_ffn_all

    def _L2_cond_setup():
        import jax, jax.numpy as jnp
        import numpy as np
        C, I, O = (32, 256, 256)
        B, T = (64, 128)
        key = jax.random.key(seed)
        kx, kc, kw, kb = jax.random.split(key, 4)
        x = jax.random.normal(kx, (B, T, I), dtype=jnp.float32)
        cat_ids = jax.random.randint(kc, (B,), 0, C)
        W = 0.02 * jax.random.normal(kw, (C, I, O), dtype=jnp.float32)
        b = jnp.zeros((C, O), dtype=jnp.float32)
        return {'x': x, 'cat_ids': cat_ids, 'W': W, 'b': b}
    _L2_cond_all = _L2_cond_setup()
    _L2_cond_in = {k: v for k, v in _L2_cond_all.items() if k in ('W', 'b')}
    del _L2_cond_all

    def _L2_ffn_setup():
        import jax, jax.numpy as jnp
        import numpy as np
        B, S, D = (4, 512, 256)
        N_EXPERTS, EXPERT_SIZE = (16, 64)
        WIDTH = N_EXPERTS * EXPERT_SIZE
        key = jax.random.key(seed)
        k_x, k_w1, k_w2, k_g = jax.random.split(key, 4)
        x = jax.random.normal(k_x, (B, S, D), dtype=jnp.float32)
        w1 = jax.random.normal(k_w1, (D, WIDTH), dtype=jnp.float32) / np.sqrt(D).astype(np.float32)
        b1 = jnp.zeros((WIDTH,), dtype=jnp.float32)
        w2 = jax.random.normal(k_w2, (WIDTH, D), dtype=jnp.float32) / np.sqrt(WIDTH).astype(np.float32)
        b2 = jnp.zeros((D,), dtype=jnp.float32)
        return {'x': x, 'w1': w1, 'b1': b1, 'w2': w2, 'b2': b2}
    _L2_ffn_all = _L2_ffn_setup()
    _L2_ffn_in = {k: v for k, v in _L2_ffn_all.items() if k in ('w1', 'b1', 'w2', 'b2')}
    del _L2_ffn_all

    def _L3_cond_setup():
        import jax, jax.numpy as jnp
        import numpy as np
        IN, HID, OUT, PART, E = (256, 1024, 256, 64, 8)
        B, N = (16, 512)
        key = jax.random.key(seed)
        ks = jax.random.split(key, 8)
        s1 = 1.0 / np.sqrt(IN)
        s2 = 1.0 / np.sqrt(HID)
        return {'x': jax.random.normal(ks[0], (B, N, IN), dtype=jnp.float32), 'indices': jax.random.randint(ks[1], (B,), 0, E, dtype=jnp.int64), 'W1': jax.random.uniform(ks[2], (IN, HID), jnp.float32, -s1, s1), 'b1': jax.random.uniform(ks[3], (HID,), jnp.float32, -s1, s1), 'W2': jax.random.uniform(ks[4], (HID, OUT - PART), jnp.float32, -s2, s2), 'b2': jax.random.uniform(ks[5], (OUT - PART,), jnp.float32, -s2, s2), 'We': jax.random.uniform(ks[6], (E, HID, PART), jnp.float32, -s2, s2), 'be': jax.random.uniform(ks[7], (E, PART), jnp.float32, -s2, s2)}
    _L3_cond_all = _L3_cond_setup()
    _L3_cond_in = {k: v for k, v in _L3_cond_all.items() if k in ('W1', 'b1', 'W2', 'b2', 'We', 'be')}
    del _L3_cond_all

    def _L3_ffn_setup():
        import jax, jax.numpy as jnp
        import numpy as np
        D = 256
        H = 512
        E = 8
        TOP_K = 2
        N_SHARED = 1
        B, S = (2, 256)
        key = jax.random.key(seed)
        ks = jax.random.split(key, 12)
        sc = 0.02
        return {'hidden': jax.random.normal(ks[0], (B, S, D), jnp.float32), 'router_w': jax.random.normal(ks[1], (D, E), jnp.float32) * sc, 'router_b': jnp.zeros((E,), jnp.float32), 'sw1': jax.random.normal(ks[2], (D, H), jnp.float32) * sc, 'sb1': jnp.zeros((H,), jnp.float32), 'sw2': jax.random.normal(ks[3], (H, D), jnp.float32) * sc, 'sb2': jnp.zeros((D,), jnp.float32), 'rw1': jax.random.normal(ks[4], (E, D, H), jnp.float32) * sc, 'rb1': jnp.zeros((E, H), jnp.float32), 'rw2': jax.random.normal(ks[5], (E, H, D), jnp.float32) * sc, 'rb2': jnp.zeros((E, D), jnp.float32)}
    _L3_ffn_all = _L3_ffn_setup()
    _L3_ffn_in = {k: v for k, v in _L3_ffn_all.items() if k in ('router_w', 'router_b', 'sw1', 'sb1', 'sw2', 'sb2', 'rw1', 'rb1', 'rw2', 'rb2')}
    del _L3_ffn_all
    return {'x': x, 'itok_B_0_7': itok_B_0_7, 'condB_zX': condB_zX, 'condB_zY': condB_zY, 'condB_zR': condB_zR, 'itok_B_0_30': itok_B_0_30, 'L0_cond_weight': _L0_cond_in['weight'], 'L0_cond_bias': _L0_cond_in['bias'], 'L0_ffn_cn_w1': _L0_ffn_in['cn_w1'], 'L0_ffn_cn_b1': _L0_ffn_in['cn_b1'], 'L0_ffn_cn_w2': _L0_ffn_in['cn_w2'], 'L0_ffn_cn_b2': _L0_ffn_in['cn_b2'], 'L0_ffn_cn_w3': _L0_ffn_in['cn_w3'], 'L0_ffn_cn_b3': _L0_ffn_in['cn_b3'], 'L0_ffn_cn_w4': _L0_ffn_in['cn_w4'], 'L0_ffn_cn_b4': _L0_ffn_in['cn_b4'], 'L0_ffn_gc_w1': _L0_ffn_in['gc_w1'], 'L0_ffn_gc_b1': _L0_ffn_in['gc_b1'], 'L0_ffn_gc_w2': _L0_ffn_in['gc_w2'], 'L0_ffn_gc_b2': _L0_ffn_in['gc_b2'], 'L0_ffn_gc_w3': _L0_ffn_in['gc_w3'], 'L0_ffn_gc_b3': _L0_ffn_in['gc_b3'], 'L0_ffn_adaptive_range': _L0_ffn_in['adaptive_range'], 'L1_ffn_W_in': _L1_ffn_in['W_in'], 'L1_ffn_b_in': _L1_ffn_in['b_in'], 'L1_ffn_W_out': _L1_ffn_in['W_out'], 'L1_ffn_b_out': _L1_ffn_in['b_out'], 'L2_cond_W': _L2_cond_in['W'], 'L2_cond_b': _L2_cond_in['b'], 'L2_ffn_w1': _L2_ffn_in['w1'], 'L2_ffn_b1': _L2_ffn_in['b1'], 'L2_ffn_w2': _L2_ffn_in['w2'], 'L2_ffn_b2': _L2_ffn_in['b2'], 'L3_cond_W1': _L3_cond_in['W1'], 'L3_cond_b1': _L3_cond_in['b1'], 'L3_cond_W2': _L3_cond_in['W2'], 'L3_cond_b2': _L3_cond_in['b2'], 'L3_cond_We': _L3_cond_in['We'], 'L3_cond_be': _L3_cond_in['be'], 'L3_ffn_router_w': _L3_ffn_in['router_w'], 'L3_ffn_router_b': _L3_ffn_in['router_b'], 'L3_ffn_sw1': _L3_ffn_in['sw1'], 'L3_ffn_sb1': _L3_ffn_in['sb1'], 'L3_ffn_sw2': _L3_ffn_in['sw2'], 'L3_ffn_sb2': _L3_ffn_in['sb2'], 'L3_ffn_rw1': _L3_ffn_in['rw1'], 'L3_ffn_rb1': _L3_ffn_in['rb1'], 'L3_ffn_rw2': _L3_ffn_in['rw2'], 'L3_ffn_rb2': _L3_ffn_in['rb2']}

def reference(x, itok_B_0_7, condB_zX, condB_zY, condB_zR, itok_B_0_30, L0_cond_weight, L0_cond_bias, L0_ffn_cn_w1, L0_ffn_cn_b1, L0_ffn_cn_w2, L0_ffn_cn_b2, L0_ffn_cn_w3, L0_ffn_cn_b3, L0_ffn_cn_w4, L0_ffn_cn_b4, L0_ffn_gc_w1, L0_ffn_gc_b1, L0_ffn_gc_w2, L0_ffn_gc_b2, L0_ffn_gc_w3, L0_ffn_gc_b3, L0_ffn_adaptive_range, L1_ffn_W_in, L1_ffn_b_in, L1_ffn_W_out, L1_ffn_b_out, L2_cond_W, L2_cond_b, L2_ffn_w1, L2_ffn_b1, L2_ffn_w2, L2_ffn_b2, L3_cond_W1, L3_cond_b1, L3_cond_W2, L3_cond_b2, L3_cond_We, L3_cond_be, L3_ffn_router_w, L3_ffn_router_b, L3_ffn_sw1, L3_ffn_sb1, L3_ffn_sw2, L3_ffn_sb2, L3_ffn_rw1, L3_ffn_rb1, L3_ffn_rw2, L3_ffn_rb2):
    import jax
    import jax.numpy as jnp

    def _L0_cond_ref(x, subject_id, weight, bias):
        import jax, jax.numpy as jnp
        import numpy as np
        S, O, H = (8, 256, 256)
        B, N = (32, 128)
        W = weight[subject_id]
        b = bias[subject_id]
        y = jnp.einsum('bnh,boh->bno', x, W) + b[:, None, :]
        return y

    def _L0_ffn_ref(x, cn_w1, cn_b1, cn_w2, cn_b2, cn_w3, cn_b3, cn_w4, cn_b4, gc_w1, gc_b1, gc_w2, gc_b2, gc_w3, gc_b3, adaptive_range):
        import jax, jax.numpy as jnp
        import numpy as np
        B, S, DIM = (4, 1024, 256)
        BASE_COUPLING = 0.1
        NUM_CYCLES = 3

        def _gelu(x):
            return jax.nn.gelu(x, approximate=False)

        def _coupling_net(h, w1, b1, w2, b2, w3, b3, w4, b4):
            h = _gelu(h @ w1 + b1)
            h = _gelu(h @ w2 + b2)
            h = _gelu(h @ w3 + b3)
            return jax.nn.sigmoid(h @ w4 + b4)

        def _global_net(h, w1, b1, w2, b2, w3, b3):
            h = _gelu(h @ w1 + b1)
            h = _gelu(h @ w2 + b2)
            return jax.nn.sigmoid(h @ w3 + b3)

        def _twist(x):
            o_r, o_i, p_r, p_i = jnp.split(x, 4, axis=-1)
            return jnp.concatenate([p_r, -p_i, -o_r, o_i], axis=-1)
        global_context = x.mean(axis=1, keepdims=True)
        gf = _global_net(global_context, gc_w1, gc_b1, gc_w2, gc_b2, gc_w3, gc_b3)
        out = x
        for _ in range(NUM_CYCLES):
            tf = _coupling_net(out, cn_w1, cn_b1, cn_w2, cn_b2, cn_w3, cn_b3, cn_w4, cn_b4)
            combined = 0.7 * gf + 0.3 * tf
            coupling = BASE_COUPLING + adaptive_range * (combined - 0.5) * 2.0
            out = out + coupling * _twist(out)
        return out

    def _L1_cond_ref(y, zX, zY, zR, dx, dy):
        import jax, jax.numpy as jnp
        import numpy as np
        yp_x = jnp.pad(y, ((0, 0), (0, 0), (1, 1)), mode='reflect')
        lap_x = (yp_x[:, :, :-2] - 2.0 * y + yp_x[:, :, 2:]) / (dx * dx)
        yp_y = jnp.pad(y, ((0, 0), (1, 1), (0, 0)), mode='reflect')
        lap_y = (yp_y[:, :-2, :] - 2.0 * y + yp_y[:, 2:, :]) / (dy * dy)
        du_dt = zX[:, :, None] * lap_x + zY[:, :, None] * lap_y + zR[:, :, None] * y * (1.0 - y)
        return du_dt

    def _L1_ffn_ref(x, W_in, b_in, W_out, b_out):
        import jax, jax.numpy as jnp
        import numpy as np

        def _ste(w, w_q):
            return w + jax.lax.stop_gradient(w_q - w)

        def quantize_w8_per(w, axis):
            amax = jnp.clip(jnp.max(jnp.abs(w), axis=axis, keepdims=True), 1e-08, None)
            scale = 127.0 / amax
            w_q = jnp.clip(jnp.round(w * scale), -128.0, 127.0) / scale
            return _ste(w, w_q)

        def quantize_a16(x):
            amax = jnp.clip(jnp.max(jnp.abs(x)), 1e-08, None)
            scale = 32767.0 / amax
            x_q = jnp.clip(jnp.round(x * scale), -32768.0, 32767.0) / scale
            return _ste(x, x_q)
        W_in_sim = quantize_w8_per(W_in, axis=0)
        W_out_sim = quantize_w8_per(W_out, axis=1)
        x_sim = quantize_a16(x)
        hidden = jax.nn.gelu(x_sim @ W_in_sim + b_in, approximate=False)
        hidden_sim = quantize_a16(hidden)
        out = hidden_sim @ W_out_sim + b_out
        return out

    def _L2_cond_ref(x, cat_ids, W, b):
        import jax, jax.numpy as jnp
        import numpy as np
        C, I, O = (32, 256, 256)
        B, T = (64, 128)
        selected_W = W[cat_ids]
        selected_b = b[cat_ids]
        if x.ndim == 2:
            return jnp.einsum('bi,bio->bo', x, selected_W) + selected_b
        return jnp.einsum('bti,bio->bto', x, selected_W) + selected_b[:, None, :]

    def _L2_ffn_ref(x, w1, b1, w2, b2):
        import jax, jax.numpy as jnp
        import numpy as np
        B, S, D = (4, 512, 256)
        N_EXPERTS, EXPERT_SIZE = (16, 64)
        WIDTH = N_EXPERTS * EXPERT_SIZE
        h = jax.nn.relu(jnp.einsum('bsd,dw->bsw', x, w1) + b1)
        return jnp.einsum('bsw,wd->bsd', h, w2) + b2

    def _L3_cond_ref(x, indices, W1, b1, W2, b2, We, be):
        import jax, jax.numpy as jnp
        import numpy as np
        IN, HID, OUT, PART, E = (256, 1024, 256, 64, 8)
        B, N = (16, 512)
        h = jax.nn.gelu(jnp.einsum('bni,ih->bnh', x, W1) + b1, approximate=False)
        shared_x = jnp.einsum('bnh,ho->bno', h, W2) + b2
        We_sel = We[indices]
        be_sel = be[indices]
        expert_x = jnp.einsum('bnh,bhp->bnp', h, We_sel) + be_sel[:, None, :]
        return jnp.concatenate([shared_x, expert_x], axis=-1)

    def _L3_ffn_ref(hidden, router_w, router_b, sw1, sb1, sw2, sb2, rw1, rb1, rw2, rb2):
        import jax, jax.numpy as jnp
        import numpy as np
        D = 256
        H = 512
        E = 8
        TOP_K = 2
        N_SHARED = 1
        B, S = (2, 256)
        b, s, d = hidden.shape
        T = b * s
        flat = hidden.reshape(T, d)
        router_logits = flat @ router_w + router_b
        router_probs = jax.nn.softmax(router_logits, axis=-1)
        topk_probs, topk_idx = jax.lax.top_k(router_probs, TOP_K)
        weights = jnp.zeros_like(router_probs).at[jnp.arange(T)[:, None], topk_idx].add(topk_probs)
        sh = jax.nn.gelu(flat @ sw1 + sb1, approximate=False)
        shared_out = (sh @ sw2 + sb2) / N_SHARED
        h1 = jax.nn.gelu(jnp.einsum('td,edh->teh', flat, rw1) + rb1[None], approximate=False)
        expert_out = jnp.einsum('teh,ehd->ted', h1, rw2) + rb2[None]
        mixed = jnp.einsum('ted,te->td', expert_out, weights)
        return (shared_out + mixed).reshape(b, s, d)
    x = x + _L0_ffn_ref(_L0_cond_ref(x, itok_B_0_7, L0_cond_weight, L0_cond_bias), L0_ffn_cn_w1, L0_ffn_cn_b1, L0_ffn_cn_w2, L0_ffn_cn_b2, L0_ffn_cn_w3, L0_ffn_cn_b3, L0_ffn_cn_w4, L0_ffn_cn_b4, L0_ffn_gc_w1, L0_ffn_gc_b1, L0_ffn_gc_w2, L0_ffn_gc_b2, L0_ffn_gc_w3, L0_ffn_gc_b3, L0_ffn_adaptive_range)
    x = x + _L1_ffn_ref(_L1_cond_ref(x, condB_zX[:, None], condB_zY[:, None], condB_zR[:, None], 1, 1), L1_ffn_W_in, L1_ffn_b_in, L1_ffn_W_out, L1_ffn_b_out)
    x = x + _L2_ffn_ref(_L2_cond_ref(x, itok_B_0_30, L2_cond_W, L2_cond_b), L2_ffn_w1, L2_ffn_b1, L2_ffn_w2, L2_ffn_b2)
    x = x + _L3_ffn_ref(_L3_cond_ref(x, itok_B_0_7, L3_cond_W1, L3_cond_b1, L3_cond_W2, L3_cond_b2, L3_cond_We, L3_cond_be), L3_ffn_router_w, L3_ffn_router_b, L3_ffn_sw1, L3_ffn_sb1, L3_ffn_sw2, L3_ffn_sb2, L3_ffn_rw1, L3_ffn_rb1, L3_ffn_rw2, L3_ffn_rb2)
    return x

_drawn_inputs = setup_inputs


def setup_inputs(seed=0):
    import zlib

    import numpy as np

    out = dict(_drawn_inputs(seed))
    spreads = {'L0_ffn_cn_b1': (0.0, 0.8),
     'L0_ffn_cn_b2': (0.0, 0.8),
     'L0_ffn_cn_b3': (0.0, 2.0),
     'L0_ffn_gc_b1': (0.0, 0.8),
     'L0_ffn_gc_b2': (0.0, 0.8),
     'L1_ffn_b_in': (0.0, 0.28),
     'L1_ffn_b_out': (0.0, 0.1),
     'L2_cond_b': (0.0, 0.287),
     'L2_ffn_b1': (0.0, 0.267),
     'L2_ffn_b2': (0.0, 0.1),
     'L3_ffn_router_b': (0.0, 0.8),
     'L3_ffn_sb1': (0.0, 2.0),
     'L3_ffn_sb2': (0.0, 2.0),
     'L3_ffn_rb1': (0.0, 0.8),
     'L3_ffn_rb2': (0.0, 2.0)}
    factors = {'L0_ffn_cn_w1': 8.0,
     'L0_ffn_cn_w2': 8.0,
     'L0_ffn_cn_w3': 8.0,
     'L0_ffn_cn_w4': 8.0,
     'L0_ffn_gc_w1': 8.0,
     'L0_ffn_gc_w2': 8.0,
     'L0_ffn_gc_w3': 6.097,
     'L3_cond_W1': 3.478,
     'L3_cond_b1': 8.0,
     'L3_cond_W2': 3.381,
     'L3_cond_b2': 8.0,
     'L3_cond_We': 5.31,
     'L3_cond_be': 8.0,
     'L3_ffn_router_w': 7.806,
     'L3_ffn_sw1': 3.232,
     'L3_ffn_sw2': 2.932,
     'L3_ffn_rw1': 8.0,
     'L3_ffn_rw2': 8.0}
    for name, (base, spread) in spreads.items():
        noise = np.random.default_rng([zlib.crc32(name.encode()), seed]).standard_normal(out[name].shape)
        drawn = base * np.exp(spread * noise) if base else spread * noise
        out[name] = jnp.asarray(drawn.astype(out[name].dtype))
    for name, factor in factors.items():
        out[name] = (out[name] * factor).astype(out[name].dtype)
    return out
```

```python
import concourse.bass as bass
from concourse import mybir

ALU = mybir.AluOpType
ACT = mybir.ActivationFunctionType
F32 = mybir.dt.float32
F32R = mybir.dt.float32r
BF16 = mybir.dt.bfloat16
I32 = mybir.dt.int32
U32 = mybir.dt.uint32
AX = mybir.AxisListType
ds, ts = bass.ds, bass.ts


class Names(dict):
    def __getattr__(self, name):
        return self[name]


P = 128
BATCH, SEQ, D = 64, 64, 256
T = BATCH * SEQ
KD = D // P
CH = 512
NC = T // CH
BPC = CH // SEQ
PAIRS = CH // P
SLOTS = 6
NCYCLE = 3
NITEM = NCYCLE * NC
KB = 1024
MAGIC = 1.5 * 2.0 ** 23
PARTS = ((0, 0), (0, 1), (1, 0))


def segments(eng, cuts, body):
    for lo, hi in zip(cuts, cuts[1:]):
        if hi - lo == 1:
            body(lo, lo)
        else:
            with eng.Fori(lo, hi) as step:
                body(step, lo)


def apart(eng, x):
    return x if isinstance(x, int) else eng.snap(x)


def within(x, lo, hi):
    return lo <= x < hi


def per_batch(ap, n=BPC):
    return ap.unsqueeze(2).broadcast_to([P, n, SEQ])


def by_batch(ap):
    return ap.rearrange("p (b s) -> p b s", s=SEQ)


def products(nc, out, weights, data, start, stop):
    for n, (a, b) in enumerate(PARTS):
        last = nc.tensor.matmul(out, weights[a], data[b], start=start and n == 0,
                                stop=stop and n == len(PARTS) - 1)
    return last



def place(nc, m, name, shape, dt, at):
    m[name] = nc.alloc_sbuf_tensor_at(name, shape, dt, offset=m.base + at)


ROWS = {}


def bias_rows(d):
    out, r = [], 0
    for name, ap in (("cn_b1", d.cn_b1), ("cn_b2", d.cn_b2), ("cn_b3", d.cn_b3), ("gc_b1", d.gc_b1),
                     ("gc_b2", d.gc_b2), ("b_in", d.b_in), ("b_out", d.b_out), ("f2_b1", d.f2_b1),
                     ("f2_b2", d.f2_b2), ("c3_b1", d.c3_b1), ("c3_b2", d.c3_b2), ("sb1", d.sb1),
                     ("sb2", d.sb2)):
        n = ap.shape[0]
        ROWS[name] = r
        full = n // P
        if full:
            out.append((r, full, P, ap[0:full * P].rearrange("(k p) -> k p", p=P)))
        if n % P:
            out.append((r + full, 1, n % P, ap[full * P:n].rearrange("(k p) -> k p", k=1)))
        r += (n + P - 1) // P
    ROWS["end"] = r
    return out


def common_memory(nc, m):
    m.base = (nc.sbuf_base + 31) // 32 * 32
    place(nc, m, "X", [P, KD, T], F32, 0)
    c = 32 * KB

    def const(name, cols, dt=F32):
        nonlocal c
        place(nc, m, name, [P, cols], dt, c)
        c += (cols * 4 + 31) // 32 * 32

    const("ident", P)
    const("biases", 48)
    const("cond0", KD * BATCH)
    const("coupl_b", BATCH)
    const("zxyz", 3 * BATCH)
    const("zk", BATCH)
    const("cond2", KD * BATCH)
    const("cond3", BATCH)
    const("scal", 16)
    const("magic", 1)
    const("nmagic", 1)
    const("ones1", P)
    const("ids0", BATCH, I32)
    const("ids2", BATCH, I32)
    m.work = 36 * KB + 512
    assert c <= m.work

    m.AR, m.SIGN, m.AMUL, m.GMUL, m.TENTH, m.CNB4, m.GCB3 = range(7)


def sc(m, col, rows=P):
    return m.scal[0:rows, col:col + 1]



def prepare(nc, m, d, sem):
    W = m.work
    w = W + 98 * KB + 16 * KB
    for name, rows, cols in (("cnw1", P, KD * 256), ("cnw2", P, KD * 128), ("cnw3", P, 64), ("cnw4", 64, 128)):
        for part in "HL":
            place(nc, m, name + part, [rows, cols], F32R, w)
            w += cols * 4
    for name, rows, cols in (("gcw1", P, KD * 128), ("gcw2", P, 64), ("gcw3", 64, 128)):
        place(nc, m, name, [rows, cols], F32, w)
        w += cols * 4
    m.l0_work = w
    s = w
    stage = {}
    for name, rows, cols in (("cnw1", P, KD * 256), ("cnw2", P, KD * 128), ("cnw3", P, 64), ("cnw4", 64, 128)):
        place(nc, m, "stage_" + name, [rows, cols], F32, s)
        stage[name] = m["stage_" + name]
        s += cols * 4
    for name, rows, cols, dt in (("rows", 48, P, F32), ("w4col", 64, 1, F32), ("g3col", 64, 1, F32),
                                 ("b0tab", 8, 256, F32), ("b2tab", 32, 256, F32), ("betab", 8, 64, F32),
                                 ("idsB0", 32, BATCH, I32), ("idsB2", 32, BATCH, I32),
                                 ("hot0", 32, BATCH, F32), ("hot2", 32, BATCH, F32),
                                 ("lane", P, 1, F32), ("laneI", P, 1, I32), ("b4col", P, 1, F32),
                                 ("gb3col", P, 1, F32), ("ones", 64, P, F32)):
        place(nc, m, "t_" + name, [rows, cols], dt, s)
        s += max(32, cols * 4)
    with nc.psum_tensor("prep_psum", [P, 5, 512], F32) as ps:
        rows = bias_rows(d)
        with nc.Block() as block:
            @block.gpsimd
            def _(pool):
                pool.memset(m.t_rows[:], 0.0).then_inc(sem.rows_clear, 1)
                pool.memset(m.ident[:], 1.0).then_inc(sem.prep_pool, 1)
                pool.memset(m.t_ones[:], 1.0)
                pool.memset(m.magic[:], MAGIC)
                pool.memset(m.nmagic[:], -MAGIC).then_inc(sem.prep_pool, 1)
                pool.iota(m.t_laneI[:], pattern=[[0, 1]], base=0, channel_multiplier=1).then_inc(sem.prep_pool, 1)
                pool.memset(m.scal[:], 0.0).then_inc(sem.prep_pool, 1)
                pool.wait_ge(sem.prep_pool, 4)
                pool.affine_select(out=m.ident[:], in_=m.ident[:], compare_op=ALU.is_equal, fill=0.0, base=0,
                                   pattern=[[1, P]], channel_multiplier=-1).then_inc(sem.prep_pool, 1)
                pool.wait_ge(sem.prep_pool, 5)

            @block.sync
            def _(sp):
                n = 0
                for dst, src in ((m.ids0[0:1, :], d.ids0.unsqueeze(0)), (m.ids2[0:1, :], d.ids2.unsqueeze(0)),
                                 (stage["cnw1"].rearrange("p (k n) -> p k n", k=KD), d.cn_w1.rearrange("(k p) n -> p k n", p=P)),
                                 (stage["cnw2"].rearrange("p (k n) -> p k n", k=KD), d.cn_w2.rearrange("(k p) n -> p k n", p=P)),
                                 (stage["cnw3"][:], d.cn_w3),
                                 (m.t_w4col[:], d.cn_w4), (m.t_g3col[:], d.gc_w3),
                                 (m.gcw1.rearrange("p (k n) -> p k n", k=KD), d.gc_w1.rearrange("(k p) n -> p k n", p=P)),
                                 (m.gcw2[:], d.gc_w2)):
                    sp.dma_start(dst, src).then_inc(sem.prep_load, 16)
                    n += 1
                for c in range(4):
                    sp.dma_start(m.X[:, :, ts(c, CH)], d.xT.rearrange("(k p) t -> p k t", p=P)[:, :, ts(c, CH)])\
                      .then_inc(sem.x_loaded[c], 16)
                sp.dma_start(m.X[:, :, 4 * CH:T], d.xT.rearrange("(k p) t -> p k t", p=P)[:, :, 4 * CH:T])\
                  .then_inc(sem.x_loaded[4], 16)

            @block.scalar
            def _(act):
                for dst, src in ((m.t_b0tab[:], d.c0_b), (m.t_b2tab[:], d.c2_b), (m.t_betab[:], d.be),
                                 (m.t_idsB0[:], d.ids0.partition_broadcast(32)), (m.t_idsB2[:], d.ids2.partition_broadcast(32)),
                                 (m.t_b4col[:], d.cn_b4.partition_broadcast(P)), (m.t_gb3col[:], d.gc_b3.partition_broadcast(P)),
                                 (m.scal[:, m.AR:m.AR + 1], d.ar.partition_broadcast(P)),
                                 (m.zxyz[:, 0:64], d.zX.partition_broadcast(P)),
                                 (m.zxyz[:, 64:128], d.zY.partition_broadcast(P)),
                                 (m.zxyz[:, 128:192], d.zR.partition_broadcast(P))):
                    act.wait_ge(sem.prep_pool, 4)
                    act.dma_start(dst, src).then_inc(sem.prep_load, 16)
                act.wait_ge(sem.rows_clear, 1)
                for r, n, cols, src in rows:
                    act.dma_start(m.t_rows[r:r + n, 0:cols], src).then_inc(sem.prep_load, 16)

        n_loads = 9 + 11 + len(rows)
        with nc.Block() as block:
            @block.tensor
            def _(pe):
                pe.wait_ge(sem.prep_load, 16 * n_loads)
                nc.tensor.transpose(ps[:, 0, 0:48], m.t_rows[:], m.ident[0:48, 0:48]).then_inc(sem.prep_pe, 1)
                pe.wait_ge(sem.prep_hot, 2)
                for k in range(KD):
                    nc.tensor.matmul(ps[:, 1, ts(k, BATCH)], m.t_b0tab[:, ts(k, P)], m.t_hot0[0:8, :], start=True, stop=True)
                    nc.tensor.matmul(ps[:, 2, ts(k, BATCH)], m.t_b2tab[:, ts(k, P)], m.t_hot2[:], start=True, stop=True)
                nc.tensor.matmul(ps[64:128, 3, 0:BATCH], m.t_betab[:], m.t_hot0[0:8, :], start=True, stop=True)\
                  .then_inc(sem.prep_pe, 1)

            @block.vector
            def _(dve):
                own = sem.prep_dve
                n = [0]

                def mark(i):
                    i.then_inc(own, 1)
                    n[0] += 1
                    return n[0]
                dve.wait_ge(sem.prep_load, 16 * n_loads)
                mark(nc.vector.tensor_copy(m.t_lane[:], m.t_laneI[:]))
                mark(nc.vector.tensor_copy(m.t_hot0[:], m.t_idsB0[:]))
                dve.wait_ge(own, mark(nc.vector.tensor_copy(m.t_hot2[:], m.t_idsB2[:])))
                for t in (m.t_hot0, m.t_hot2):
                    nc.vector.tensor_scalar(t[:], t[:], m.t_lane[0:32, :], None, ALU.is_equal).then_inc(sem.prep_hot, 1)
                mark(nc.vector.memset(m.scal[0:64, m.SIGN:m.SIGN + 1], 1.0))
                mark(nc.vector.memset(m.scal[64:128, m.SIGN:m.SIGN + 1], -1.0))
                mark(nc.vector.tensor_scalar(m.stage_cnw4[:], m.t_ones[:], m.t_w4col[:], None, ALU.mult))
                mark(nc.vector.tensor_scalar(m.gcw3[:], m.t_ones[:], m.t_g3col[:], None, ALU.mult))
                mark(nc.vector.tensor_scalar(sc(m, m.CNB4), m.t_b4col[:], 0.5, None, ALU.mult))
                mark(nc.vector.tensor_scalar(sc(m, m.GCB3), m.t_gb3col[:], 0.5, None, ALU.mult))
                for name in ("cnw1", "cnw2", "cnw3"):
                    mark(nc.vector.tensor_copy(m[name + "H"][:], stage[name][:]))
                dve.wait_ge(own, n[0])
                mark(nc.vector.tensor_copy(m.cnw4H[:], m.stage_cnw4[:]))
                mark(nc.vector.tensor_scalar(sc(m, m.AMUL), sc(m, m.AR), sc(m, m.SIGN), 0.3, ALU.mult, ALU.mult))
                mark(nc.vector.tensor_scalar(sc(m, m.GMUL), sc(m, m.AR), sc(m, m.SIGN), 0.7, ALU.mult, ALU.mult))
                mark(nc.vector.tensor_scalar(sc(m, m.TENTH), sc(m, m.SIGN), 0.1, None, ALU.mult))
                mark(nc.vector.scalar_tensor_tensor(m.zk[:], m.zxyz[:, 64:128], -2.0, m.zxyz[:, 128:192],
                                                    ALU.mult, ALU.add))
                dve.wait_ge(own, n[0])
                for name in ("cnw1", "cnw2", "cnw3", "cnw4"):
                    nc.vector.tensor_tensor(m[name + "L"][:], stage[name][:],
                                            m[name + "H"][:].bitcast(F32), ALU.subtract)
                dve.wait_ge(sem.prep_pe, 1)
                mark(nc.vector.tensor_copy(m.biases[:], ps[:, 0, 0:48]))
                dve.wait_ge(sem.prep_pe, 2)
                mark(nc.vector.tensor_copy(m.cond0[:], ps[:, 1, 0:KD * BATCH]))
                mark(nc.vector.tensor_copy(m.cond2[:], ps[:, 2, 0:KD * BATCH]))
                mark(nc.vector.tensor_copy(m.cond3[64:128, :], ps[64:128, 3, 0:BATCH]))
                dve.wait_ge(own, n[0])
                mark(nc.vector.memset(m.cond3[0:64, :], 0.0))
                dve.wait_ge(own, n[0])
                r = ROWS["c3_b2"] + 1
                mark(nc.vector.tensor_scalar(m.cond3[0:64, :], m.cond3[0:64, :], m.biases[0:64, r:r + 1], None, ALU.add))
                dve.wait_ge(own, n[0])


def bias(m, name, k=0, rows=P):
    r = ROWS[name] + k
    return m.biases[0:rows, r:r + 1]



def layer0(nc, m, d, sem):
    W = m.work
    place(nc, m, "Y", [P, KD, T], F32, W)
    place(nc, m, "YH", [P, KD, T], F32R, W + 32 * KB)
    place(nc, m, "YL", [P, KD, T], F32R, W + 64 * KB)
    place(nc, m, "cw", [P, SLOTS, KD, D], F32, W + 98 * KB)
    place(nc, m, "yt", [P, PAIRS, D], F32, W + 110 * KB)
    place(nc, m, "l0_small", [P, 72], F32, W + 96 * KB)
    a = m.l0_work
    for name, rows, shape, dt in (("h1F", P, [KD, CH], F32), ("h1H", P, [2, KD, CH], F32R), ("h1L", P, [2, KD, CH], F32R),
                                  ("h2F", P, [CH], F32), ("h2H", P, [2, CH], F32R), ("h2L", P, [2, CH], F32R),
                                  ("h3F", 64, [CH], F32), ("h3H", 64, [2, CH], F32R), ("h3L", 64, [2, CH], F32R),
                                  ("th", P, [CH], F32), ("cs", P, [CH], F32), ("t0", P, [CH], F32), ("t1", P, [CH], F32)):
        place(nc, m, name, [rows] + shape, dt, a)
        size = 4
        for x in shape:
            size *= x
        a += size
    gsum = m.l0_small[:, 40:72].rearrange("p (s n) -> p s n", s=2)
    g1 = m.l0_small[:, 16:24]
    g2 = m.l0_small[0:64, 24:32]
    tg = m.l0_small[:, 32:40]
    cnw1 = [x.rearrange("p (k n) -> p k n", k=KD) for x in (m.cnw1H, m.cnw1L)]
    cnw2 = [x.rearrange("p (k n) -> p k n", k=KD) for x in (m.cnw2H, m.cnw2L)]
    gcw1 = m.gcw1.rearrange("p (k n) -> p k n", k=KD)
    LAST_SPLIT = NITEM - NC

    CUTS = [*range(NC + 5), LAST_SPLIT + 4, *range(NITEM, NITEM + 5)]

    with nc.psum_tensor("l0_tok", [P, CH], F32) as ps_tok, nc.psum_tensor("l0_turn", [P, CH], F32) as ps_turn, \
            nc.psum_tensor("l0_h1", [P, KD, CH], F32) as ps_h1, \
            nc.psum_tensor("l0_h2", [P, CH], F32) as ps_h2, nc.psum_tensor("l0_h3", [P, CH], F32) as ps_h3, \
            nc.psum_tensor("l0_th", [P, CH], F32) as ps_th, nc.psum_tensor("l0_g", [P, CH], F32) as ps_g, \
            nc.Block() as block:

        @block.sync
        def _(sp):
            for b in range(BATCH):
                i = sp.value_load(m.ids0[0:1, b:b + 1], min_val=0, max_val=7)
                if b >= SLOTS:
                    sp.wait_ge(sem.tok_mm, (b - SLOTS) // 2 + 1)
                sp.dma_start(m.cw[:, b % SLOTS], d.c0_wT[ds(i, 1)].rearrange("e (k p) o -> p (e k) o", p=P))\
                  .then_inc(sem.cw_loaded[b % SLOTS], 16)

        @block.tensor
        def _(pe):
            def pair(c, rep, q):
                if q == 0:
                    pe.wait_ge(sem.x_loaded[min(c, 4)], 16)
                if c >= 1 or q >= 1:
                    pe.wait_ge(sem.tok_act, c * PAIRS + q)
                for b in (c * BPC + 2 * q, c * BPC + 2 * q + 1):
                    pe.wait_ge(sem.cw_loaded[b % SLOTS], 16 * (b // SLOTS + 1))
                    for k in range(KD):
                        last = nc.tensor.matmul(ps_tok[ts(b % 2, SEQ), 0:D], m.X[:, k, ts(b, SEQ)], m.cw[:, b % SLOTS, k],
                                                start=k == 0, stop=k == KD - 1)
                last.then_inc(sem.tok_mm, 1)

            def turn(c, rep, h):
                pe.wait_ge(sem.tok_act, (c + 1) * PAIRS)
                if rep >= 1 or h >= 1:
                    pe.wait_ge(sem.y_added, 2 * c + h)
                for q in range(PAIRS):
                    last = nc.tensor.transpose(ps_turn[:, ts(q, P)], m.yt[:, q, ts(h, P)], m.ident[:])
                last.then_inc(sem.turn_mm, 1)

            def body(j, rep):
                cond = rep + 2 < NC
                if cond:
                    pair(j + 2, rep + 2, 0)
                if rep < NITEM:
                    c = j % NC
                    if rep < NC:
                        pe.wait_ge(sem.yh_cond, 2 * j + 2)
                        pe.wait_ge(sem.yl_cond, 2 * j + 2)
                    else:
                        pe.wait_ge(sem.yh_upd, 2 * (j - NC) + 2)
                        pe.wait_ge(sem.yl_upd, 2 * (j - NC) + 2)
                    for h in range(KD):
                        if rep >= 1:
                            pe.wait_ge(sem.h1_act, 2 * j - 1 + h)
                        for k in range(KD):
                            last = products(nc, ps_h1[:, h], [w[:, k, ts(h, P)] for w in cnw1],
                                            [y[:, k, ds(c * CH, CH)] for y in (m.YH, m.YL)], k == 0, k == KD - 1)
                        last.then_inc(sem.h1_mm, 1)
                        if cond and h == 0:
                            pair(j + 2, rep + 2, 1)
                if rep < NC + 2:
                    if rep >= 1:
                        pe.wait_ge(sem.g_act, j)
                    if rep < NC:
                        pe.wait_ge(sem.sums, j + 1)
                        for k in range(KD):
                            last = nc.tensor.matmul(ps_g[:, 0:BPC], gcw1[:, k], gsum[:, j % 2, ts(k, BPC)], start=k == 0, stop=k == KD - 1)
                    if within(rep - 1, 0, NC):
                        last = nc.tensor.matmul(ps_g[0:64, 8:16], m.gcw2[:], g1, start=True, stop=True)
                    if within(rep - 2, 0, NC):
                        last = nc.tensor.matmul(ps_g[:, 16:24], m.gcw3[:], g2, start=True, stop=True)
                    last.then_inc(sem.g_mm, 1)
                if cond:
                    pair(j + 2, rep + 2, 2)
                if within(rep - 1, 0, NITEM):
                    i = j - 1
                    pe.wait_ge(sem.h1_act, 2 * i + 2)
                    pe.wait_ge(sem.h1_low, 2 * i + 2)
                    if rep - 1 >= 1:
                        pe.wait_ge(sem.h2_act, i)
                    for k in range(KD):
                        last = products(nc, ps_h2[:], [w[:, k] for w in cnw2],
                                        [x[:, i % 2, k] for x in (m.h1H, m.h1L)], k == 0, k == KD - 1)
                    last.then_inc(sem.h2_mm, 1)
                if cond:
                    pair(j + 2, rep + 2, 3)
                if within(rep - 2, 0, NITEM):
                    i = j - 2
                    pe.wait_ge(sem.h2_act, i + 1)
                    pe.wait_ge(sem.h2_low, i + 1)
                    if rep - 2 >= 1:
                        pe.wait_ge(sem.h3_act, i)
                    products(nc, ps_h3[0:64, :], (m.cnw3H[:], m.cnw3L[:]),
                             [x[:, i % 2] for x in (m.h2H, m.h2L)], True, True).then_inc(sem.h3_mm, 1)
                if cond:
                    turn(j + 2, rep + 2, 0)
                if within(rep - 3, 0, NITEM):
                    i = j - 3
                    pe.wait_ge(sem.h3_act, i + 1)
                    pe.wait_ge(sem.h3_low, i + 1)
                    if rep - 3 >= 1:
                        pe.wait_ge(sem.th_act, i)
                    products(nc, ps_th[:], (m.cnw4H[:], m.cnw4L[:]),
                             [x[:, i % 2] for x in (m.h3H, m.h3L)], True, True).then_inc(sem.th_mm, 1)
                if cond:
                    turn(j + 2, rep + 2, 1)

            for c in range(2):
                for q in range(PAIRS):
                    pair(c, c, q)
                for h in range(KD):
                    turn(c, c, h)
            segments(pe, CUTS, body)

        @block.scalar
        def _(act):
            def pair(c, rep, q):
                act.wait_ge(sem.tok_mm, c * PAIRS + q + 1)
                if rep >= 1:
                    act.wait_ge(sem.turn_mm, 2 * c)
                nc.scalar.copy(m.yt[:, q], ps_tok[:, 0:D]).then_inc(sem.tok_act, 1)

            def body(j, rep):
                cond = rep + 2 < NC
                if cond:
                    pair(j + 2, rep + 2, 0)
                if rep < NITEM:
                    for h in range(KD):
                        act.wait_ge(sem.h1_mm, 2 * j + h + 1)
                        if rep >= 1:
                            act.wait_ge(sem.h1_low, 2 * j - 1 + h)
                        if rep >= 2:
                            act.wait_ge(sem.h2_mm, j - 1)
                        nc.scalar.activation(m.h1H[:, j % 2, h], ps_h1[:, h], ACT.Gelu, bias=bias(m, "cn_b1", h))
                        nc.scalar.activation(m.h1F[:, h], ps_h1[:, h], ACT.Gelu, bias=bias(m, "cn_b1", h))\
                          .then_inc(sem.h1_act, 1)
                        if cond and h == 0:
                            pair(j + 2, rep + 2, 1)
                if rep < NC + 2:
                    act.wait_ge(sem.g_mm, j + 1)
                    if within(rep - 2, 0, NC):
                        if rep - 2 >= 1:
                            act.wait_ge(sem.coupl_b, j - 2)
                        last = nc.scalar.activation(tg, ps_g[:, 16:24], ACT.Tanh, bias=sc(m, m.GCB3), scale=0.5)
                    if within(rep - 1, 0, NC):
                        last = nc.scalar.activation(g2, ps_g[0:64, 8:16], ACT.Gelu, bias=bias(m, "gc_b2", rows=64))
                    if rep < NC:
                        last = nc.scalar.activation(g1, ps_g[:, 0:BPC], ACT.Gelu, bias=bias(m, "gc_b1"), scale=1.0 / SEQ)
                    last.then_inc(sem.g_act, 1)
                if cond:
                    pair(j + 2, rep + 2, 2)
                if within(rep - 1, 0, NITEM):
                    i = j - 1
                    act.wait_ge(sem.h2_mm, i + 1)
                    if rep - 1 >= 1:
                        act.wait_ge(sem.h2_low, i)
                    if rep - 1 >= 2:
                        act.wait_ge(sem.h3_mm, i - 1)
                    nc.scalar.activation(m.h2H[:, i % 2], ps_h2[:], ACT.Gelu, bias=bias(m, "cn_b2"))
                    nc.scalar.activation(m.h2F[:], ps_h2[:], ACT.Gelu, bias=bias(m, "cn_b2")).then_inc(sem.h2_act, 1)
                if cond:
                    pair(j + 2, rep + 2, 3)
                if within(rep - 2, 0, NITEM):
                    i = j - 2
                    act.wait_ge(sem.h3_mm, i + 1)
                    if rep - 2 >= 1:
                        act.wait_ge(sem.h3_low, i)
                    if rep - 2 >= 2:
                        act.wait_ge(sem.th_mm, i - 1)
                    nc.scalar.activation(m.h3H[:, i % 2], ps_h3[0:64, :], ACT.Gelu, bias=bias(m, "cn_b3", rows=64))
                    nc.scalar.activation(m.h3F[:], ps_h3[0:64, :], ACT.Gelu, bias=bias(m, "cn_b3", rows=64))\
                      .then_inc(sem.h3_act, 1)
                if within(rep - 3, 0, NITEM):
                    i = j - 3
                    act.wait_ge(sem.th_mm, i + 1)
                    if rep - 3 >= 1:
                        act.wait_ge(sem.cs_done, i)
                    nc.scalar.activation(m.th[:], ps_th[:], ACT.Tanh, bias=sc(m, m.CNB4), scale=0.5)\
                      .then_inc(sem.th_act, 1)
            for c in range(2):
                for q in range(PAIRS):
                    pair(c, c, q)
            segments(act, CUTS, body)

        @block.vector
        def _(dve):
            def cond(c, rep):
                if rep >= 2:
                    dve.wait_ge(sem.g_mm, c - 1)
                for h in range(KD):
                    dve.wait_ge(sem.turn_mm, KD * c + h + 1)
                    nc.vector.tensor_tensor(by_batch(m.Y[:, h, ds(c * CH, CH)]), by_batch(ps_turn[:]),
                                            per_batch(m.cond0[:, ds(h * BATCH + c * BPC, BPC)]), ALU.add)\
                      .then_inc(sem.y_added, 1)
                for h in range(KD):
                    dve.wait_ge(sem.y_added, 2 * c + 1 + h)
                    nc.vector.tensor_copy(m.YH[:, h, ds(c * CH, CH)], m.Y[:, h, ds(c * CH, CH)]).then_inc(sem.yh_cond, 1)
                for h in range(KD):
                    last = nc.vector.tensor_reduce(gsum[:, c % 2, ts(h, BPC)], by_batch(m.Y[:, h, ds(c * CH, CH)]), AX.X, ALU.add)
                last.then_inc(sem.sums, 1)

            def body(j, rep):
                upd = within(rep - 4, 0, NITEM)
                u = j - 4
                if rep < NITEM:
                    for h in range(KD):
                        dve.wait_ge(sem.h1_act, 2 * j + h + 1)
                        if rep >= 2:
                            dve.wait_ge(sem.h2_mm, j - 1)
                        nc.vector.tensor_tensor(m.h1L[:, j % 2, h], m.h1F[:, h], m.h1H[:, j % 2, h].bitcast(F32),
                                                ALU.subtract).then_inc(sem.h1_low, 1)
                if upd:
                    uc = u % NC
                    dve.wait_ge(sem.th_act, u + 1)
                    if rep - 4 < NC:
                        dve.wait_ge(sem.coupl_b, u + 1)
                    if rep - 4 >= 1:
                        dve.wait_ge(sem.t1_done, u)
                    nc.vector.scalar_tensor_tensor(by_batch(m.cs[:]), by_batch(m.th[:]), sc(m, m.AMUL),
                                                   per_batch(m.coupl_b[:, ds(uc * BPC, BPC)]), ALU.mult, ALU.add)\
                      .then_inc(sem.cs_done, 1)
                    dve.wait_ge(sem.cs_done, u + 1)
                    nc.vector.tensor_tensor(m.t0[:], m.cs[:], m.Y[:, 1, ds(uc * CH, CH)], ALU.mult).then_inc(sem.t0_done, 1)
                if within(rep - 1, 0, NITEM):
                    i = j - 1
                    dve.wait_ge(sem.h2_act, i + 1)
                    if rep - 1 >= 2:
                        dve.wait_ge(sem.h3_mm, i - 1)
                    nc.vector.tensor_tensor(m.h2L[:, i % 2], m.h2F[:], m.h2H[:, i % 2].bitcast(F32), ALU.subtract)\
                      .then_inc(sem.h2_low, 1)
                if within(rep - 2, 0, NITEM):
                    i = j - 2
                    dve.wait_ge(sem.h3_act, i + 1)
                    if rep - 2 >= 2:
                        dve.wait_ge(sem.th_mm, i - 1)
                    nc.vector.tensor_tensor(m.h3L[:, i % 2], m.h3F[:], m.h3H[:, i % 2].bitcast(F32), ALU.subtract)\
                      .then_inc(sem.h3_low, 1)
                if within(rep - 2, 0, NC):
                    i = j - 2
                    dve.wait_ge(sem.g_act, j + 1)
                    nc.vector.tensor_scalar(m.coupl_b[:, ds(i * BPC, BPC)], tg, sc(m, m.GMUL), sc(m, m.TENTH),
                                            ALU.mult, ALU.add).then_inc(sem.coupl_b, 1)
                if rep + 2 < NC:
                    cond(j + 2, rep + 2)
                if upd:
                    dve.wait_ge(sem.t0_done, u + 1)
                    dve.wait_ge(sem.t1_done, u + 1)
                    nc.vector.tensor_tensor(m.Y[:, 0, ds(uc * CH, CH)], m.Y[:, 0, ds(uc * CH, CH)], m.t0[:], ALU.add)\
                      .then_inc(sem.y_upd, 1)
                    nc.vector.tensor_tensor(m.Y[:, 1, ds(uc * CH, CH)], m.Y[:, 1, ds(uc * CH, CH)], m.t1[:], ALU.subtract)\
                      .then_inc(sem.y_upd, 1)
                    if rep - 4 < LAST_SPLIT:
                        for h in range(KD):
                            dve.wait_ge(sem.y_upd, 2 * u + 1 + h)
                            nc.vector.tensor_copy(m.YH[:, h, ds(uc * CH, CH)], m.Y[:, h, ds(uc * CH, CH)])\
                              .then_inc(sem.yh_upd, 1)
            cond(0, 0)
            cond(1, 1)
            segments(dve, CUTS, body)

        @block.gpsimd
        def _(pool):
            def low(c, done, made, at):
                for h in range(KD):
                    pool.wait_ge(made, 2 * at + h + 1)
                    pool.tensor_tensor(m.YL[:, h, ds(c * CH, CH)], m.Y[:, h, ds(c * CH, CH)],
                                       m.YH[:, h, ds(c * CH, CH)].bitcast(F32), ALU.subtract).then_inc(done, 1)

            def body(j, rep):
                upd = within(rep - 4, 0, NITEM)
                u = j - 4
                if upd:
                    uc = u % NC
                    pool.wait_ge(sem.cs_done, u + 1)
                    if rep - 4 >= 1:
                        pool.wait_ge(sem.y_upd, 2 * u)
                    pool.tensor_tensor(m.t1[:], m.cs[:], m.Y[:, 0, ds(uc * CH, CH)], ALU.mult).then_inc(sem.t1_done, 1)
                if rep + 2 < NC:
                    low(j + 2, sem.yl_cond, sem.yh_cond, j + 2)
                if upd and rep - 4 < LAST_SPLIT:
                    low(uc, sem.yl_upd, sem.yh_upd, u)
            low(0, sem.yl_cond, sem.yh_cond, 0)
            low(1, sem.yl_cond, sem.yh_cond, 1)
            segments(pool, CUTS, body)



FF1 = 1024
KF1 = FF1 // P


def layer1(nc, m, d, sem):
    W = m.work
    NT = NC * KF1
    place(nc, m, "hid", [P, NT, CH], F32, W)
    place(nc, m, "du", [P, NC, KD, CH], F32, W + 96 * KB)
    w = W + 128 * KB
    place(nc, m, "w_in", [P, KD, FF1], BF16, w)
    place(nc, m, "w_out", [P, KF1, D], F32R, w + 4 * KB)
    place(nc, m, "s1", [P, 64], F32, w + 12 * KB)
    w += 13 * KB
    place(nc, m, "lap", [P, KD, D], F32, W + 32 * KB)
    place(nc, m, "st", [P, KF1, D], F32, W + 34 * KB)
    place(nc, m, "st2", [P, KF1, D], F32, W + 42 * KB)
    place(nc, m, "stq", [P, KF1, D], BF16, W + 50 * KB)
    for i, name in enumerate(("ub", "cb", "db", "ab")):
        place(nc, m, name, [P, 2, CH], F32, W + (54 + 4 * i) * KB)
    place(nc, m, "identb", [P, P], BF16, W + 70 * KB)
    place(nc, m, "mx1", [P, 2 * NC], F32, W + 71 * KB)
    place(nc, m, "qt", [P, 2, KD, CH], F32, w)
    place(nc, m, "qH", [P, 2, KD, CH], BF16, w + 8 * KB)
    place(nc, m, "qL", [P, 2, KD, CH], BF16, w + 12 * KB)
    place(nc, m, "mx2", [P, NT], F32, w + 16 * KB)
    GS = 4
    place(nc, m, "gH", [P, GS, CH], F32R, w)
    place(nc, m, "gL", [P, GS, CH], F32R, w + 8 * KB)
    place(nc, m, "o1", [P, 2, KD, CH], F32, w + 18 * KB)
    s1 = m.s1
    WIN_A, WIN_S, WOUT_A, WOUT_S, DEQ, KOUT = (slice(8 * i, 8 * i + 8) for i in range(6))
    MX, AMAX, SX, ISX, SH, ISH, C32767, C127 = (slice(48 + i, 49 + i) for i in range(8))

    def reduce_part(block, ps, mx, scale, inverse, stage):
        mm, v = sem.red_mm[stage - 1], sem.red_v[stage - 1]

        @block.tensor
        def _(pe):
            pe.wait_ge(v, 1)
            nc.tensor.transpose(ps[0:1, 0:P], s1[:, MX], m.ident[:]).then_inc(mm, 1)
            pe.wait_ge(v, 2)
            nc.tensor.matmul(ps[:, P:P + 1], m.ones1[0:1, :], s1[0:1, AMAX], start=True, stop=True).then_inc(mm, 1)

        @block.vector
        def _(dve):
            nc.vector.tensor_reduce(s1[:, MX], mx, AX.X, ALU.max).then_inc(v, 1)
            dve.wait_ge(mm, 1)
            nc.vector.tensor_reduce(s1[0:1, AMAX], ps[0:1, 0:P], AX.X, ALU.max).then_inc(v, 1)
            dve.wait_ge(mm, 2)
            nc.vector.tensor_scalar(s1[:, MX], ps[:, P:P + 1], 1e-8, None, ALU.max).then_inc(v, 1)
            dve.wait_ge(v, 3)
            nc.vector.reciprocal(s1[:, AMAX], s1[:, MX]).then_inc(v, 1)
            dve.wait_ge(v, 4)
            nc.vector.tensor_scalar(s1[:, scale], s1[:, AMAX], 32767.0, None, ALU.mult).then_inc(v, 1)
            dve.wait_ge(v, 5)
            nc.vector.reciprocal(s1[:, inverse], s1[:, scale]).then_inc(v, 1)
            dve.wait_ge(v, 6)
            if stage == 1:
                nc.vector.tensor_scalar(s1[:, DEQ], s1[:, WIN_A], s1[:, inverse], None, ALU.mult).then_inc(v, 1)
                dve.wait_ge(v, 7)

    with nc.Block() as block:
        @block.sync
        def _(sp):
            sp.dma_start(m.st[:], d.w_inT.rearrange("(j p) k -> p j k", p=P)).then_inc(sem.w1_loaded, 16)
            sp.dma_start(m.st2[:], d.w_out.rearrange("(j p) k -> p j k", p=P)).then_inc(sem.w1_loaded, 16)

        @block.vector
        def _(dve):
            nc.vector.memset(s1[:, C32767], 32767.0)
            nc.vector.memset(s1[:, C127], 127.0)
            nc.vector.tensor_copy(m.identb[:], m.ident[:])
            nc.vector.memset(m.ones1[:], 1.0).then_inc(sem.l1_const, 1)
            dve.wait_ge(sem.l1_const, 1)

        @block.gpsimd
        def _(pool):
            n = [0]

            def step(i):
                i.then_inc(sem.lap, 1)
                n[0] += 1
                pool.wait_ge(sem.lap, n[0])
            step(pool.memset(m.lap[:], 0.0))
            for k in range(KD):
                for off, v in ((0, -2.0), (1, 1.0), (-1, 1.0)):
                    step(pool.affine_select(out=m.lap[:, k], in_=m.lap[:, k], compare_op=ALU.not_equal, fill=v,
                                            base=k * P - off, pattern=[[-1, D]], channel_multiplier=1))
            step(pool.affine_select(out=m.lap[:, 0, 0:1], in_=m.lap[:, 0, 0:1], compare_op=ALU.not_equal, fill=2.0,
                                    base=-1, pattern=[[0, 1]], channel_multiplier=1))
            step(pool.affine_select(out=m.lap[:, 1, D - 1:D], in_=m.lap[:, 1, D - 1:D], compare_op=ALU.not_equal, fill=2.0,
                                    base=-(P - 2), pattern=[[0, 1]], channel_multiplier=1))

    zX, zY, zR = (m.zxyz[:, ts(i, BATCH)] for i in range(3))

    with nc.psum_tensor("l1_lap", [P, 2, CH], F32) as ps_lap, nc.psum_tensor("l1_u", [P, 2, CH], F32) as ps_u, \
            nc.psum_tensor("l1_wt", [P, 2, 1024], BF16) as ps_w, nc.Block() as block:

        @block.tensor
        def _(pe):
            def body(c, rep):
                pe.wait_ge(sem.x1_sum, 2 * c + 2)
                for h in range(KD):
                    if rep >= 1:
                        pe.wait_ge(sem.du_a, 2 * c - 1 + h)
                    for k in range(KD):
                        nc.tensor.matmul(ps_lap[:, h], m.lap[:, k, ts(h, P)], m.X[:, k, ds(c * CH, CH)],
                                         start=k == 0, stop=k == KD - 1)
                    x = by_batch(m.X[:, h, ds(c * CH, CH)])
                    u = by_batch(ps_u[:, h])
                    nc.tensor.matmul(u[:, :, 1:64], m.ident[:], x[:, :, 0:63], start=True, stop=False)
                    nc.tensor.matmul(u[:, :, 1:63], m.ident[:], x[:, :, 2:64], start=False, stop=False)
                    nc.tensor.matmul(u[:, :, 0:1], m.ident[:], x[:, :, 1:2], start=False, stop=False)
                    nc.tensor.matmul(u[:, :, 0:64:63], m.ident[:], x[:, :, 1:63:61], start=False, stop=True)\
                      .then_inc(sem.lap_mm, 1)
            body(0, 0)
            pe.wait_ge(sem.win_q, 1)
            for g in range(4):
                if g >= 2:
                    pe.wait_ge(sem.win_t, g - 1)
                for i in range(4):
                    j, k = (4 * g + i) // KD, (4 * g + i) % KD
                    last = nc.tensor.transpose(ps_w[:, g % 2, ts(i, P)], m.stq[:, j, ts(k, P)], m.identb[:])
                last.then_inc(sem.win_mm, 1)
            segments(pe, [1, NC], body)

        @block.scalar
        def _(act):
            for t, s, done in ((m.st, WIN_S, sem.win_m), (m.st2, WOUT_S, sem.wout_m)):
                act.wait_ge(sem.w1_scale, 1 if t is m.st else 2)
                for j in range(KF1):
                    last = nc.scalar.activation(t[:, j], t[:, j], ACT.Identity, bias=m.magic[:], scale=s1[:, s][:, j:j + 1])
                last.then_inc(done, 1)
            act.wait_ge(sem.w1_clip, 1)
            nc.scalar.activation(m.stq[:], m.st[:], ACT.Identity, bias=m.nmagic[:]).then_inc(sem.win_q, 1)
            for g in range(4):
                act.wait_ge(sem.win_mm, g + 1)
                for i in range(4):
                    j, k = (4 * g + i) // KD, (4 * g + i) % KD
                    last = nc.scalar.copy(m.w_in[:, k, ts(j, P)], ps_w[:, g % 2, ts(i, P)])
                last.then_inc(sem.win_t, 1)
            act.wait_ge(sem.w1_clip, 2)
            nc.scalar.activation(m.w_out[:], m.st2[:], ACT.Identity, bias=m.nmagic[:]).then_inc(sem.wout_q, 1)
            act.wait_ge(sem.wout_q, 1)

        @block.vector
        def _(dve):
            def weights_scale(n, t, a, s):
                dve.wait_ge(sem.w1_loaded, 32)
                nc.vector.tensor_reduce(s1[:, a], t[:], AX.X, ALU.max, apply_absolute_value=True).then_inc(sem.w1_dve, 1)
                dve.wait_ge(sem.w1_dve, 3 * n + 1)
                nc.vector.tensor_scalar(s1[:, a], s1[:, a], 1e-8, None, ALU.max).then_inc(sem.w1_dve, 1)
                dve.wait_ge(sem.w1_dve, 3 * n + 2)
                nc.vector.reciprocal(s1[:, s], s1[:, a]).then_inc(sem.w1_rec, 1)
                dve.wait_ge(sem.w1_rec, n + 1)
                nc.vector.tensor_scalar(s1[:, s], s1[:, s], 127.0, None, ALU.mult).then_inc(sem.w1_scale, 1)
                dve.wait_ge(sem.w1_scale, n + 1)
                nc.vector.reciprocal(s1[:, a], s1[:, s]).then_inc(sem.w1_dve, 1)

            def clip(done, t):
                dve.wait_ge(done, 1)
                nc.vector.tensor_scalar(t[:], t[:], MAGIC + 127.0, MAGIC - 128.0, ALU.min, ALU.max).then_inc(sem.w1_clip, 1)

            def add(c, rep):
                for h in range(KD):
                    x = m.X[:, h, ds(c * CH, CH)]
                    nc.vector.tensor_tensor(x, x, m.Y[:, h, ds(c * CH, CH)], ALU.add).then_inc(sem.x1_sum, 1)

            def body(c, rep):
                if rep + 1 < NC:
                    add(c + 1, rep + 1)
                for h in range(KD):
                    i = 2 * c + h
                    dve.wait_ge(sem.lap_mm, i + 1)
                    nc.vector.tensor_tensor(by_batch(m.ub[:, h]), by_batch(ps_u[:, h]), per_batch(zY[:, ds(c * BPC, BPC)]), ALU.mult)
                    nc.vector.tensor_tensor(by_batch(m.ab[:, h]), by_batch(ps_lap[:, h]), per_batch(zX[:, ds(c * BPC, BPC)]), ALU.mult)\
                      .then_inc(sem.du_a, 1)
                for h in range(KD):
                    i = 2 * c + h
                    dve.wait_ge(sem.du_a, i + 1)
                    nc.vector.tensor_tensor(m.ab[:, h], m.ab[:, h], m.ub[:, h], ALU.add).then_inc(sem.du_b, 1)
                for h in range(KD):
                    i = 2 * c + h
                    dve.wait_ge(sem.du_d, i + 1)
                    dve.wait_ge(sem.du_b, i + 1)
                    nc.vector.tensor_tensor(m.du[:, c, h], m.ab[:, h], m.db[:, h], ALU.add).then_inc(sem.du_done, 1)
                for h in range(KD):
                    i = 2 * c + h
                    dve.wait_ge(sem.du_done, i + 1)
                    i2 = apart(dve, i)
                    nc.vector.tensor_reduce(m.mx1[:, ds(i2, 1)], m.du[:, c, h], AX.X, ALU.max, apply_absolute_value=True)\
                      .then_inc(sem.du_max, 1)
            add(0, 0)
            weights_scale(0, m.st, WIN_A, WIN_S)
            weights_scale(1, m.st2, WOUT_A, WOUT_S)
            body(0, 0)
            clip(sem.win_m, m.st)
            body(1, 1)
            clip(sem.wout_m, m.st2)
            segments(dve, [2, NC - 1, NC], body)
            dve.wait_ge(sem.w1_dve, 6)

        @block.gpsimd
        def _(pool):
            def body(c, rep):
                for h in range(KD):
                    i = 2 * c + h
                    x = by_batch(m.X[:, h, ds(c * CH, CH)])
                    pool.wait_ge(sem.x1_sum, i + 1)
                    pool.tensor_tensor(by_batch(m.cb[:, h]), x, per_batch(zR[:, ds(c * BPC, BPC)]), ALU.mult).then_inc(sem.du_c, 1)
                    pool.wait_ge(sem.du_c, 2 * i + 1)
                    at = apart(pool, c * BPC)
                    pool.tensor_tensor(by_batch(m.cb[:, h]), per_batch(m.zk[:, ds(at, BPC)]), by_batch(m.cb[:, h]),
                                       ALU.subtract).then_inc(sem.du_c, 1)
                    if rep >= 1:
                        pool.wait_ge(sem.du_done, i - 1)
                    pool.wait_ge(sem.du_c, 2 * i + 2)
                    at = apart(pool, c * CH)
                    pool.tensor_tensor(m.db[:, h], m.cb[:, h], m.X[:, h, ds(at, CH)], ALU.mult).then_inc(sem.du_d, 1)
            segments(pool, range(NC + 1), body)

    with nc.psum_tensor("l1_red", [P, CH], F32) as ps, nc.Block() as block:
        reduce_part(block, ps, m.mx1[:], SX, ISX, 1)

    with nc.psum_tensor("l1_h", [P, 4, CH], F32) as ps_h, nc.Block() as block:

        @block.tensor
        def _(pe):
            def body(c, rep):
                pe.wait_ge(sem.q_done, 2 * c + 2)
                for j in range(KF1):
                    t = c * KF1 + j
                    if rep >= 1 or j >= 4:
                        pe.wait_ge(sem.hid_act, t - 3)
                    for k in range(KD):
                        for n, q in enumerate((m.qH, m.qL)):
                            last = nc.tensor.matmul(ps_h[:, j % 4], m.w_in[:, k, ts(j, P)], q[:, c % 2, k],
                                                    start=k == 0 and n == 0, stop=k == KD - 1 and n == 1)
                    last.then_inc(sem.hid_mm, 1)
            segments(pe, [0, 1, NC], body)

        @block.scalar
        def _(act):
            def body(c, rep):
                for j in range(KF1):
                    t = c * KF1 + j
                    act.wait_ge(sem.hid_mm, t + 1)
                    t = apart(act, t)
                    nc.scalar.activation(m.hid[:, t], ps_h[:, j % 4], ACT.Gelu, bias=bias(m, "b_in", j),
                                         scale=s1[:, DEQ][:, j:j + 1]).then_inc(sem.hid_act, 1)
            segments(act, [0, NC], body)

        @block.vector
        def _(dve):
            def quantize(c, rep):
                for h in range(KD):
                    i = 2 * c + h
                    t = m.qt[:, c % 2, h]
                    nc.vector.tensor_scalar(t, m.du[:, c, h], s1[:, SX], MAGIC, ALU.mult, ALU.add).then_inc(sem.q_dve, 1)
                    dve.wait_ge(sem.q_dve, 3 * i + 1)
                    nc.vector.tensor_scalar(t, t, MAGIC + 32767.0, MAGIC - 32768.0, ALU.min, ALU.max).then_inc(sem.q_dve, 1)
                    dve.wait_ge(sem.q_dve, 3 * i + 2)
                    if rep >= 2:
                        dve.wait_ge(sem.hid_mm, (c - 1) * KF1)
                    nc.vector.tensor_scalar(m.qH[:, c % 2, h], t, MAGIC, None, ALU.subtract).then_inc(sem.q_dve, 1)
                    dve.wait_ge(sem.q_dve, 3 * i + 3)
                    nc.vector.scalar_tensor_tensor(m.qL[:, c % 2, h], t, MAGIC, m.qH[:, c % 2, h], ALU.subtract, ALU.subtract)\
                      .then_inc(sem.q_done, 1)

            def body(c, rep):
                if rep + 1 < NC:
                    quantize(c + 1, rep + 1)
                for j in range(KF1):
                    t = c * KF1 + j
                    dve.wait_ge(sem.hid_act, t + 1)
                    t = apart(dve, t)
                    nc.vector.tensor_reduce(m.mx2[:, ds(t, 1)], m.hid[:, t], AX.X, ALU.max, apply_absolute_value=True)\
                      .then_inc(sem.hid_max, 1)
            quantize(0, 0)
            segments(dve, [0, 1, NC - 1, NC], body)
            dve.wait_ge(sem.hid_max, NT)

    with nc.psum_tensor("l1_red2", [P, CH], F32) as ps, nc.Block() as block:
        reduce_part(block, ps, m.mx2[:], SH, ISH, 2)

    with nc.psum_tensor("l1_o", [P, 2, KD, CH], F32) as ps_o, nc.Block() as block:
        AHEAD = 3

        @block.scalar
        def _(act):
            def magic(t):
                nc.scalar.activation(m.hid[:, t], m.hid[:, t], ACT.Identity, bias=m.magic[:], scale=s1[:, SH])\
                  .then_inc(sem.g_round, 1)

            def result(c, rep):
                act.wait_ge(sem.g_mm1, KF1 * (c + 1))
                for h in range(KD):
                    if rep >= 2:
                        act.wait_ge(sem.x2_sum, 2 * c - 3 + h)
                    nc.scalar.activation(m.o1[:, c % 2, h], ps_o[:, c % 2, h], ACT.Identity, bias=bias(m, "b_out", h),
                                         scale=s1[:, ISH]).then_inc(sem.o1_act, 1)

            def body(c, rep):
                for k in range(KF1):
                    t = c * KF1 + k
                    if rep < NC - 1 or k + AHEAD < KF1:
                        magic(t + AHEAD)
                    act.wait_ge(sem.g_scaled, t + 1)
                    t = apart(act, t)
                    nc.scalar.activation(m.gH[:, k % GS], m.hid[:, t], ACT.Identity).then_inc(sem.g_high, 1)
                    if rep >= 1 and k == 2:
                        result(c - 1, rep - 1)
            for t in range(AHEAD):
                magic(t)
            segments(act, range(NC + 1), body)
            result(NC - 1, NC - 1)

        def low(eng, t, k, used, done):
            eng.wait_ge(sem.g_high, t + 1)
            if used:
                eng.wait_ge(sem.g_mm1, t - GS + 1)
            t = apart(eng, t)
            eng.tensor_tensor(m.gL[:, k % GS], m.hid[:, t], m.gH[:, k % GS].bitcast(F32), ALU.subtract).then_inc(done, 1)

        @block.gpsimd
        def _(pool):
            def result(c, rep):
                for h in range(KD):
                    pool.wait_ge(sem.o1_act, 2 * c + h + 1)
                    at = apart(pool, c * CH)
                    x = m.X[:, h, ds(at, CH)]
                    pool.tensor_tensor(x, x, m.o1[:, c % 2, h], ALU.add).then_inc(sem.x2_sum, 1)

            def body(c, rep):
                for k in range(1, KF1, 2):
                    low(pool, c * KF1 + k, k, rep >= 1 or k >= GS, sem.g_low_odd)
                    if rep >= 1 and k == 3:
                        result(c - 1, rep - 1)
            segments(pool, [0, 1, NC], body)
            result(NC - 1, NC - 1)

        @block.vector
        def _(dve):
            def clip(t):
                dve.wait_ge(sem.g_round, t + 1)
                nc.vector.tensor_scalar(m.hid[:, t], m.hid[:, t], MAGIC + 32767.0, MAGIC - 32768.0, ALU.min, ALU.max)\
                  .then_inc(sem.g_clip, 1)

            def body(c, rep):
                for k in range(KF1):
                    t = c * KF1 + k
                    if rep < NC - 1 or k < KF1 - 1:
                        clip(t + 1)
                    dve.wait_ge(sem.g_clip, t + 1)
                    if rep >= 1 or k >= GS:
                        dve.wait_ge(sem.g_mm1, t - GS + 1)
                    nc.vector.tensor_scalar(m.hid[:, t], m.hid[:, t], MAGIC, s1[:, WOUT_A][:, k:k + 1], ALU.subtract, ALU.mult)\
                      .then_inc(sem.g_scaled, 1)
                    if k % 2 == 1:
                        low(dve, t - 1, k - 1, rep >= 1 or k - 1 >= GS, sem.g_low)
            clip(0)
            segments(dve, [0, 1, NC - 1, NC], body)

        @block.tensor
        def _(pe):
            def body(c, rep):
                if rep >= 2:
                    pe.wait_ge(sem.o1_act, 2 * c - 2)
                for k in range(KF1):
                    t = c * KF1 + k
                    pe.wait_ge((sem.g_low, sem.g_low_odd)[k % 2], c * (KF1 // 2) + k // 2 + 1)
                    for h in range(KD):
                        for n, g in enumerate((m.gH, m.gL)):
                            last = nc.tensor.matmul(ps_o[:, c % 2, h], m.w_out[:, k, ts(h, P)], g[:, k % GS],
                                                    start=k == 0 and n == 0, stop=k == KF1 - 1 and n == 1)
                    last.then_inc(sem.g_mm1, 1)
            segments(pe, [0, 1, 2, NC], body)


def split_weights(nc, m, sem, loads, loaded, high, low):
    with nc.Block() as block:
        @block.sync
        def _(sp):
            for stage, src, _, _ in loads:
                sp.dma_start(stage, src).then_inc(loaded, 16)

        @block.vector
        def _(dve):
            dve.wait_ge(loaded, 16 * len(loads))
            for n, (stage, _, hi, lo) in enumerate(loads):
                nc.vector.tensor_copy(hi[:], stage).then_inc(high, 1)
            for n, (stage, _, hi, lo) in enumerate(loads):
                dve.wait_ge(high, n + 1)
                nc.vector.tensor_tensor(lo[:], stage, hi[:].bitcast(F32), ALU.subtract).then_inc(low, 1)
            dve.wait_ge(low, len(loads))


def layer2(nc, m, d, sem):
    W = m.work
    for i, name in enumerate(("f2w1H", "f2w1L")):
        place(nc, m, name, [P, KD, FF1], F32R, W + 8 * i * KB)
    for i, name in enumerate(("f2w2H", "f2w2L")):
        place(nc, m, name, [P, KF1, D], F32R, W + (16 + 8 * i) * KB)
    place(nc, m, "cw2", [P, BPC, KD, D], F32, W + 68 * KB)
    place(nc, m, "xs", [P, KD, CH], F32, W + 84 * KB)
    place(nc, m, "y2t", [P, PAIRS, D], F32, W + 88 * KB)
    place(nc, m, "y2F", [P, KD, CH], F32, W + 92 * KB)
    place(nc, m, "y2H", [P, 2, KD, CH], F32R, W + 96 * KB)
    place(nc, m, "y2L", [P, 2, KD, CH], F32R, W + 104 * KB)
    place(nc, m, "h2F_", [P, 4, CH], F32, W + 112 * KB)
    place(nc, m, "h2H_", [P, KF1, CH], F32R, W + 120 * KB)
    place(nc, m, "h2L_", [P, KF1, CH], F32R, W + 136 * KB)
    place(nc, m, "st_a", [P, KD, FF1], F32, W + 152 * KB)
    place(nc, m, "st_b", [P, KF1, D], F32, W + 160 * KB)
    w1, w2 = (m.f2w1H, m.f2w1L), (m.f2w2H, m.f2w2L)
    split_weights(nc, m, sem, ((m.st_a[:], d.f2_w1.rearrange("(k p) n -> p k n", p=P), *w1),
                               (m.st_b[:], d.f2_w2.rearrange("(k p) n -> p k n", p=P), *w2)),
                  sem.w2_loaded, sem.w2_high, sem.w2_low)

    with nc.psum_tensor("l2_tok", [P, CH], F32) as ps_tok, nc.psum_tensor("l2_turn", [P, CH], F32) as ps_turn, \
            nc.psum_tensor("l2_h", [P, 4, CH], F32) as ps_h, nc.psum_tensor("l2_o", [P, KD, CH], F32) as ps_o, \
            nc.Block() as block:

        @block.sync
        def _(sp):
            def body(c, rep):
                for b in range(BPC):
                    i = sp.value_load(m.ids2[0:1, ds(c * BPC + b, 1)], min_val=0, max_val=31)
                    if rep >= 1:
                        sp.wait_ge(sem.tok2_mm, (c - 1) * PAIRS + b // 2 + 1)
                    i = apart(sp, i)
                    sp.dma_start(m.cw2[:, b], d.c2_w[ds(i, 1)].rearrange("e (k p) o -> p (e k) o", p=P))\
                      .then_inc(sem.cw2_loaded[b], 16)
            segments(sp, [0, 1, NC], body)

        @block.tensor
        def _(pe):
            def cond(c, rep):
                pe.wait_ge(sem.xs_copied, c + 1)
                for q in range(PAIRS):
                    if rep >= 1 or q >= 1:
                        pe.wait_ge(sem.tok2_act, c * PAIRS + q)
                    for b in (2 * q, 2 * q + 1):
                        pe.wait_ge(sem.cw2_loaded[b], 16 * (c + 1))
                        for k in range(KD):
                            last = nc.tensor.matmul(ps_tok[ts(b % 2, SEQ), 0:D], m.xs[:, k, ts(b, SEQ)], m.cw2[:, b, k],
                                                    start=k == 0, stop=k == KD - 1)
                    last.then_inc(sem.tok2_mm, 1)
                pe.wait_ge(sem.tok2_act, (c + 1) * PAIRS)
                for h in range(KD):
                    if rep >= 1 or h >= 1:
                        pe.wait_ge(sem.y2_added, 2 * c + h)
                    for q in range(PAIRS):
                        last = nc.tensor.transpose(ps_turn[:, ts(q, P)], m.y2t[:, q, ts(h, P)], m.ident[:])
                    last.then_inc(sem.turn2_mm, 1)

            def body(c, rep):
                pe.wait_ge(sem.y2_low, 2 * c + 2)
                for j in range(KF1):
                    if rep >= 1 or j >= 4:
                        pe.wait_ge(sem.h2a_act, c * KF1 + j - 3)
                    for k in range(KD):
                        last = products(nc, ps_h[:, j % 4], [w[:, k, ts(j, P)] for w in w1],
                                        [y[:, c % 2, k] for y in (m.y2H, m.y2L)], k == 0, k == KD - 1)
                    last.then_inc(sem.h2a_mm, 1)
                if rep + 1 < NC:
                    cond(c + 1, rep + 1)
                if rep >= 1:
                    pe.wait_ge(sem.x3_sum, 2 * c)
                for k in range(KF1):
                    pe.wait_ge(sem.h2a_low, c * KF1 + k + 1)
                    for h in range(KD):
                        last = products(nc, ps_o[:, h], [w[:, k, ts(h, P)] for w in w2],
                                        (m.h2H_[:, k], m.h2L_[:, k]), k == 0, k == KF1 - 1)
                    last.then_inc(sem.o2_mm, 1)
            cond(0, 0)
            segments(pe, [0, 1, NC - 1, NC], body)

        @block.scalar
        def _(act):
            def cond(c, rep):
                for q in range(PAIRS):
                    act.wait_ge(sem.tok2_mm, c * PAIRS + q + 1)
                    if rep >= 1:
                        act.wait_ge(sem.turn2_mm, 2 * c)
                    nc.scalar.copy(m.y2t[:, q], ps_tok[:, 0:D]).then_inc(sem.tok2_act, 1)

            def body(c, rep):
                for j in range(KF1):
                    act.wait_ge(sem.h2a_mm, c * KF1 + j + 1)
                    if rep >= 1:
                        act.wait_ge(sem.o2_mm, (c - 1) * KF1 + j + 1)
                    if rep >= 1 or j >= 4:
                        act.wait_ge(sem.h2a_low, c * KF1 + j - 3)
                    nc.scalar.activation(m.h2H_[:, j], ps_h[:, j % 4], ACT.Relu, bias=bias(m, "f2_b1", j))
                    nc.scalar.activation(m.h2F_[:, j % 4], ps_h[:, j % 4], ACT.Relu, bias=bias(m, "f2_b1", j))\
                      .then_inc(sem.h2a_act, 1)
                if rep + 1 < NC:
                    cond(c + 1, rep + 1)
            cond(0, 0)
            segments(act, [0, 1, NC - 1, NC], body)

        @block.vector
        def _(dve):
            def copy_x(c, rep):
                if rep >= 1:
                    dve.wait_ge(sem.tok2_mm, c * PAIRS)
                c = apart(dve, c)
                nc.vector.tensor_copy(m.xs[:], m.X[:, :, ds(c * CH, CH)]).then_inc(sem.xs_copied, 1)

            def cond(c, rep):
                for h in range(KD):
                    i = 2 * c + h
                    dve.wait_ge(sem.turn2_mm, i + 1)
                    if rep >= 1:
                        dve.wait_ge(sem.y2_low, i - 1)
                    if rep >= 2:
                        dve.wait_ge(sem.h2a_mm, (c - 1) * KF1)
                    nc.vector.tensor_tensor(by_batch(m.y2F[:, h]), by_batch(ps_turn[:]),
                                            per_batch(m.cond2[:, ds(h * BATCH + c * BPC, BPC)]), ALU.add)\
                      .then_inc(sem.y2_added, 1)
                for h in range(KD):
                    dve.wait_ge(sem.y2_added, 2 * c + h + 1)
                    nc.vector.tensor_copy(m.y2H[:, c % 2, h], m.y2F[:, h]).then_inc(sem.y2_high, 1)
                for h in range(KD):
                    dve.wait_ge(sem.y2_high, 2 * c + h + 1)
                    nc.vector.tensor_tensor(m.y2L[:, c % 2, h], m.y2F[:, h], m.y2H[:, c % 2, h].bitcast(F32), ALU.subtract)\
                      .then_inc(sem.y2_low, 1)

            def result(c, rep):
                dve.wait_ge(sem.o2_mm, KF1 * (c + 1))
                for h in range(KD):
                    x = m.X[:, h, ds(c * CH, CH)]
                    nc.vector.scalar_tensor_tensor(x, ps_o[:, h], bias(m, "f2_b2", h), x, ALU.add, ALU.add)\
                      .then_inc(sem.x3_sum, 1)

            def body(c, rep):
                if rep + 1 < NC:
                    copy_x(c + 1, rep + 1)
                if rep >= 1:
                    result(c - 1, rep - 1)
                for j in range(KF1):
                    dve.wait_ge(sem.h2a_act, c * KF1 + j + 1)
                    nc.vector.tensor_tensor(m.h2L_[:, j], m.h2F_[:, j % 4], m.h2H_[:, j].bitcast(F32), ALU.subtract)\
                      .then_inc(sem.h2a_low, 1)
                if rep + 1 < NC:
                    cond(c + 1, rep + 1)
            copy_x(0, 0)
            cond(0, 0)
            segments(dve, [0, 1, NC - 1, NC], body)
            result(NC - 1, NC - 1)
            dve.wait_ge(sem.x3_sum, 2 * NC)


HS = 512
KS = HS // P
NE = 8
PART = 64
TT_ = T // P


def layer3_shared(nc, m, d, sem, zd):
    W = m.work
    for name, shape, at in (("c3w1H", [KD, FF1], 0), ("c3w1L", [KD, FF1], 8), ("c3w2H", [KF1, 192], 16),
                            ("c3w2L", [KF1, 192], 22), ("weH", [4, KF1, PART], 36), ("weL", [4, KF1, PART], 44),
                            ("x3H", [2, KD, CH], 52), ("x3L", [2, KD, CH], 60), ("h3aH", [KF1, CH], 76),
                            ("h3aL", [KF1, CH], 92), ("sw1H", [KD, HS], 112), ("sw1L", [KD, HS], 116),
                            ("sw2H", [KS, D], 120), ("sw2L", [KS, D], 124), ("zH", [KD, CH], 132), ("zL", [KD, CH], 136),
                            ("shH", [KS, CH], 140), ("shL", [KS, CH], 148)):
        place(nc, m, name, [P] + shape, F32R, W + at * KB)
    place(nc, m, "we", [P, 4, KF1, PART], F32, W + 28 * KB)
    place(nc, m, "h3aF", [P, 4, CH], F32, W + 68 * KB)
    place(nc, m, "ye", [PART, BPC, P], F32, W + 108 * KB)
    place(nc, m, "zF", [P, KD, CH], F32, W + 128 * KB)
    place(nc, m, "logits", [P, TT_, NE], F32, W + 160 * KB)
    place(nc, m, "rw", [P, KD, NE], F32, W + 161 * KB)
    place(nc, m, "rb", [P, NE], F32, W + 161 * KB + 512)
    place(nc, m, "st3a", [P, KD, FF1], F32, W + 76 * KB)
    place(nc, m, "st3b", [P, KF1, 192], F32, W + 84 * KB)
    place(nc, m, "st3c", [P, KD, HS], F32, W + 92 * KB)
    place(nc, m, "st3d", [P, KS, D], F32, W + 96 * KB)
    w1, w2, sw1, sw2 = (m.c3w1H, m.c3w1L), (m.c3w2H, m.c3w2L), (m.sw1H, m.sw1L), (m.sw2H, m.sw2L)
    split_weights(nc, m, sem, ((m.st3a[:], d.c3_w1.rearrange("(k p) n -> p k n", p=P), *w1),
                               (m.st3b[:], d.c3_w2.rearrange("(k p) n -> p k n", p=P), *w2),
                               (m.st3c[:], d.sw1.rearrange("(k p) n -> p k n", p=P), *sw1),
                               (m.st3d[:], d.sw2.rearrange("(k p) n -> p k n", p=P), *sw2)),
                  sem.w3_loaded, sem.w3_high, sem.w3_low)

    CUTS = [0, 1, 2, NC - 1, NC, NC + 1]
    with nc.psum_tensor("l3_h", [P, 4, CH], F32) as ps_h, nc.psum_tensor("l3_o", [P, KD, CH], F32) as ps_o, \
            nc.psum_tensor("l3_e", [P, CH], F32) as ps_e, nc.psum_tensor("l3_t", [P, CH], F32) as ps_t, \
            nc.Block() as block:

        @block.sync
        def _(sp):
            sp.dma_start(m.rw[:], d.rw.rearrange("(k p) n -> p k n", p=P)).then_inc(sem.r_loaded, 16)
            sp.dma_start(m.rb[:], d.rb.partition_broadcast(P)).then_inc(sem.r_loaded, 16)

            def body(c, rep):
                for b in range(BPC):
                    i = sp.value_load(m.ids0[0:1, ds(c * BPC + b, 1)], min_val=0, max_val=7)
                    if rep >= 1 or b >= 4:
                        sp.wait_ge(sem.we_low, c * BPC + b - 3)
                    i = apart(sp, i)
                    sp.dma_start(m.we[:, b % 4], d.we[ds(i, 1)].rearrange("e (k p) o -> p (e k) o", p=P))\
                      .then_inc(sem.we_loaded[b % 4], 16)
                    if rep >= 1 and b == 3:
                        spill(c - 1)

            def spill(c):
                sp.wait_ge(sem.z_done, 3 * (c + 1))
                c = apart(sp, c)
                sp.dma_start(zd[:, :, ds(c * CH, CH)], m.zF[:]).then_inc(sem.z_spilled, 16)
            segments(sp, [0, 1, NC], body)
            spill(NC - 1)
            sp.wait_ge(sem.z_spilled, 16 * NC)

        @block.tensor
        def _(pe):
            def body(c, rep):
                main, shared = rep < NC, rep >= 1
                if main:
                    pe.wait_ge(sem.x3_low, 2 * c + 2)
                    for j in range(KF1):
                        if j < 4:
                            if rep == 1:
                                pe.wait_ge(sem.h3a_act, KF1)
                            elif rep >= 2 and j < 2:
                                pe.wait_ge(sem.x4_sum, 2 * (c - 1))
                            elif rep >= 2:
                                pe.wait_ge(sem.sh_act, KS * (c - 1))
                        else:
                            pe.wait_ge(sem.h3a_act, c * KF1 + j - 3)
                        for k in range(KD):
                            last = products(nc, ps_h[:, j % 4], [w[:, k, ts(j, P)] for w in w1],
                                            [x[:, c % 2, k] for x in (m.x3H, m.x3L)], k == 0, k == KD - 1)
                        last.then_inc(sem.h3a_mm, 1)
                if shared:
                    pe.wait_ge(sem.z_low, 2 * c)
                    if not main:
                        pe.wait_ge(sem.x4_sum, 2 * (NC - 1))
                        pe.wait_ge(sem.sh_act, KS * (NC - 1))
                    for j in range(KS):
                        if main:
                            pe.wait_ge(sem.h3a_act, c * KF1 + j + 5)
                        for k in range(KD):
                            last = products(nc, ps_h[:, j], [w[:, k, ts(j, P)] for w in sw1],
                                            (m.zH[:, k], m.zL[:, k]), k == 0, k == KD - 1)
                        last.then_inc(sem.sh_mm, 1)
                    if rep == 1:
                        pe.wait_ge(sem.r_loaded, 32)
                    pe.wait_ge(sem.ye_act, c)
                    for q in range(PAIRS):
                        for k in range(KD):
                            last = nc.tensor.matmul(ps_e[:, ts(q, NE)], m.zF[:, k, ts(q, P)], m.rw[:, k],
                                                    start=k == 0, stop=k == KD - 1)
                    last.then_inc(sem.r_mm, 1)
                if main:
                    if rep >= 1:
                        pe.wait_ge(sem.z_done, 3 * c)
                    for k in range(KF1):
                        pe.wait_ge(sem.h3a_low, c * KF1 + k + 1)
                        products(nc, ps_o[:, 0], [w[:, k, 0:P] for w in w2],
                                 (m.h3aH[:, k], m.h3aL[:, k]), k == 0, k == KF1 - 1)
                        last = products(nc, ps_o[0:PART, 1], [w[:, k, P:192] for w in w2],
                                        (m.h3aH[:, k], m.h3aL[:, k]), k == 0, k == KF1 - 1)
                    last.then_inc(sem.o3_mm, 1)
                    if rep >= 1:
                        pe.wait_ge(sem.r_copied, c)
                    for b in range(BPC):
                        pe.wait_ge(sem.we_low, c * BPC + b + 1)
                        for k in range(KF1):
                            last = products(nc, ps_e[0:PART, ts(b, PART)], [h[:, k, ts(b, SEQ)] for h in (m.h3aH, m.h3aL)],
                                            [w[:, b % 4, k] for w in (m.weH, m.weL)], k == 0, k == KF1 - 1)
                        last.then_inc(sem.e_mm, 1)
                if shared:
                    for h in range(KD):
                        for k in range(KS):
                            pe.wait_ge(sem.sh_low, KS * (c - 1) + k + 1)
                            if main and h == 0 and k == KS - 1:
                                pe.wait_ge(sem.ye_act, c + 1)
                            last = products(nc, ps_h[:, h], [w[:, k, ts(h, P)] for w in sw2],
                                            (m.shH[:, k], m.shL[:, k]), k == 0, k == KS - 1)
                        last.then_inc(sem.s2_mm, 1)
                        if main and h == 0:
                            turn(c)
                elif main:
                    pe.wait_ge(sem.ye_act, c + 1)
                    turn(c)

            def turn(c):
                for b in range(BPC):
                    last = nc.tensor.transpose(ps_t[:, ts(b, SEQ)], m.ye[:, b], m.ident[0:PART, 0:PART])
                last.then_inc(sem.t3_mm, 1)
            segments(pe, CUTS, body)

        @block.scalar
        def _(act):
            def body(c, rep):
                main, shared = rep < NC, rep >= 1
                if main:
                    for j in range(KF1):
                        act.wait_ge(sem.h3a_mm, c * KF1 + j + 1)
                        if rep >= 1:
                            act.wait_ge(sem.e_mm, c * BPC)
                        if j >= 4:
                            act.wait_ge(sem.h3a_low, c * KF1 + j - 3)
                        elif rep >= 2:
                            act.wait_ge(sem.sh_low, KS * (c - 1))
                        elif rep == 1:
                            act.wait_ge(sem.h3a_low, KF1)
                        nc.scalar.activation(m.h3aH[:, j], ps_h[:, j % 4], ACT.Gelu, bias=bias(m, "c3_b1", j))
                        nc.scalar.activation(m.h3aF[:, j % 4], ps_h[:, j % 4], ACT.Gelu, bias=bias(m, "c3_b1", j))\
                          .then_inc(sem.h3a_act, 1)
                if shared:
                    for j in range(KS):
                        act.wait_ge(sem.sh_mm, KS * (c - 1) + j + 1)
                        if rep >= 2:
                            act.wait_ge(sem.s2_mm, 2 * (c - 1))
                        if main:
                            act.wait_ge(sem.h3a_low, c * KF1 + j + 5)
                        else:
                            act.wait_ge(sem.sh_low, KS * (NC - 1))
                        nc.scalar.activation(m.shH[:, j], ps_h[:, j], ACT.Gelu, bias=bias(m, "sb1", j))
                        nc.scalar.activation(m.h3aF[:, j], ps_h[:, j], ACT.Gelu, bias=bias(m, "sb1", j))\
                          .then_inc(sem.sh_act, 1)
                if main:
                    act.wait_ge(sem.e_mm, (c + 1) * BPC)
                    if rep >= 1:
                        act.wait_ge(sem.t3_mm, c)
                    else:
                        act.wait_ge(sem.ye_clear, 1)
                    nc.scalar.copy(m.ye[:, :, PART:P], ps_e[0:PART, :].rearrange("p (b s) -> p b s", s=PART))\
                      .then_inc(sem.ye_act, 1)
            segments(act, CUTS, body)

        @block.vector
        def _(dve):
            def split_x(c, rep):
                if rep >= 2:
                    dve.wait_ge(sem.h3a_mm, (c - 1) * KF1)
                for h in range(KD):
                    nc.vector.tensor_copy(m.x3H[:, c % 2, h], m.X[:, h, ds(c * CH, CH)]).then_inc(sem.x3_high, 1)
                for h in range(KD):
                    dve.wait_ge(sem.x3_high, 2 * c + h + 1)
                    nc.vector.tensor_tensor(m.x3L[:, c % 2, h], m.X[:, h, ds(c * CH, CH)],
                                            m.x3H[:, c % 2, h].bitcast(F32), ALU.subtract).then_inc(sem.x3_low, 1)

            def high_we(c, rep, b):
                dve.wait_ge(sem.we_loaded[b % 4], 16 * (2 * c + b // 4 + 1))
                if rep >= 1 or b >= 4:
                    dve.wait_ge(sem.e_mm, c * BPC + b - 3)
                nc.vector.tensor_copy(m.weH[:, b % 4], m.we[:, b % 4]).then_inc(sem.we_high, 1)

            def body(c, rep):
                main, shared = rep < NC, rep >= 1
                if main:
                    if rep + 1 < NC:
                        split_x(c + 1, rep + 1)
                    for j in range(KF1):
                        dve.wait_ge(sem.h3a_act, c * KF1 + j + 1)
                        nc.vector.tensor_tensor(m.h3aL[:, j], m.h3aF[:, j % 4], m.h3aH[:, j].bitcast(F32), ALU.subtract)\
                          .then_inc(sem.h3a_low, 1)
                        if j < 4:
                            high_we(c, rep, j)
                if shared:
                    for j in range(KS):
                        dve.wait_ge(sem.sh_act, KS * (c - 1) + j + 1)
                        nc.vector.tensor_tensor(m.shL[:, j], m.h3aF[:, j], m.shH[:, j].bitcast(F32), ALU.subtract)\
                          .then_inc(sem.sh_low, 1)
                    dve.wait_ge(sem.r_mm, c)
                    cc = apart(dve, c - 1)
                    nc.vector.tensor_tensor(m.logits[:, ds(cc * PAIRS, PAIRS)],
                                            ps_e[:, 0:PAIRS * NE].rearrange("p (q e) -> p q e", e=NE),
                                            m.rb[:].unsqueeze(1).broadcast_to([P, PAIRS, NE]), ALU.add)\
                      .then_inc(sem.r_copied, 1)
                if main:
                    for b in range(4, BPC):
                        high_we(c, rep, b)
                    dve.wait_ge(sem.o3_mm, c + 1)
                    if rep >= 1:
                        dve.wait_ge(sem.z_spilled, 16 * c)
                        dve.wait_ge(sem.r_mm, c)
                    nc.vector.tensor_scalar(m.zF[:, 0], ps_o[:, 0], bias(m, "c3_b2"), None, ALU.add).then_inc(sem.z_done, 1)
                    nc.vector.tensor_scalar(m.zF[0:PART, 1], ps_o[0:PART, 1], m.biases[0:PART, ROWS["c3_b2"] + 1:ROWS["c3_b2"] + 2],
                                            None, ALU.add).then_inc(sem.z_done, 1)
                if shared:
                    result(c - 1, 0)
                if main:
                    dve.wait_ge(sem.t3_mm, c + 1)
                    nc.vector.tensor_tensor(by_batch(m.zF[PART:P, 1]), by_batch(ps_t[PART:P, :]),
                                            m.cond3[PART:P, ds(c * BPC, BPC)].unsqueeze(2).broadcast_to([PART, BPC, SEQ]), ALU.add)\
                      .then_inc(sem.z_done, 1)
                    if rep >= 1:
                        dve.wait_ge(sem.sh_mm, KS * c)
                    for h in range(KD):
                        dve.wait_ge(sem.z_done, 3 * (c + 1))
                        nc.vector.tensor_copy(m.zH[:, h], m.zF[:, h]).then_inc(sem.z_high, 1)
                    for h in range(KD):
                        dve.wait_ge(sem.z_high, 2 * c + h + 1)
                        nc.vector.tensor_tensor(m.zL[:, h], m.zF[:, h], m.zH[:, h].bitcast(F32), ALU.subtract)\
                          .then_inc(sem.z_low, 1)
                if shared:
                    result(c - 1, 1)

            def result(c, h):
                dve.wait_ge(sem.s2_mm, 2 * c + h + 1)
                x = m.X[:, h, ds(c * CH, CH)]
                nc.vector.scalar_tensor_tensor(x, ps_h[:, h], bias(m, "sb2", h), x, ALU.add, ALU.add).then_inc(sem.x4_sum, 1)
            split_x(0, 0)
            segments(dve, CUTS, body)
            dve.wait_ge(sem.x4_sum, 2 * NC)

        @block.gpsimd
        def _(pool):
            pool.memset(m.ye[:, :, 0:PART], 0.0).then_inc(sem.ye_clear, 1)

            def body(c, rep):
                for b in range(BPC):
                    pool.wait_ge(sem.we_high, c * BPC + b + 1)
                    pool.tensor_tensor(m.weL[:, b % 4], m.we[:, b % 4], m.weH[:, b % 4].bitcast(F32), ALU.subtract)\
                      .then_inc(sem.we_low, 1)
            segments(pool, [0, NC], body)


def layer3_router(nc, m, d, sem):
    W = m.work
    r = W
    for name in ("prob", "left", "hot_a", "hot_b", "wgt"):
        place(nc, m, name, [P, TT_, NE], F32, r)
        r += KB
    place(nc, m, "rank8", [P, NE], F32, r)
    place(nc, m, "rank8i", [P, NE], I32, r + 32)
    place(nc, m, "rt", [P, TT_, 1], F32, r + 64)
    place(nc, m, "rt2", [P, TT_, NE], F32, r + 256)


    def wide(t):
        return t[:].broadcast_to([P, TT_, NE])
    with nc.Block() as block:
        @block.gpsimd
        def _(pool):
            pool.iota(m.rank8i[:], pattern=[[-1, NE]], base=NE, channel_multiplier=0).then_inc(sem.iota_done, 1)

        @block.scalar
        def _(act):
            act.wait_ge(sem.rt_dve, 2)
            nc.scalar.activation(m.prob[:], m.prob[:], ACT.Exp).then_inc(sem.rt_exp, 1)

        @block.vector
        def _(dve):
            n = [0]

            def step(i):
                i.then_inc(sem.rt_dve, 1)
                n[0] += 1
                dve.wait_ge(sem.rt_dve, n[0])
            step(nc.vector.tensor_reduce(m.rt[:], m.logits[:], AX.X, ALU.max))
            step(nc.vector.tensor_tensor(m.prob[:], m.logits[:], wide(m.rt), ALU.subtract))
            dve.wait_ge(sem.iota_done, 1)
            step(nc.vector.tensor_copy(m.rank8[:], m.rank8i[:]))
            dve.wait_ge(sem.rt_exp, 1)
            step(nc.vector.tensor_reduce(m.rt[:], m.prob[:], AX.X, ALU.add))
            step(nc.vector.reciprocal(m.rt[:], m.rt[:]))
            step(nc.vector.tensor_tensor(m.prob[:], m.prob[:], wide(m.rt), ALU.mult))

            def first_of_max(hot, p):
                step(nc.vector.tensor_reduce(m.rt[:], p[:], AX.X, ALU.max))
                step(nc.vector.tensor_tensor(m.rt2[:], p[:], wide(m.rt), ALU.is_equal))
                step(nc.vector.tensor_tensor(m.rt2[:], m.rt2[:], m.rank8[:].unsqueeze(1).broadcast_to([P, TT_, NE]), ALU.mult))
                step(nc.vector.tensor_reduce(m.rt[:], m.rt2[:], AX.X, ALU.max))
                step(nc.vector.tensor_tensor(hot[:], m.rank8[:].unsqueeze(1).broadcast_to([P, TT_, NE]), wide(m.rt), ALU.is_equal))
            first_of_max(m.hot_a, m.prob)
            step(nc.vector.scalar_tensor_tensor(m.left[:], m.hot_a[:], -2.0, m.prob[:], ALU.mult, ALU.add))
            first_of_max(m.hot_b, m.left)
            step(nc.vector.tensor_tensor(m.wgt[:], m.hot_a[:], m.hot_b[:], ALU.add))
            step(nc.vector.tensor_tensor(m.wgt[:], m.wgt[:], m.prob[:], ALU.mult))

def layer3_experts(nc, m, d, sem, zd, out):
    W = m.work
    place(nc, m, "weights_t", [NE, T], F32, W + 4 * KB)
    place(nc, m, "eb2", [NE, D], F32, W + 20 * KB)
    place(nc, m, "pick", [NE, NE, P], F32, W + 21 * KB)
    place(nc, m, "eb1t", [P, NE * KS], F32, W + 25 * KB)
    place(nc, m, "eb1r", [NE * KS, P], F32, W + 26 * KB)
    place(nc, m, "zin", [P, 2, KD, CH], F32, W + 27 * KB)
    place(nc, m, "zHa", [P, NC, KD, CH], F32R, W + 35 * KB)
    place(nc, m, "zLa", [P, NC, KD, CH], F32R, W + 67 * KB)
    place(nc, m, "ew", [P, 2048], F32, W + 99 * KB)
    place(nc, m, "ewH", [P, 2048], F32R, W + 107 * KB)
    place(nc, m, "ewL", [P, 2048], F32R, W + 115 * KB)
    place(nc, m, "ehF", [P, 4, CH], F32, W + 123 * KB)
    place(nc, m, "ehH", [P, KS, CH], F32R, W + 131 * KB)
    place(nc, m, "ehL", [P, KS, CH], F32R, W + 139 * KB)
    place(nc, m, "pb", [P, CH], F32, W + 147 * KB)
    with nc.psum_tensor("l3_wt", [P, NC, CH], F32) as ps, nc.Block() as block:
        @block.sync
        def _(sp):
            sp.dma_start(m.eb2[:], d.eb2).then_inc(sem.b_loaded, 16)
            sp.dma_start(m.eb1r[:], d.eb1.rearrange("e (k p) -> (e k) p", p=P)).then_inc(sem.b_loaded, 16)

            def body(c, rep):
                if rep >= 2:
                    sp.wait_ge(sem.za_low, c - 1)
                sp.dma_start(m.zin[:, c % 2], zd[:, :, ds(c * CH, CH)]).then_inc(sem.zin_loaded[c % 2], 16)
            for c in range(NC):
                body(c, c)

        @block.gpsimd
        def _(pool):
            pool.memset(m.pick[:], 1.0).then_inc(sem.pick_done, 1)
            pool.wait_ge(sem.pick_done, 1)
            pool.affine_select(out=m.pick[:], in_=m.pick[:], compare_op=ALU.is_equal, fill=0.0, base=0,
                               pattern=[[1, NE], [0, P]], channel_multiplier=-1).then_inc(sem.pick_done, 1)

        @block.tensor
        def _(pe):
            for t in range(TT_):
                last = nc.tensor.transpose(ps[0:NE, t // 4, ts(t % 4, P)], m.wgt[:, t], m.ident[:])
            last.then_inc(sem.wt_mm, 1)
            pe.wait_ge(sem.wt_copied, 1)
            pe.wait_ge(sem.b_loaded, 32)
            nc.tensor.transpose(ps[:, 0, 0:NE * KS], m.eb1r[:], m.ident[0:NE * KS, 0:NE * KS]).then_inc(sem.wt_mm, 1)

        @block.vector
        def _(dve):
            dve.wait_ge(sem.wt_mm, 1)
            nc.vector.tensor_copy(m.weights_t[:], ps[0:NE].rearrange("p c n -> p (c n)")).then_inc(sem.wt_copied, 1)
            dve.wait_ge(sem.wt_mm, 2)
            nc.vector.tensor_copy(m.eb1t[:], ps[:, 0, 0:NE * KS]).then_inc(sem.wt_copied, 1)
            for c in range(NC):
                dve.wait_ge(sem.zin_loaded[c % 2], 16 * (c // 2 + 1))
                nc.vector.tensor_copy(m.zHa[:, c], m.zin[:, c % 2]).then_inc(sem.za_high, 1)
                dve.wait_ge(sem.za_high, c + 1)
                nc.vector.tensor_tensor(m.zLa[:, c], m.zin[:, c % 2], m.zHa[:, c].bitcast(F32), ALU.subtract)\
                  .then_inc(sem.za_low, 1)
            dve.wait_ge(sem.wt_copied, 2)

    for e in range(NE):
        with nc.psum_tensor(f"ex_h{e}", [P, 4, CH], F32) as ps_h, nc.psum_tensor(f"ex_o{e}", [P, KD, CH], F32) as ps_o, \
                nc.psum_tensor(f"ex_p{e}", [P, CH], F32) as ps_p, nc.Block() as block:
            N1 = KD * HS
            E0 = e * NC
            w1 = [t[:, 0:N1].rearrange("p (k n) -> p k n", k=KD) for t in (m.ewH, m.ewL)]
            w2 = [t[:, N1:2048].rearrange("p (k n) -> p k n", k=KS) for t in (m.ewH, m.ewL)]

            @block.sync
            def _(sp):
                sp.dma_start(m.ew[:, 0:N1].rearrange("p (k n) -> p k n", k=KD), d.ew1[e].rearrange("(k p) n -> p k n", p=P)).then_inc(sem.ew_loaded, 16)
                sp.dma_start(m.ew[:, N1:2048].rearrange("p (k n) -> p k n", k=KS), d.ew2[e].rearrange("(k p) n -> p k n", p=P)).then_inc(sem.ew_loaded, 16)

            @block.tensor
            def _(pe):
                pe.wait_ge(sem.ew_low, e + 1)

                def body(c, rep):
                    t = c + E0
                    if rep >= 1:
                        pe.wait_ge(sem.pb_act, t)
                    nc.tensor.matmul(ps_p[:], m.pick[:, e], m.weights_t[:, ds(c * CH, CH)], start=True, stop=True).then_inc(sem.pb_mm, 1)
                    for j in range(KS):
                        if rep >= 1:
                            pe.wait_ge(sem.eh_act, (t - 1) * KS + j + 1)
                        for k in range(KD):
                            last = products(nc, ps_h[:, j], [w[:, k, ts(j, P)] for w in w1],
                                            [z[:, c, k] for z in (m.zHa, m.zLa)], k == 0, k == KD - 1)
                        last.then_inc(sem.eh_mm, 1)
                    if rep >= 1:
                        pe.wait_ge(sem.x5_sum, 2 * t)
                    for h in range(KD):
                        for k in range(KS):
                            pe.wait_ge(sem.eh_low, t * KS + k + 1)
                            last = products(nc, ps_o[:, h], [w[:, k, ts(h, P)] for w in w2],
                                            (m.ehH[:, k], m.ehL[:, k]), k == 0, e > 0 and k == KS - 1)
                        if e == 0:
                            last = nc.tensor.matmul(ps_o[:, h], m.eb2[:, ts(h, P)], m.weights_t[:, ds(c * CH, CH)], start=False, stop=True)
                        last.then_inc(sem.eo_mm, 1)
                segments(pe, [0, 1, NC], body)

            @block.scalar
            def _(act):
                def body(c, rep):
                    t = c + E0
                    act.wait_ge(sem.pb_mm, t + 1)
                    if rep >= 1:
                        act.wait_ge(sem.eh_mul, t * KS)
                    nc.scalar.copy(m.pb[:], ps_p[:]).then_inc(sem.pb_act, 1)
                    for j in range(KS):
                        act.wait_ge(sem.eh_mm, t * KS + j + 1)
                        if rep >= 1:
                            act.wait_ge(sem.eh_low, (t - 1) * KS + j + 1)
                        nc.scalar.activation(m.ehF[:, j], ps_h[:, j], ACT.Gelu, bias=m.eb1t[:, e * KS + j:e * KS + j + 1])\
                          .then_inc(sem.eh_act, 1)
                segments(act, [0, 1, NC], body)

            @block.vector
            def _(dve):
                dve.wait_ge(sem.ew_loaded, 32 * (e + 1))
                nc.vector.tensor_copy(m.ewH[:], m.ew[:]).then_inc(sem.ew_high, 1)
                dve.wait_ge(sem.ew_high, e + 1)
                nc.vector.tensor_tensor(m.ewL[:], m.ew[:], m.ewH[:].bitcast(F32), ALU.subtract).then_inc(sem.ew_low, 1)

                def result(c, rep):
                    t = c + E0
                    for h in range(KD):
                        dve.wait_ge(sem.eo_mm, 2 * t + h + 1)
                        x = m.X[:, h, ds(c * CH, CH)]
                        nc.vector.tensor_tensor(x, ps_o[:, h], x, ALU.add).then_inc(sem.x5_sum, 1)

                def body(c, rep):
                    t = c + E0
                    for j in range(KS):
                        dve.wait_ge(sem.eh_act, t * KS + j + 1)
                        nc.vector.tensor_tensor(m.ehF[:, j], m.ehF[:, j], m.pb[:], ALU.mult).then_inc(sem.eh_mul, 1)
                        dve.wait_ge(sem.eh_mul, t * KS + j + 1)
                        if rep >= 1:
                            dve.wait_ge(sem.eo_mm, 2 * t)
                        nc.vector.tensor_copy(m.ehH[:, j], m.ehF[:, j]).then_inc(sem.eh_high, 1)
                        dve.wait_ge(sem.eh_high, t * KS + j + 1)
                        nc.vector.tensor_tensor(m.ehL[:, j], m.ehF[:, j], m.ehH[:, j].bitcast(F32), ALU.subtract).then_inc(sem.eh_low, 1)
                    result(c, rep)
                segments(dve, [0, 1, NC], body)
                dve.wait_ge(sem.x5_sum, 2 * NC * (e + 1))

    with nc.Block() as block:
        @block.sync
        def _(sp):
            sp.dma_start(out.rearrange("(k p) t -> p k t", p=P), m.X[:]).then_inc(sem.out_stored, 16)
            sp.wait_ge(sem.out_stored, 16)


L0_SEMS = """rows_clear prep_pool prep_load prep_pe prep_hot prep_dve tok_mm tok_act turn_mm y_added yh_cond yl_cond yh_upd
yl_upd h1_act h1_mm h1_low h2_act h2_mm h2_low h3_act h3_mm h3_low th_act th_mm sums g_act g_mm coupl_b
cs_done t0_done t1_done y_upd""".split()
L1_SEMS = """x1_sum lap l1_const w1_loaded w1_rec w1_dve w1_scale w1_clip win_m wout_m win_q wout_q win_mm win_t lap_mm
du_a du_b du_c du_d du_done du_max q_done q_dve hid_mm hid_act hid_max g_round g_clip g_low_odd g_scaled
g_high g_low g_mm1 o1_act x2_sum""".split()
L2_SEMS = """w2_loaded w2_high w2_low xs_copied tok2_mm tok2_act turn2_mm y2_added y2_high y2_low h2a_mm h2a_act h2a_low
o2_mm x3_sum""".split()
L3_SEMS = """b_loaded pick_done wt_mm wt_copied za_high za_low ew_loaded ew_high ew_low pb_mm pb_act eh_mm eh_act eh_mul
eh_high eh_low eo_mm x5_sum out_stored w3_loaded w3_high w3_low r_loaded we_low we_high z_done z_spilled
x3_low x3_high h3a_act h3a_mm h3a_low x4_sum sh_act sh_mm sh_low z_low z_high ye_act ye_clear r_mm r_copied
o3_mm e_mm s2_mm t3_mm iota_done rt_dve rt_exp""".split()


INPUTS = {
    "xT": "x", "ids0": "itok_B_0_7", "ids2": "itok_B_0_30", "zX": "condB_zX", "zY": "condB_zY", "zR": "condB_zR",
    "c0_wT": "L0_cond_weight", "c0_b": "L0_cond_bias",
    "cn_w1": "L0_ffn_cn_w1", "cn_b1": "L0_ffn_cn_b1", "cn_w2": "L0_ffn_cn_w2", "cn_b2": "L0_ffn_cn_b2",
    "cn_w3": "L0_ffn_cn_w3", "cn_b3": "L0_ffn_cn_b3", "cn_w4": "L0_ffn_cn_w4", "cn_b4": "L0_ffn_cn_b4",
    "gc_w1": "L0_ffn_gc_w1", "gc_b1": "L0_ffn_gc_b1", "gc_w2": "L0_ffn_gc_w2", "gc_b2": "L0_ffn_gc_b2",
    "gc_w3": "L0_ffn_gc_w3", "gc_b3": "L0_ffn_gc_b3", "ar": "L0_ffn_adaptive_range",
    "w_inT": "L1_ffn_W_in", "b_in": "L1_ffn_b_in", "w_out": "L1_ffn_W_out", "b_out": "L1_ffn_b_out",
    "c2_w": "L2_cond_W", "c2_b": "L2_cond_b", "f2_w1": "L2_ffn_w1", "f2_b1": "L2_ffn_b1",
    "f2_w2": "L2_ffn_w2", "f2_b2": "L2_ffn_b2", "c3_w1": "L3_cond_W1", "c3_b1": "L3_cond_b1",
    "c3_w2": "L3_cond_W2", "c3_b2": "L3_cond_b2", "we": "L3_cond_We", "be": "L3_cond_be",
    "rw": "L3_ffn_router_w", "rb": "L3_ffn_router_b", "sw1": "L3_ffn_sw1", "sb1": "L3_ffn_sb1",
    "sw2": "L3_ffn_sw2", "sb2": "L3_ffn_sb2", "ew1": "L3_ffn_rw1", "eb1": "L3_ffn_rb1",
    "ew2": "L3_ffn_rw2", "eb2": "L3_ffn_rb2",
}


def acquire(nc, sem, names, groups=()):
    for name in names:
        sem[name] = nc.alloc_semaphore(name)
    for name, n in groups:
        sem[name] = [nc.alloc_semaphore(f"{name}{i}") for i in range(n)]


def retire(nc, sem):
    for s in list(sem.values()):
        nc.clear_and_free_semaphores(s if isinstance(s, list) else [s])
    sem.clear()
    nc.all_engine_barrier()


def build(nc, d, out):
    sem, m = Names(), Names()
    common_memory(nc, m)
    acquire(nc, sem, L0_SEMS, (("x_loaded", 5), ("cw_loaded", SLOTS)))
    prepare(nc, m, d, sem)
    layer0(nc, m, d, sem)
    retire(nc, sem)
    acquire(nc, sem, L1_SEMS, (("red_mm", 2), ("red_v", 2)))
    layer1(nc, m, d, sem)
    retire(nc, sem)
    acquire(nc, sem, L2_SEMS, (("cw2_loaded", BPC),))
    layer2(nc, m, d, sem)
    retire(nc, sem)
    acquire(nc, sem, L3_SEMS, (("we_loaded", 4), ("zin_loaded", 2)))
    zd = nc.dram_tensor("z_rows", (P, KD, T), F32).ap()
    layer3_shared(nc, m, d, sem, zd)
    layer3_router(nc, m, d, sem)
    layer3_experts(nc, m, d, sem, zd, out)


def lay_out(program_name, a):
    if program_name == "xT":
        return a.reshape(T, D).T
    if program_name == "c0_wT":
        return a.transpose(0, 2, 1)
    if program_name == "w_inT":
        return a.T
    return a


def kernel(**inputs):
    import numpy as np
    import concourse.bacc as bacc
    from concourse.bass_utils import run_bass_kernel_spmd

    nc = bacc.Bacc("TRN2", target_bir_lowering=False, num_devices=1)
    arrays, aps = {}, {}
    for name, source in INPUTS.items():
        a = np.ascontiguousarray(lay_out(name, np.asarray(inputs[source])))
        arrays["in_" + name] = a
        aps[name] = nc.dram_tensor("in_" + name, a.shape, mybir.dt.from_np(a.dtype), kind="ExternalInput").ap()
    out = nc.dram_tensor("out_0", (D, T), F32, kind="ExternalOutput").ap()
    build(nc, Names(aps), out)
    result = run_bass_kernel_spmd(nc, [arrays], core_ids=[0])
    return np.ascontiguousarray(result.results[0]["out_0"].T).reshape(BATCH, SEQ, D)
```

```python
import concourse.bass as bass
from concourse import mybir

ALU = mybir.AluOpType
ACT = mybir.ActivationFunctionType
F32 = mybir.dt.float32
F32R = mybir.dt.float32r
BF16 = mybir.dt.bfloat16
I32 = mybir.dt.int32
U32 = mybir.dt.uint32
AX = mybir.AxisListType
ds, ts = bass.ds, bass.ts


class Names(dict):
    def __getattr__(self, name):
        return self[name]


P = 128
BATCH, SEQ, D = 64, 64, 256
T = BATCH * SEQ
KD = D // P
CH = 512
NC = T // CH
BPC = CH // SEQ
PAIRS = CH // P
SLOTS = 6
NCYCLE = 3
NITEM = NCYCLE * NC
KB = 1024
MAGIC = 1.5 * 2.0 ** 23
PARTS = ((0, 0), (0, 1), (1, 0))


def segments(eng, cuts, body):
    for lo, hi in zip(cuts, cuts[1:]):
        if hi - lo == 1:
            body(lo, lo)
        else:
            with eng.Fori(lo, hi) as step:
                body(step, lo)


def apart(eng, x):
    return x if isinstance(x, int) else eng.snap(x)


def within(x, lo, hi):
    return lo <= x < hi


def per_batch(ap, n=BPC):
    return ap.unsqueeze(2).broadcast_to([P, n, SEQ])


def by_batch(ap):
    return ap.rearrange("p (b s) -> p b s", s=SEQ)


def products(nc, out, weights, data, start, stop):
    for n, (a, b) in enumerate(PARTS):
        last = nc.tensor.matmul(out, weights[a], data[b], start=start and n == 0,
                                stop=stop and n == len(PARTS) - 1)
    return last



def place(nc, m, name, shape, dt, at):
    m[name] = nc.alloc_sbuf_tensor_at(name, shape, dt, offset=m.base + at)


ROWS = {}


def bias_rows(d):
    out, r = [], 0
    for name, ap in (("cn_b1", d.cn_b1), ("cn_b2", d.cn_b2), ("cn_b3", d.cn_b3), ("gc_b1", d.gc_b1),
                     ("gc_b2", d.gc_b2), ("b_in", d.b_in), ("b_out", d.b_out), ("f2_b1", d.f2_b1),
                     ("f2_b2", d.f2_b2), ("c3_b1", d.c3_b1), ("c3_b2", d.c3_b2), ("sb1", d.sb1),
                     ("sb2", d.sb2)):
        n = ap.shape[0]
        ROWS[name] = r
        full = n // P
        if full:
            out.append((r, full, P, ap[0:full * P].rearrange("(k p) -> k p", p=P)))
        if n % P:
            out.append((r + full, 1, n % P, ap[full * P:n].rearrange("(k p) -> k p", k=1)))
        r += (n + P - 1) // P
    ROWS["end"] = r
    return out


def common_memory(nc, m):
    m.base = (nc.sbuf_base + 31) // 32 * 32
    place(nc, m, "X", [P, KD, T], F32, 0)
    c = 32 * KB

    def const(name, cols, dt=F32):
        nonlocal c
        place(nc, m, name, [P, cols], dt, c)
        c += (cols * 4 + 31) // 32 * 32

    const("ident", P)
    const("biases", 48)
    const("cond0", KD * BATCH)
    const("coupl_b", BATCH)
    const("zxyz", 3 * BATCH)
    const("zk", BATCH)
    const("cond2", KD * BATCH)
    const("cond3", BATCH)
    const("scal", 16)
    const("magic", 1)
    const("nmagic", 1)
    const("ones1", P)
    const("ids0", BATCH, I32)
    const("ids2", BATCH, I32)
    m.work = 36 * KB + 512
    assert c <= m.work

    m.AR, m.SIGN, m.AMUL, m.GMUL, m.TENTH, m.CNB4, m.GCB3 = range(7)


def sc(m, col, rows=P):
    return m.scal[0:rows, col:col + 1]



def prepare(nc, m, d, sem):
    W = m.work
    w = W + 98 * KB + 16 * KB
    for name, rows, cols in (("cnw1", P, KD * 256), ("cnw2", P, KD * 128), ("cnw3", P, 64), ("cnw4", 64, 128)):
        for part in "HL":
            place(nc, m, name + part, [rows, cols], F32R, w)
            w += cols * 4
    for name, rows, cols in (("gcw1", P, KD * 128), ("gcw2", P, 64), ("gcw3", 64, 128)):
        place(nc, m, name, [rows, cols], F32, w)
        w += cols * 4
    m.l0_work = w
    s = w
    stage = {}
    for name, rows, cols in (("cnw1", P, KD * 256), ("cnw2", P, KD * 128), ("cnw3", P, 64), ("cnw4", 64, 128)):
        place(nc, m, "stage_" + name, [rows, cols], F32, s)
        stage[name] = m["stage_" + name]
        s += cols * 4
    for name, rows, cols, dt in (("rows", 48, P, F32), ("w4col", 64, 1, F32), ("g3col", 64, 1, F32),
                                 ("b0tab", 8, 256, F32), ("b2tab", 32, 256, F32), ("betab", 8, 64, F32),
                                 ("idsB0", 32, BATCH, I32), ("idsB2", 32, BATCH, I32),
                                 ("hot0", 32, BATCH, F32), ("hot2", 32, BATCH, F32),
                                 ("lane", P, 1, F32), ("laneI", P, 1, I32), ("b4col", P, 1, F32),
                                 ("gb3col", P, 1, F32), ("ones", 64, P, F32)):
        place(nc, m, "t_" + name, [rows, cols], dt, s)
        s += max(32, cols * 4)
    with nc.psum_tensor("prep_psum", [P, 5, 512], F32) as ps:
        rows = bias_rows(d)
        with nc.Block() as block:
            @block.gpsimd
            def _(pool):
                pool.memset(m.t_rows[:], 0.0).then_inc(sem.rows_clear, 1)
                pool.memset(m.ident[:], 1.0).then_inc(sem.prep_pool, 1)
                pool.memset(m.t_ones[:], 1.0)
                pool.memset(m.magic[:], MAGIC)
                pool.memset(m.nmagic[:], -MAGIC).then_inc(sem.prep_pool, 1)
                pool.iota(m.t_laneI[:], pattern=[[0, 1]], base=0, channel_multiplier=1).then_inc(sem.prep_pool, 1)
                pool.memset(m.scal[:], 0.0).then_inc(sem.prep_pool, 1)
                pool.wait_ge(sem.prep_pool, 4)
                pool.affine_select(out=m.ident[:], in_=m.ident[:], compare_op=ALU.is_equal, fill=0.0, base=0,
                                   pattern=[[1, P]], channel_multiplier=-1).then_inc(sem.prep_pool, 1)
                pool.wait_ge(sem.prep_pool, 5)

            @block.sync
            def _(sp):
                n = 0
                for dst, src in ((m.ids0[0:1, :], d.ids0.unsqueeze(0)), (m.ids2[0:1, :], d.ids2.unsqueeze(0)),
                                 (stage["cnw1"].rearrange("p (k n) -> p k n", k=KD), d.cn_w1.rearrange("(k p) n -> p k n", p=P)),
                                 (stage["cnw2"].rearrange("p (k n) -> p k n", k=KD), d.cn_w2.rearrange("(k p) n -> p k n", p=P)),
                                 (stage["cnw3"][:], d.cn_w3),
                                 (m.t_w4col[:], d.cn_w4), (m.t_g3col[:], d.gc_w3),
                                 (m.gcw1.rearrange("p (k n) -> p k n", k=KD), d.gc_w1.rearrange("(k p) n -> p k n", p=P)),
                                 (m.gcw2[:], d.gc_w2)):
                    sp.dma_start(dst, src).then_inc(sem.prep_load, 16)
                    n += 1
                for c in range(4):
                    sp.dma_start(m.X[:, :, ts(c, CH)], d.xT.rearrange("(k p) t -> p k t", p=P)[:, :, ts(c, CH)])\
                      .then_inc(sem.x_loaded[c], 16)
                sp.dma_start(m.X[:, :, 4 * CH:T], d.xT.rearrange("(k p) t -> p k t", p=P)[:, :, 4 * CH:T])\
                  .then_inc(sem.x_loaded[4], 16)

            @block.scalar
            def _(act):
                for dst, src in ((m.t_b0tab[:], d.c0_b), (m.t_b2tab[:], d.c2_b), (m.t_betab[:], d.be),
                                 (m.t_idsB0[:], d.ids0.partition_broadcast(32)), (m.t_idsB2[:], d.ids2.partition_broadcast(32)),
                                 (m.t_b4col[:], d.cn_b4.partition_broadcast(P)), (m.t_gb3col[:], d.gc_b3.partition_broadcast(P)),
                                 (m.scal[:, m.AR:m.AR + 1], d.ar.partition_broadcast(P)),
                                 (m.zxyz[:, 0:64], d.zX.partition_broadcast(P)),
                                 (m.zxyz[:, 64:128], d.zY.partition_broadcast(P)),
                                 (m.zxyz[:, 128:192], d.zR.partition_broadcast(P))):
                    act.wait_ge(sem.prep_pool, 4)
                    act.dma_start(dst, src).then_inc(sem.prep_load, 16)
                act.wait_ge(sem.rows_clear, 1)
                for r, n, cols, src in rows:
                    act.dma_start(m.t_rows[r:r + n, 0:cols], src).then_inc(sem.prep_load, 16)

        n_loads = 9 + 11 + len(rows)
        with nc.Block() as block:
            @block.tensor
            def _(pe):
                pe.wait_ge(sem.prep_load, 16 * n_loads)
                nc.tensor.transpose(ps[:, 0, 0:48], m.t_rows[:], m.ident[0:48, 0:48]).then_inc(sem.prep_pe, 1)
                pe.wait_ge(sem.prep_hot, 2)
                for k in range(KD):
                    nc.tensor.matmul(ps[:, 1, ts(k, BATCH)], m.t_b0tab[:, ts(k, P)], m.t_hot0[0:8, :], start=True, stop=True)
                    nc.tensor.matmul(ps[:, 2, ts(k, BATCH)], m.t_b2tab[:, ts(k, P)], m.t_hot2[:], start=True, stop=True)
                nc.tensor.matmul(ps[64:128, 3, 0:BATCH], m.t_betab[:], m.t_hot0[0:8, :], start=True, stop=True)\
                  .then_inc(sem.prep_pe, 1)

            @block.vector
            def _(dve):
                own = sem.prep_dve
                n = [0]

                def mark(i):
                    i.then_inc(own, 1)
                    n[0] += 1
                    return n[0]
                dve.wait_ge(sem.prep_load, 16 * n_loads)
                mark(nc.vector.tensor_copy(m.t_lane[:], m.t_laneI[:]))
                mark(nc.vector.tensor_copy(m.t_hot0[:], m.t_idsB0[:]))
                dve.wait_ge(own, mark(nc.vector.tensor_copy(m.t_hot2[:], m.t_idsB2[:])))
                for t in (m.t_hot0, m.t_hot2):
                    nc.vector.tensor_scalar(t[:], t[:], m.t_lane[0:32, :], None, ALU.is_equal).then_inc(sem.prep_hot, 1)
                mark(nc.vector.memset(m.scal[0:64, m.SIGN:m.SIGN + 1], 1.0))
                mark(nc.vector.memset(m.scal[64:128, m.SIGN:m.SIGN + 1], -1.0))
                mark(nc.vector.tensor_scalar(m.stage_cnw4[:], m.t_ones[:], m.t_w4col[:], None, ALU.mult))
                mark(nc.vector.tensor_scalar(m.gcw3[:], m.t_ones[:], m.t_g3col[:], None, ALU.mult))
                mark(nc.vector.tensor_scalar(sc(m, m.CNB4), m.t_b4col[:], 0.5, None, ALU.mult))
                mark(nc.vector.tensor_scalar(sc(m, m.GCB3), m.t_gb3col[:], 0.5, None, ALU.mult))
                for name in ("cnw1", "cnw2", "cnw3"):
                    mark(nc.vector.tensor_copy(m[name + "H"][:], stage[name][:]))
                dve.wait_ge(own, n[0])
                mark(nc.vector.tensor_copy(m.cnw4H[:], m.stage_cnw4[:]))
                mark(nc.vector.tensor_scalar(sc(m, m.AMUL), sc(m, m.AR), sc(m, m.SIGN), 0.3, ALU.mult, ALU.mult))
                mark(nc.vector.tensor_scalar(sc(m, m.GMUL), sc(m, m.AR), sc(m, m.SIGN), 0.7, ALU.mult, ALU.mult))
                mark(nc.vector.tensor_scalar(sc(m, m.TENTH), sc(m, m.SIGN), 0.1, None, ALU.mult))
                mark(nc.vector.scalar_tensor_tensor(m.zk[:], m.zxyz[:, 64:128], -2.0, m.zxyz[:, 128:192],
                                                    ALU.mult, ALU.add))
                dve.wait_ge(own, n[0])
                for name in ("cnw1", "cnw2", "cnw3", "cnw4"):
                    nc.vector.tensor_tensor(m[name + "L"][:], stage[name][:],
                                            m[name + "H"][:].bitcast(F32), ALU.subtract)
                dve.wait_ge(sem.prep_pe, 1)
                mark(nc.vector.tensor_copy(m.biases[:], ps[:, 0, 0:48]))
                dve.wait_ge(sem.prep_pe, 2)
                mark(nc.vector.tensor_copy(m.cond0[:], ps[:, 1, 0:KD * BATCH]))
                mark(nc.vector.tensor_copy(m.cond2[:], ps[:, 2, 0:KD * BATCH]))
                mark(nc.vector.tensor_copy(m.cond3[64:128, :], ps[64:128, 3, 0:BATCH]))
                dve.wait_ge(own, n[0])
                mark(nc.vector.memset(m.cond3[0:64, :], 0.0))
                dve.wait_ge(own, n[0])
                r = ROWS["c3_b2"] + 1
                mark(nc.vector.tensor_scalar(m.cond3[0:64, :], m.cond3[0:64, :], m.biases[0:64, r:r + 1], None, ALU.add))
                dve.wait_ge(own, n[0])


def bias(m, name, k=0, rows=P):
    r = ROWS[name] + k
    return m.biases[0:rows, r:r + 1]



def layer0(nc, m, d, sem):
    W = m.work
    place(nc, m, "Y", [P, KD, T], F32, W)
    place(nc, m, "YH", [P, KD, T], F32R, W + 32 * KB)
    place(nc, m, "YL", [P, KD, T], F32R, W + 64 * KB)
    place(nc, m, "cw", [P, SLOTS, KD, D], F32, W + 98 * KB)
    place(nc, m, "yt", [P, PAIRS, D], F32, W + 110 * KB)
    place(nc, m, "l0_small", [P, 72], F32, W + 96 * KB)
    a = m.l0_work
    for name, rows, shape, dt in (("h1F", P, [KD, CH], F32), ("h1H", P, [2, KD, CH], F32R), ("h1L", P, [2, KD, CH], F32R),
                                  ("h2F", P, [CH], F32), ("h2H", P, [2, CH], F32R), ("h2L", P, [2, CH], F32R),
                                  ("h3F", 64, [CH], F32), ("h3H", 64, [2, CH], F32R), ("h3L", 64, [2, CH], F32R),
                                  ("th", P, [CH], F32), ("cs", P, [CH], F32), ("t0", P, [CH], F32), ("t1", P, [CH], F32)):
        place(nc, m, name, [rows] + shape, dt, a)
        size = 4
        for x in shape:
            size *= x
        a += size
    gsum = m.l0_small[:, 40:72].rearrange("p (s n) -> p s n", s=2)
    g1 = m.l0_small[:, 16:24]
    g2 = m.l0_small[0:64, 24:32]
    tg = m.l0_small[:, 32:40]
    cnw1 = [x.rearrange("p (k n) -> p k n", k=KD) for x in (m.cnw1H, m.cnw1L)]
    cnw2 = [x.rearrange("p (k n) -> p k n", k=KD) for x in (m.cnw2H, m.cnw2L)]
    gcw1 = m.gcw1.rearrange("p (k n) -> p k n", k=KD)
    LAST_SPLIT = NITEM - NC

    CUTS = [*range(NC + 5), LAST_SPLIT + 4, *range(NITEM, NITEM + 5)]

    with nc.psum_tensor("l0_tok", [P, CH], F32) as ps_tok, nc.psum_tensor("l0_turn", [P, CH], F32) as ps_turn, \
            nc.psum_tensor("l0_h1", [P, KD, CH], F32) as ps_h1, \
            nc.psum_tensor("l0_h2", [P, CH], F32) as ps_h2, nc.psum_tensor("l0_h3", [P, CH], F32) as ps_h3, \
            nc.psum_tensor("l0_th", [P, CH], F32) as ps_th, nc.psum_tensor("l0_g", [P, CH], F32) as ps_g, \
            nc.Block() as block:

        @block.sync
        def _(sp):
            for b in range(BATCH):
                i = sp.value_load(m.ids0[0:1, b:b + 1], min_val=0, max_val=7)
                if b >= SLOTS:
                    sp.wait_ge(sem.tok_mm, (b - SLOTS) // 2 + 1)
                sp.dma_start(m.cw[:, b % SLOTS], d.c0_wT[ds(i, 1)].rearrange("e (k p) o -> p (e k) o", p=P))\
                  .then_inc(sem.cw_loaded[b % SLOTS], 16)

        @block.tensor
        def _(pe):
            def pair(c, rep, q):
                if q == 0:
                    pe.wait_ge(sem.x_loaded[min(c, 4)], 16)
                if c >= 1 or q >= 1:
                    pe.wait_ge(sem.tok_act, c * PAIRS + q)
                for b in (c * BPC + 2 * q, c * BPC + 2 * q + 1):
                    pe.wait_ge(sem.cw_loaded[b % SLOTS], 16 * (b // SLOTS + 1))
                    for k in range(KD):
                        last = nc.tensor.matmul(ps_tok[ts(b % 2, SEQ), 0:D], m.X[:, k, ts(b, SEQ)], m.cw[:, b % SLOTS, k],
                                                start=k == 0, stop=k == KD - 1)
                last.then_inc(sem.tok_mm, 1)

            def turn(c, rep, h):
                pe.wait_ge(sem.tok_act, (c + 1) * PAIRS)
                if rep >= 1 or h >= 1:
                    pe.wait_ge(sem.y_added, 2 * c + h)
                for q in range(PAIRS):
                    last = nc.tensor.transpose(ps_turn[:, ts(q, P)], m.yt[:, q, ts(h, P)], m.ident[:])
                last.then_inc(sem.turn_mm, 1)

            def body(j, rep):
                cond = rep + 2 < NC
                if cond:
                    pair(j + 2, rep + 2, 0)
                if rep < NITEM:
                    c = j % NC
                    if rep < NC:
                        pe.wait_ge(sem.yh_cond, 2 * j + 2)
                        pe.wait_ge(sem.yl_cond, 2 * j + 2)
                    else:
                        pe.wait_ge(sem.yh_upd, 2 * (j - NC) + 2)
                        pe.wait_ge(sem.yl_upd, 2 * (j - NC) + 2)
                    for h in range(KD):
                        if rep >= 1:
                            pe.wait_ge(sem.h1_act, 2 * j - 1 + h)
                        for k in range(KD):
                            last = products(nc, ps_h1[:, h], [w[:, k, ts(h, P)] for w in cnw1],
                                            [y[:, k, ds(c * CH, CH)] for y in (m.YH, m.YL)], k == 0, k == KD - 1)
                        last.then_inc(sem.h1_mm, 1)
                        if cond and h == 0:
                            pair(j + 2, rep + 2, 1)
                if rep < NC + 2:
                    if rep >= 1:
                        pe.wait_ge(sem.g_act, j)
                    if rep < NC:
                        pe.wait_ge(sem.sums, j + 1)
                        for k in range(KD):
                            last = nc.tensor.matmul(ps_g[:, 0:BPC], gcw1[:, k], gsum[:, j % 2, ts(k, BPC)], start=k == 0, stop=k == KD - 1)
                    if within(rep - 1, 0, NC):
                        last = nc.tensor.matmul(ps_g[0:64, 8:16], m.gcw2[:], g1, start=True, stop=True)
                    if within(rep - 2, 0, NC):
                        last = nc.tensor.matmul(ps_g[:, 16:24], m.gcw3[:], g2, start=True, stop=True)
                    last.then_inc(sem.g_mm, 1)
                if cond:
                    pair(j + 2, rep + 2, 2)
                if within(rep - 1, 0, NITEM):
                    i = j - 1
                    pe.wait_ge(sem.h1_act, 2 * i + 2)
                    pe.wait_ge(sem.h1_low, 2 * i + 2)
                    if rep - 1 >= 1:
                        pe.wait_ge(sem.h2_act, i)
                    for k in range(KD):
                        last = products(nc, ps_h2[:], [w[:, k] for w in cnw2],
                                        [x[:, i % 2, k] for x in (m.h1H, m.h1L)], k == 0, k == KD - 1)
                    last.then_inc(sem.h2_mm, 1)
                if cond:
                    pair(j + 2, rep + 2, 3)
                if within(rep - 2, 0, NITEM):
                    i = j - 2
                    pe.wait_ge(sem.h2_act, i + 1)
                    pe.wait_ge(sem.h2_low, i + 1)
                    if rep - 2 >= 1:
                        pe.wait_ge(sem.h3_act, i)
                    products(nc, ps_h3[0:64, :], (m.cnw3H[:], m.cnw3L[:]),
                             [x[:, i % 2] for x in (m.h2H, m.h2L)], True, True).then_inc(sem.h3_mm, 1)
                if cond:
                    turn(j + 2, rep + 2, 0)
                if within(rep - 3, 0, NITEM):
                    i = j - 3
                    pe.wait_ge(sem.h3_act, i + 1)
                    pe.wait_ge(sem.h3_low, i + 1)
                    if rep - 3 >= 1:
                        pe.wait_ge(sem.th_act, i)
                    products(nc, ps_th[:], (m.cnw4H[:], m.cnw4L[:]),
                             [x[:, i % 2] for x in (m.h3H, m.h3L)], True, True).then_inc(sem.th_mm, 1)
                if cond:
                    turn(j + 2, rep + 2, 1)

            for c in range(2):
                for q in range(PAIRS):
                    pair(c, c, q)
                for h in range(KD):
                    turn(c, c, h)
            segments(pe, CUTS, body)

        @block.scalar
        def _(act):
            def pair(c, rep, q):
                act.wait_ge(sem.tok_mm, c * PAIRS + q + 1)
                if rep >= 1:
                    act.wait_ge(sem.turn_mm, 2 * c)
                nc.scalar.copy(m.yt[:, q], ps_tok[:, 0:D]).then_inc(sem.tok_act, 1)

            def body(j, rep):
                cond = rep + 2 < NC
                if cond:
                    pair(j + 2, rep + 2, 0)
                if rep < NITEM:
                    for h in range(KD):
                        act.wait_ge(sem.h1_mm, 2 * j + h + 1)
                        if rep >= 1:
                            act.wait_ge(sem.h1_low, 2 * j - 1 + h)
                        if rep >= 2:
                            act.wait_ge(sem.h2_mm, j - 1)
                        nc.scalar.activation(m.h1H[:, j % 2, h], ps_h1[:, h], ACT.Gelu, bias=bias(m, "cn_b1", h))
                        nc.scalar.activation(m.h1F[:, h], ps_h1[:, h], ACT.Gelu, bias=bias(m, "cn_b1", h))\
                          .then_inc(sem.h1_act, 1)
                        if cond and h == 0:
                            pair(j + 2, rep + 2, 1)
                if rep < NC + 2:
                    act.wait_ge(sem.g_mm, j + 1)
                    if within(rep - 2, 0, NC):
                        if rep - 2 >= 1:
                            act.wait_ge(sem.coupl_b, j - 2)
                        last = nc.scalar.activation(tg, ps_g[:, 16:24], ACT.Tanh, bias=sc(m, m.GCB3), scale=0.5)
                    if within(rep - 1, 0, NC):
                        last = nc.scalar.activation(g2, ps_g[0:64, 8:16], ACT.Gelu, bias=bias(m, "gc_b2", rows=64))
                    if rep < NC:
                        last = nc.scalar.activation(g1, ps_g[:, 0:BPC], ACT.Gelu, bias=bias(m, "gc_b1"), scale=1.0 / SEQ)
                    last.then_inc(sem.g_act, 1)
                if cond:
                    pair(j + 2, rep + 2, 2)
                if within(rep - 1, 0, NITEM):
                    i = j - 1
                    act.wait_ge(sem.h2_mm, i + 1)
                    if rep - 1 >= 1:
                        act.wait_ge(sem.h2_low, i)
                    if rep - 1 >= 2:
                        act.wait_ge(sem.h3_mm, i - 1)
                    nc.scalar.activation(m.h2H[:, i % 2], ps_h2[:], ACT.Gelu, bias=bias(m, "cn_b2"))
                    nc.scalar.activation(m.h2F[:], ps_h2[:], ACT.Gelu, bias=bias(m, "cn_b2")).then_inc(sem.h2_act, 1)
                if cond:
                    pair(j + 2, rep + 2, 3)
                if within(rep - 2, 0, NITEM):
                    i = j - 2
                    act.wait_ge(sem.h3_mm, i + 1)
                    if rep - 2 >= 1:
                        act.wait_ge(sem.h3_low, i)
                    if rep - 2 >= 2:
                        act.wait_ge(sem.th_mm, i - 1)
                    nc.scalar.activation(m.h3H[:, i % 2], ps_h3[0:64, :], ACT.Gelu, bias=bias(m, "cn_b3", rows=64))
                    nc.scalar.activation(m.h3F[:], ps_h3[0:64, :], ACT.Gelu, bias=bias(m, "cn_b3", rows=64))\
                      .then_inc(sem.h3_act, 1)
                if within(rep - 3, 0, NITEM):
                    i = j - 3
                    act.wait_ge(sem.th_mm, i + 1)
                    if rep - 3 >= 1:
                        act.wait_ge(sem.cs_done, i)
                    nc.scalar.activation(m.th[:], ps_th[:], ACT.Tanh, bias=sc(m, m.CNB4), scale=0.5)\
                      .then_inc(sem.th_act, 1)
            for c in range(2):
                for q in range(PAIRS):
                    pair(c, c, q)
            segments(act, CUTS, body)

        @block.vector
        def _(dve):
            def cond(c, rep):
                if rep >= 2:
                    dve.wait_ge(sem.g_mm, c - 1)
                for h in range(KD):
                    dve.wait_ge(sem.turn_mm, KD * c + h + 1)
                    nc.vector.tensor_tensor(by_batch(m.Y[:, h, ds(c * CH, CH)]), by_batch(ps_turn[:]),
                                            per_batch(m.cond0[:, ds(h * BATCH + c * BPC, BPC)]), ALU.add)\
                      .then_inc(sem.y_added, 1)
                for h in range(KD):
                    dve.wait_ge(sem.y_added, 2 * c + 1 + h)
                    nc.vector.tensor_copy(m.YH[:, h, ds(c * CH, CH)], m.Y[:, h, ds(c * CH, CH)]).then_inc(sem.yh_cond, 1)
                for h in range(KD):
                    last = nc.vector.tensor_reduce(gsum[:, c % 2, ts(h, BPC)], by_batch(m.Y[:, h, ds(c * CH, CH)]), AX.X, ALU.add)
                last.then_inc(sem.sums, 1)

            def body(j, rep):
                upd = within(rep - 4, 0, NITEM)
                u = j - 4
                if rep < NITEM:
                    for h in range(KD):
                        dve.wait_ge(sem.h1_act, 2 * j + h + 1)
                        if rep >= 2:
                            dve.wait_ge(sem.h2_mm, j - 1)
                        nc.vector.tensor_tensor(m.h1L[:, j % 2, h], m.h1F[:, h], m.h1H[:, j % 2, h].bitcast(F32),
                                                ALU.subtract).then_inc(sem.h1_low, 1)
                if upd:
                    uc = u % NC
                    dve.wait_ge(sem.th_act, u + 1)
                    if rep - 4 < NC:
                        dve.wait_ge(sem.coupl_b, u + 1)
                    if rep - 4 >= 1:
                        dve.wait_ge(sem.t1_done, u)
                    nc.vector.scalar_tensor_tensor(by_batch(m.cs[:]), by_batch(m.th[:]), sc(m, m.AMUL),
                                                   per_batch(m.coupl_b[:, ds(uc * BPC, BPC)]), ALU.mult, ALU.add)\
                      .then_inc(sem.cs_done, 1)
                    dve.wait_ge(sem.cs_done, u + 1)
                    nc.vector.tensor_tensor(m.t0[:], m.cs[:], m.Y[:, 1, ds(uc * CH, CH)], ALU.mult).then_inc(sem.t0_done, 1)
                if within(rep - 1, 0, NITEM):
                    i = j - 1
                    dve.wait_ge(sem.h2_act, i + 1)
                    if rep - 1 >= 2:
                        dve.wait_ge(sem.h3_mm, i - 1)
                    nc.vector.tensor_tensor(m.h2L[:, i % 2], m.h2F[:], m.h2H[:, i % 2].bitcast(F32), ALU.subtract)\
                      .then_inc(sem.h2_low, 1)
                if within(rep - 2, 0, NITEM):
                    i = j - 2
                    dve.wait_ge(sem.h3_act, i + 1)
                    if rep - 2 >= 2:
                        dve.wait_ge(sem.th_mm, i - 1)
                    nc.vector.tensor_tensor(m.h3L[:, i % 2], m.h3F[:], m.h3H[:, i % 2].bitcast(F32), ALU.subtract)\
                      .then_inc(sem.h3_low, 1)
                if within(rep - 2, 0, NC):
                    i = j - 2
                    dve.wait_ge(sem.g_act, j + 1)
                    nc.vector.tensor_scalar(m.coupl_b[:, ds(i * BPC, BPC)], tg, sc(m, m.GMUL), sc(m, m.TENTH),
                                            ALU.mult, ALU.add).then_inc(sem.coupl_b, 1)
                if rep + 2 < NC:
                    cond(j + 2, rep + 2)
                if upd:
                    dve.wait_ge(sem.t0_done, u + 1)
                    dve.wait_ge(sem.t1_done, u + 1)
                    nc.vector.tensor_tensor(m.Y[:, 0, ds(uc * CH, CH)], m.Y[:, 0, ds(uc * CH, CH)], m.t0[:], ALU.add)\
                      .then_inc(sem.y_upd, 1)
                    nc.vector.tensor_tensor(m.Y[:, 1, ds(uc * CH, CH)], m.Y[:, 1, ds(uc * CH, CH)], m.t1[:], ALU.subtract)\
                      .then_inc(sem.y_upd, 1)
                    if rep - 4 < LAST_SPLIT:
                        for h in range(KD):
                            dve.wait_ge(sem.y_upd, 2 * u + 1 + h)
                            nc.vector.tensor_copy(m.YH[:, h, ds(uc * CH, CH)], m.Y[:, h, ds(uc * CH, CH)])\
                              .then_inc(sem.yh_upd, 1)
            cond(0, 0)
            cond(1, 1)
            segments(dve, CUTS, body)

        @block.gpsimd
        def _(pool):
            def low(c, done, made, at):
                for h in range(KD):
                    pool.wait_ge(made, 2 * at + h + 1)
                    pool.tensor_tensor(m.YL[:, h, ds(c * CH, CH)], m.Y[:, h, ds(c * CH, CH)],
                                       m.YH[:, h, ds(c * CH, CH)].bitcast(F32), ALU.subtract).then_inc(done, 1)

            def body(j, rep):
                upd = within(rep - 4, 0, NITEM)
                u = j - 4
                if upd:
                    uc = u % NC
                    pool.wait_ge(sem.cs_done, u + 1)
                    if rep - 4 >= 1:
                        pool.wait_ge(sem.y_upd, 2 * u)
                    pool.tensor_tensor(m.t1[:], m.cs[:], m.Y[:, 0, ds(uc * CH, CH)], ALU.mult).then_inc(sem.t1_done, 1)
                if rep + 2 < NC:
                    low(j + 2, sem.yl_cond, sem.yh_cond, j + 2)
                if upd and rep - 4 < LAST_SPLIT:
                    low(uc, sem.yl_upd, sem.yh_upd, u)
            low(0, sem.yl_cond, sem.yh_cond, 0)
            low(1, sem.yl_cond, sem.yh_cond, 1)
            segments(pool, CUTS, body)



FF1 = 1024
KF1 = FF1 // P


def layer1(nc, m, d, sem):
    W = m.work
    NT = NC * KF1
    place(nc, m, "hid", [P, NT, CH], F32, W)
    place(nc, m, "du", [P, NC, KD, CH], F32, W + 96 * KB)
    w = W + 128 * KB
    place(nc, m, "w_in", [P, KD, FF1], BF16, w)
    place(nc, m, "w_out", [P, KF1, D], F32R, w + 4 * KB)
    place(nc, m, "s1", [P, 64], F32, w + 12 * KB)
    w += 13 * KB
    place(nc, m, "lap", [P, KD, D], F32, W + 32 * KB)
    place(nc, m, "st", [P, KF1, D], F32, W + 34 * KB)
    place(nc, m, "st2", [P, KF1, D], F32, W + 42 * KB)
    place(nc, m, "stq", [P, KF1, D], BF16, W + 50 * KB)
    for i, name in enumerate(("ub", "cb", "db", "ab")):
        place(nc, m, name, [P, 2, CH], F32, W + (54 + 4 * i) * KB)
    place(nc, m, "identb", [P, P], BF16, W + 70 * KB)
    place(nc, m, "mx1", [P, 2 * NC], F32, W + 71 * KB)
    place(nc, m, "qt", [P, 2, KD, CH], F32, w)
    place(nc, m, "qH", [P, 2, KD, CH], BF16, w + 8 * KB)
    place(nc, m, "qL", [P, 2, KD, CH], BF16, w + 12 * KB)
    place(nc, m, "mx2", [P, NT], F32, w + 16 * KB)
    GS = 4
    place(nc, m, "gH", [P, GS, CH], F32R, w)
    place(nc, m, "gL", [P, GS, CH], F32R, w + 8 * KB)
    place(nc, m, "o1", [P, 2, KD, CH], F32, w + 18 * KB)
    s1 = m.s1
    WIN_A, WIN_S, WOUT_A, WOUT_S, DEQ, KOUT = (slice(8 * i, 8 * i + 8) for i in range(6))
    MX, AMAX, SX, ISX, SH, ISH, C32767, C127 = (slice(48 + i, 49 + i) for i in range(8))

    def reduce_part(block, ps, mx, scale, inverse, stage):
        mm, v = sem.red_mm[stage - 1], sem.red_v[stage - 1]

        @block.tensor
        def _(pe):
            pe.wait_ge(v, 1)
            nc.tensor.transpose(ps[0:1, 0:P], s1[:, MX], m.ident[:]).then_inc(mm, 1)
            pe.wait_ge(v, 2)
            nc.tensor.matmul(ps[:, P:P + 1], m.ones1[0:1, :], s1[0:1, AMAX], start=True, stop=True).then_inc(mm, 1)

        @block.vector
        def _(dve):
            nc.vector.tensor_reduce(s1[:, MX], mx, AX.X, ALU.max).then_inc(v, 1)
            dve.wait_ge(mm, 1)
            nc.vector.tensor_reduce(s1[0:1, AMAX], ps[0:1, 0:P], AX.X, ALU.max).then_inc(v, 1)
            dve.wait_ge(mm, 2)
            nc.vector.tensor_scalar(s1[:, MX], ps[:, P:P + 1], 1e-8, None, ALU.max).then_inc(v, 1)
            dve.wait_ge(v, 3)
            nc.vector.reciprocal(s1[:, AMAX], s1[:, MX]).then_inc(v, 1)
            dve.wait_ge(v, 4)
            nc.vector.tensor_scalar(s1[:, scale], s1[:, AMAX], 32767.0, None, ALU.mult).then_inc(v, 1)
            dve.wait_ge(v, 5)
            nc.vector.reciprocal(s1[:, inverse], s1[:, scale]).then_inc(v, 1)
            dve.wait_ge(v, 6)
            if stage == 1:
                nc.vector.tensor_scalar(s1[:, DEQ], s1[:, WIN_A], s1[:, inverse], None, ALU.mult).then_inc(v, 1)
                dve.wait_ge(v, 7)

    with nc.Block() as block:
        @block.sync
        def _(sp):
            sp.dma_start(m.st[:], d.w_inT.rearrange("(j p) k -> p j k", p=P)).then_inc(sem.w1_loaded, 16)
            sp.dma_start(m.st2[:], d.w_out.rearrange("(j p) k -> p j k", p=P)).then_inc(sem.w1_loaded, 16)

        @block.vector
        def _(dve):
            nc.vector.memset(s1[:, C32767], 32767.0)
            nc.vector.memset(s1[:, C127], 127.0)
            nc.vector.tensor_copy(m.identb[:], m.ident[:])
            nc.vector.memset(m.ones1[:], 1.0).then_inc(sem.l1_const, 1)
            dve.wait_ge(sem.l1_const, 1)

        @block.gpsimd
        def _(pool):
            n = [0]

            def step(i):
                i.then_inc(sem.lap, 1)
                n[0] += 1
                pool.wait_ge(sem.lap, n[0])
            step(pool.memset(m.lap[:], 0.0))
            for k in range(KD):
                for off, v in ((0, -2.0), (1, 1.0), (-1, 1.0)):
                    step(pool.affine_select(out=m.lap[:, k], in_=m.lap[:, k], compare_op=ALU.not_equal, fill=v,
                                            base=k * P - off, pattern=[[-1, D]], channel_multiplier=1))
            step(pool.affine_select(out=m.lap[:, 0, 0:1], in_=m.lap[:, 0, 0:1], compare_op=ALU.not_equal, fill=2.0,
                                    base=-1, pattern=[[0, 1]], channel_multiplier=1))
            step(pool.affine_select(out=m.lap[:, 1, D - 1:D], in_=m.lap[:, 1, D - 1:D], compare_op=ALU.not_equal, fill=2.0,
                                    base=-(P - 2), pattern=[[0, 1]], channel_multiplier=1))

    zX, zY, zR = (m.zxyz[:, ts(i, BATCH)] for i in range(3))

    with nc.psum_tensor("l1_lap", [P, 2, CH], F32) as ps_lap, nc.psum_tensor("l1_u", [P, 2, CH], F32) as ps_u, \
            nc.psum_tensor("l1_wt", [P, 2, 1024], BF16) as ps_w, nc.Block() as block:

        @block.tensor
        def _(pe):
            def body(c, rep):
                pe.wait_ge(sem.x1_sum, 2 * c + 2)
                for h in range(KD):
                    if rep >= 1:
                        pe.wait_ge(sem.du_a, 2 * c - 1 + h)
                    for k in range(KD):
                        nc.tensor.matmul(ps_lap[:, h], m.lap[:, k, ts(h, P)], m.X[:, k, ds(c * CH, CH)],
                                         start=k == 0, stop=k == KD - 1)
                    x = by_batch(m.X[:, h, ds(c * CH, CH)])
                    u = by_batch(ps_u[:, h])
                    nc.tensor.matmul(u[:, :, 1:64], m.ident[:], x[:, :, 0:63], start=True, stop=False)
                    nc.tensor.matmul(u[:, :, 1:63], m.ident[:], x[:, :, 2:64], start=False, stop=False)
                    nc.tensor.matmul(u[:, :, 0:1], m.ident[:], x[:, :, 1:2], start=False, stop=False)
                    nc.tensor.matmul(u[:, :, 0:64:63], m.ident[:], x[:, :, 1:63:61], start=False, stop=True)\
                      .then_inc(sem.lap_mm, 1)
            body(0, 0)
            pe.wait_ge(sem.win_q, 1)
            for g in range(4):
                if g >= 2:
                    pe.wait_ge(sem.win_t, g - 1)
                for i in range(4):
                    j, k = (4 * g + i) // KD, (4 * g + i) % KD
                    last = nc.tensor.transpose(ps_w[:, g % 2, ts(i, P)], m.stq[:, j, ts(k, P)], m.identb[:])
                last.then_inc(sem.win_mm, 1)
            segments(pe, [1, NC], body)

        @block.scalar
        def _(act):
            for t, s, done in ((m.st, WIN_S, sem.win_m), (m.st2, WOUT_S, sem.wout_m)):
                act.wait_ge(sem.w1_scale, 1 if t is m.st else 2)
                for j in range(KF1):
                    last = nc.scalar.activation(t[:, j], t[:, j], ACT.Identity, bias=m.magic[:], scale=s1[:, s][:, j:j + 1])
                last.then_inc(done, 1)
            act.wait_ge(sem.w1_clip, 1)
            nc.scalar.activation(m.stq[:], m.st[:], ACT.Identity, bias=m.nmagic[:]).then_inc(sem.win_q, 1)
            for g in range(4):
                act.wait_ge(sem.win_mm, g + 1)
                for i in range(4):
                    j, k = (4 * g + i) // KD, (4 * g + i) % KD
                    last = nc.scalar.copy(m.w_in[:, k, ts(j, P)], ps_w[:, g % 2, ts(i, P)])
                last.then_inc(sem.win_t, 1)
            act.wait_ge(sem.w1_clip, 2)
            nc.scalar.activation(m.w_out[:], m.st2[:], ACT.Identity, bias=m.nmagic[:]).then_inc(sem.wout_q, 1)
            act.wait_ge(sem.wout_q, 1)

        @block.vector
        def _(dve):
            def weights_scale(n, t, a, s):
                dve.wait_ge(sem.w1_loaded, 32)
                nc.vector.tensor_reduce(s1[:, a], t[:], AX.X, ALU.max, apply_absolute_value=True).then_inc(sem.w1_dve, 1)
                dve.wait_ge(sem.w1_dve, 3 * n + 1)
                nc.vector.tensor_scalar(s1[:, a], s1[:, a], 1e-8, None, ALU.max).then_inc(sem.w1_dve, 1)
                dve.wait_ge(sem.w1_dve, 3 * n + 2)
                nc.vector.reciprocal(s1[:, s], s1[:, a]).then_inc(sem.w1_rec, 1)
                dve.wait_ge(sem.w1_rec, n + 1)
                nc.vector.tensor_scalar(s1[:, s], s1[:, s], 127.0, None, ALU.mult).then_inc(sem.w1_scale, 1)
                dve.wait_ge(sem.w1_scale, n + 1)
                nc.vector.reciprocal(s1[:, a], s1[:, s]).then_inc(sem.w1_dve, 1)

            def clip(done, t):
                dve.wait_ge(done, 1)
                nc.vector.tensor_scalar(t[:], t[:], MAGIC + 127.0, MAGIC - 128.0, ALU.min, ALU.max).then_inc(sem.w1_clip, 1)

            def add(c, rep):
                for h in range(KD):
                    x = m.X[:, h, ds(c * CH, CH)]
                    nc.vector.tensor_tensor(x, x, m.Y[:, h, ds(c * CH, CH)], ALU.add).then_inc(sem.x1_sum, 1)

            def body(c, rep):
                if rep + 1 < NC:
                    add(c + 1, rep + 1)
                for h in range(KD):
                    i = 2 * c + h
                    dve.wait_ge(sem.lap_mm, i + 1)
                    nc.vector.tensor_tensor(by_batch(m.ub[:, h]), by_batch(ps_u[:, h]), per_batch(zY[:, ds(c * BPC, BPC)]), ALU.mult)
                    nc.vector.tensor_tensor(by_batch(m.ab[:, h]), by_batch(ps_lap[:, h]), per_batch(zX[:, ds(c * BPC, BPC)]), ALU.mult)\
                      .then_inc(sem.du_a, 1)
                for h in range(KD):
                    i = 2 * c + h
                    dve.wait_ge(sem.du_a, i + 1)
                    nc.vector.tensor_tensor(m.ab[:, h], m.ab[:, h], m.ub[:, h], ALU.add).then_inc(sem.du_b, 1)
                for h in range(KD):
                    i = 2 * c + h
                    dve.wait_ge(sem.du_d, i + 1)
                    dve.wait_ge(sem.du_b, i + 1)
                    nc.vector.tensor_tensor(m.du[:, c, h], m.ab[:, h], m.db[:, h], ALU.add).then_inc(sem.du_done, 1)
                for h in range(KD):
                    i = 2 * c + h
                    dve.wait_ge(sem.du_done, i + 1)
                    i2 = apart(dve, i)
                    nc.vector.tensor_reduce(m.mx1[:, ds(i2, 1)], m.du[:, c, h], AX.X, ALU.max, apply_absolute_value=True)\
                      .then_inc(sem.du_max, 1)
            add(0, 0)
            weights_scale(0, m.st, WIN_A, WIN_S)
            weights_scale(1, m.st2, WOUT_A, WOUT_S)
            body(0, 0)
            clip(sem.win_m, m.st)
            body(1, 1)
            clip(sem.wout_m, m.st2)
            segments(dve, [2, NC - 1, NC], body)
            dve.wait_ge(sem.w1_dve, 6)

        @block.gpsimd
        def _(pool):
            def body(c, rep):
                for h in range(KD):
                    i = 2 * c + h
                    x = by_batch(m.X[:, h, ds(c * CH, CH)])
                    pool.wait_ge(sem.x1_sum, i + 1)
                    pool.tensor_tensor(by_batch(m.cb[:, h]), x, per_batch(zR[:, ds(c * BPC, BPC)]), ALU.mult).then_inc(sem.du_c, 1)
                    pool.wait_ge(sem.du_c, 2 * i + 1)
                    at = apart(pool, c * BPC)
                    pool.tensor_tensor(by_batch(m.cb[:, h]), per_batch(m.zk[:, ds(at, BPC)]), by_batch(m.cb[:, h]),
                                       ALU.subtract).then_inc(sem.du_c, 1)
                    if rep >= 1:
                        pool.wait_ge(sem.du_done, i - 1)
                    pool.wait_ge(sem.du_c, 2 * i + 2)
                    at = apart(pool, c * CH)
                    pool.tensor_tensor(m.db[:, h], m.cb[:, h], m.X[:, h, ds(at, CH)], ALU.mult).then_inc(sem.du_d, 1)
            segments(pool, range(NC + 1), body)

    with nc.psum_tensor("l1_red", [P, CH], F32) as ps, nc.Block() as block:
        reduce_part(block, ps, m.mx1[:], SX, ISX, 1)

    with nc.psum_tensor("l1_h", [P, 4, CH], F32) as ps_h, nc.Block() as block:

        @block.tensor
        def _(pe):
            def body(c, rep):
                pe.wait_ge(sem.q_done, 2 * c + 2)
                for j in range(KF1):
                    t = c * KF1 + j
                    if rep >= 1 or j >= 4:
                        pe.wait_ge(sem.hid_act, t - 3)
                    for k in range(KD):
                        for n, q in enumerate((m.qH, m.qL)):
                            last = nc.tensor.matmul(ps_h[:, j % 4], m.w_in[:, k, ts(j, P)], q[:, c % 2, k],
                                                    start=k == 0 and n == 0, stop=k == KD - 1 and n == 1)
                    last.then_inc(sem.hid_mm, 1)
            segments(pe, [0, 1, NC], body)

        @block.scalar
        def _(act):
            def body(c, rep):
                for j in range(KF1):
                    t = c * KF1 + j
                    act.wait_ge(sem.hid_mm, t + 1)
                    t = apart(act, t)
                    nc.scalar.activation(m.hid[:, t], ps_h[:, j % 4], ACT.Gelu, bias=bias(m, "b_in", j),
                                         scale=s1[:, DEQ][:, j:j + 1]).then_inc(sem.hid_act, 1)
            segments(act, [0, NC], body)

        @block.vector
        def _(dve):
            def quantize(c, rep):
                for h in range(KD):
                    i = 2 * c + h
                    t = m.qt[:, c % 2, h]
                    nc.vector.tensor_scalar(t, m.du[:, c, h], s1[:, SX], MAGIC, ALU.mult, ALU.add).then_inc(sem.q_dve, 1)
                    dve.wait_ge(sem.q_dve, 3 * i + 1)
                    nc.vector.tensor_scalar(t, t, MAGIC + 32767.0, MAGIC - 32768.0, ALU.min, ALU.max).then_inc(sem.q_dve, 1)
                    dve.wait_ge(sem.q_dve, 3 * i + 2)
                    if rep >= 2:
                        dve.wait_ge(sem.hid_mm, (c - 1) * KF1)
                    nc.vector.tensor_scalar(m.qH[:, c % 2, h], t, MAGIC, None, ALU.subtract).then_inc(sem.q_dve, 1)
                    dve.wait_ge(sem.q_dve, 3 * i + 3)
                    nc.vector.scalar_tensor_tensor(m.qL[:, c % 2, h], t, MAGIC, m.qH[:, c % 2, h], ALU.subtract, ALU.subtract)\
                      .then_inc(sem.q_done, 1)

            def body(c, rep):
                if rep + 1 < NC:
                    quantize(c + 1, rep + 1)
                for j in range(KF1):
                    t = c * KF1 + j
                    dve.wait_ge(sem.hid_act, t + 1)
                    t = apart(dve, t)
                    nc.vector.tensor_reduce(m.mx2[:, ds(t, 1)], m.hid[:, t], AX.X, ALU.max, apply_absolute_value=True)\
                      .then_inc(sem.hid_max, 1)
            quantize(0, 0)
            segments(dve, [0, 1, NC - 1, NC], body)
            dve.wait_ge(sem.hid_max, NT)

    with nc.psum_tensor("l1_red2", [P, CH], F32) as ps, nc.Block() as block:
        reduce_part(block, ps, m.mx2[:], SH, ISH, 2)

    with nc.psum_tensor("l1_o", [P, 2, KD, CH], F32) as ps_o, nc.Block() as block:
        AHEAD = 3

        @block.scalar
        def _(act):
            def magic(t):
                nc.scalar.activation(m.hid[:, t], m.hid[:, t], ACT.Identity, bias=m.magic[:], scale=s1[:, SH])\
                  .then_inc(sem.g_round, 1)

            def result(c, rep):
                act.wait_ge(sem.g_mm1, KF1 * (c + 1))
                for h in range(KD):
                    if rep >= 2:
                        act.wait_ge(sem.x2_sum, 2 * c - 3 + h)
                    nc.scalar.activation(m.o1[:, c % 2, h], ps_o[:, c % 2, h], ACT.Identity, bias=bias(m, "b_out", h),
                                         scale=s1[:, ISH]).then_inc(sem.o1_act, 1)

            def body(c, rep):
                for k in range(KF1):
                    t = c * KF1 + k
                    if rep < NC - 1 or k + AHEAD < KF1:
                        magic(t + AHEAD)
                    act.wait_ge(sem.g_scaled, t + 1)
                    t = apart(act, t)
                    nc.scalar.activation(m.gH[:, k % GS], m.hid[:, t], ACT.Identity).then_inc(sem.g_high, 1)
                    if rep >= 1 and k == 2:
                        result(c - 1, rep - 1)
            for t in range(AHEAD):
                magic(t)
            segments(act, range(NC + 1), body)
            result(NC - 1, NC - 1)

        def low(eng, t, k, used, done):
            eng.wait_ge(sem.g_high, t + 1)
            if used:
                eng.wait_ge(sem.g_mm1, t - GS + 1)
            t = apart(eng, t)
            eng.tensor_tensor(m.gL[:, k % GS], m.hid[:, t], m.gH[:, k % GS].bitcast(F32), ALU.subtract).then_inc(done, 1)

        @block.gpsimd
        def _(pool):
            def result(c, rep):
                for h in range(KD):
                    pool.wait_ge(sem.o1_act, 2 * c + h + 1)
                    at = apart(pool, c * CH)
                    x = m.X[:, h, ds(at, CH)]
                    pool.tensor_tensor(x, x, m.o1[:, c % 2, h], ALU.add).then_inc(sem.x2_sum, 1)

            def body(c, rep):
                for k in range(1, KF1, 2):
                    low(pool, c * KF1 + k, k, rep >= 1 or k >= GS, sem.g_low_odd)
                    if rep >= 1 and k == 3:
                        result(c - 1, rep - 1)
            segments(pool, [0, 1, NC], body)
            result(NC - 1, NC - 1)

        @block.vector
        def _(dve):
            def clip(t):
                dve.wait_ge(sem.g_round, t + 1)
                nc.vector.tensor_scalar(m.hid[:, t], m.hid[:, t], MAGIC + 32767.0, MAGIC - 32768.0, ALU.min, ALU.max)\
                  .then_inc(sem.g_clip, 1)

            def body(c, rep):
                for k in range(KF1):
                    t = c * KF1 + k
                    if rep < NC - 1 or k < KF1 - 1:
                        clip(t + 1)
                    dve.wait_ge(sem.g_clip, t + 1)
                    if rep >= 1 or k >= GS:
                        dve.wait_ge(sem.g_mm1, t - GS + 1)
                    nc.vector.tensor_scalar(m.hid[:, t], m.hid[:, t], MAGIC, s1[:, WOUT_A][:, k:k + 1], ALU.subtract, ALU.mult)\
                      .then_inc(sem.g_scaled, 1)
                    if k % 2 == 1:
                        low(dve, t - 1, k - 1, rep >= 1 or k - 1 >= GS, sem.g_low)
            clip(0)
            segments(dve, [0, 1, NC - 1, NC], body)

        @block.tensor
        def _(pe):
            def body(c, rep):
                if rep >= 2:
                    pe.wait_ge(sem.o1_act, 2 * c - 2)
                for k in range(KF1):
                    t = c * KF1 + k
                    pe.wait_ge((sem.g_low, sem.g_low_odd)[k % 2], c * (KF1 // 2) + k // 2 + 1)
                    for h in range(KD):
                        for n, g in enumerate((m.gH, m.gL)):
                            last = nc.tensor.matmul(ps_o[:, c % 2, h], m.w_out[:, k, ts(h, P)], g[:, k % GS],
                                                    start=k == 0 and n == 0, stop=k == KF1 - 1 and n == 1)
                    last.then_inc(sem.g_mm1, 1)
            segments(pe, [0, 1, 2, NC], body)


def split_weights(nc, m, sem, loads, loaded, high, low):
    with nc.Block() as block:
        @block.sync
        def _(sp):
            for stage, src, _, _ in loads:
                if src is not None:
                    sp.dma_start(stage, src).then_inc(loaded, 16)

        @block.vector
        def _(dve):
            dve.wait_ge(loaded, 16 * len([1 for _, src, _, _ in loads if src is not None]))
            for n, (stage, _, hi, lo) in enumerate(loads):
                nc.vector.tensor_copy(hi[:], stage).then_inc(high, 1)
            for n, (stage, _, hi, lo) in enumerate(loads):
                dve.wait_ge(high, n + 1)
                nc.vector.tensor_tensor(lo[:], stage, hi[:].bitcast(F32), ALU.subtract).then_inc(low, 1)
            dve.wait_ge(low, len(loads))


def layer2(nc, m, d, sem):
    W = m.work
    for i, name in enumerate(("f2w1H", "f2w1L")):
        place(nc, m, name, [P, KD, FF1], F32R, W + 8 * i * KB)
    for i, name in enumerate(("f2w2H", "f2w2L")):
        place(nc, m, name, [P, KF1, D], F32R, W + (16 + 8 * i) * KB)
    place(nc, m, "cw2", [P, BPC, KD, D], F32, W + 68 * KB)
    place(nc, m, "xs", [P, KD, CH], F32, W + 84 * KB)
    place(nc, m, "y2t", [P, PAIRS, D], F32, W + 88 * KB)
    place(nc, m, "y2F", [P, KD, CH], F32, W + 92 * KB)
    place(nc, m, "y2H", [P, 2, KD, CH], F32R, W + 96 * KB)
    place(nc, m, "y2L", [P, 2, KD, CH], F32R, W + 104 * KB)
    place(nc, m, "h2F_", [P, 4, CH], F32, W + 112 * KB)
    place(nc, m, "h2H_", [P, KF1, CH], F32R, W + 120 * KB)
    place(nc, m, "h2L_", [P, KF1, CH], F32R, W + 136 * KB)
    place(nc, m, "st_a", [P, KD, FF1], F32, W + 152 * KB)
    place(nc, m, "st_b", [P, KF1, D], F32, W + 160 * KB)
    w1, w2 = (m.f2w1H, m.f2w1L), (m.f2w2H, m.f2w2L)
    split_weights(nc, m, sem, ((m.st_a[:], d.f2_w1.rearrange("(k p) n -> p k n", p=P), *w1),
                               (m.st_b[:], d.f2_w2.rearrange("(k p) n -> p k n", p=P), *w2)),
                  sem.w2_loaded, sem.w2_high, sem.w2_low)

    with nc.psum_tensor("l2_tok", [P, CH], F32) as ps_tok, nc.psum_tensor("l2_turn", [P, CH], F32) as ps_turn, \
            nc.psum_tensor("l2_h", [P, 4, CH], F32) as ps_h, nc.psum_tensor("l2_o", [P, KD, CH], F32) as ps_o, \
            nc.Block() as block:

        @block.sync
        def _(sp):
            def body(c, rep):
                for b in range(BPC):
                    i = sp.value_load(m.ids2[0:1, ds(c * BPC + b, 1)], min_val=0, max_val=31)
                    if rep >= 1:
                        sp.wait_ge(sem.tok2_mm, (c - 1) * PAIRS + b // 2 + 1)
                    i = apart(sp, i)
                    sp.dma_start(m.cw2[:, b], d.c2_w[ds(i, 1)].rearrange("e (k p) o -> p (e k) o", p=P))\
                      .then_inc(sem.cw2_loaded[b], 16)
            segments(sp, [0, 1, NC], body)

        @block.tensor
        def _(pe):
            def cond(c, rep):
                pe.wait_ge(sem.xs_copied, c + 1)
                for q in range(PAIRS):
                    if rep >= 1 or q >= 1:
                        pe.wait_ge(sem.tok2_act, c * PAIRS + q)
                    for b in (2 * q, 2 * q + 1):
                        pe.wait_ge(sem.cw2_loaded[b], 16 * (c + 1))
                        for k in range(KD):
                            last = nc.tensor.matmul(ps_tok[ts(b % 2, SEQ), 0:D], m.xs[:, k, ts(b, SEQ)], m.cw2[:, b, k],
                                                    start=k == 0, stop=k == KD - 1)
                    last.then_inc(sem.tok2_mm, 1)
                pe.wait_ge(sem.tok2_act, (c + 1) * PAIRS)
                for h in range(KD):
                    if rep >= 1 or h >= 1:
                        pe.wait_ge(sem.y2_added, 2 * c + h)
                    for q in range(PAIRS):
                        last = nc.tensor.transpose(ps_turn[:, ts(q, P)], m.y2t[:, q, ts(h, P)], m.ident[:])
                    last.then_inc(sem.turn2_mm, 1)

            def body(c, rep):
                pe.wait_ge(sem.y2_low, 2 * c + 2)
                for j in range(KF1):
                    if rep >= 1 or j >= 4:
                        pe.wait_ge(sem.h2a_act, c * KF1 + j - 3)
                    for k in range(KD):
                        last = products(nc, ps_h[:, j % 4], [w[:, k, ts(j, P)] for w in w1],
                                        [y[:, c % 2, k] for y in (m.y2H, m.y2L)], k == 0, k == KD - 1)
                    last.then_inc(sem.h2a_mm, 1)
                if rep + 1 < NC:
                    cond(c + 1, rep + 1)
                if rep >= 1:
                    pe.wait_ge(sem.x3_sum, 2 * c)
                for k in range(KF1):
                    pe.wait_ge(sem.h2a_low, c * KF1 + k + 1)
                    for h in range(KD):
                        last = products(nc, ps_o[:, h], [w[:, k, ts(h, P)] for w in w2],
                                        (m.h2H_[:, k], m.h2L_[:, k]), k == 0, k == KF1 - 1)
                    last.then_inc(sem.o2_mm, 1)
            cond(0, 0)
            segments(pe, [0, 1, NC - 1, NC], body)

        @block.scalar
        def _(act):
            def cond(c, rep):
                for q in range(PAIRS):
                    act.wait_ge(sem.tok2_mm, c * PAIRS + q + 1)
                    if rep >= 1:
                        act.wait_ge(sem.turn2_mm, 2 * c)
                    nc.scalar.copy(m.y2t[:, q], ps_tok[:, 0:D]).then_inc(sem.tok2_act, 1)

            def body(c, rep):
                for j in range(KF1):
                    act.wait_ge(sem.h2a_mm, c * KF1 + j + 1)
                    if rep >= 1:
                        act.wait_ge(sem.o2_mm, (c - 1) * KF1 + j + 1)
                    if rep >= 1 or j >= 4:
                        act.wait_ge(sem.h2a_low, c * KF1 + j - 3)
                    nc.scalar.activation(m.h2H_[:, j], ps_h[:, j % 4], ACT.Relu, bias=bias(m, "f2_b1", j))
                    nc.scalar.activation(m.h2F_[:, j % 4], ps_h[:, j % 4], ACT.Relu, bias=bias(m, "f2_b1", j))\
                      .then_inc(sem.h2a_act, 1)
                if rep + 1 < NC:
                    cond(c + 1, rep + 1)
            cond(0, 0)
            segments(act, [0, 1, NC - 1, NC], body)

        @block.vector
        def _(dve):
            def copy_x(c, rep):
                if rep >= 1:
                    dve.wait_ge(sem.tok2_mm, c * PAIRS)
                c = apart(dve, c)
                nc.vector.tensor_copy(m.xs[:], m.X[:, :, ds(c * CH, CH)]).then_inc(sem.xs_copied, 1)

            def cond(c, rep):
                for h in range(KD):
                    i = 2 * c + h
                    dve.wait_ge(sem.turn2_mm, i + 1)
                    if rep >= 1:
                        dve.wait_ge(sem.y2_low, i - 1)
                    if rep >= 2:
                        dve.wait_ge(sem.h2a_mm, (c - 1) * KF1)
                    nc.vector.tensor_tensor(by_batch(m.y2F[:, h]), by_batch(ps_turn[:]),
                                            per_batch(m.cond2[:, ds(h * BATCH + c * BPC, BPC)]), ALU.add)\
                      .then_inc(sem.y2_added, 1)
                for h in range(KD):
                    dve.wait_ge(sem.y2_added, 2 * c + h + 1)
                    nc.vector.tensor_copy(m.y2H[:, c % 2, h], m.y2F[:, h]).then_inc(sem.y2_high, 1)
                for h in range(KD):
                    dve.wait_ge(sem.y2_high, 2 * c + h + 1)
                    nc.vector.tensor_tensor(m.y2L[:, c % 2, h], m.y2F[:, h], m.y2H[:, c % 2, h].bitcast(F32), ALU.subtract)\
                      .then_inc(sem.y2_low, 1)

            def result(c, rep):
                dve.wait_ge(sem.o2_mm, KF1 * (c + 1))
                for h in range(KD):
                    x = m.X[:, h, ds(c * CH, CH)]
                    nc.vector.scalar_tensor_tensor(x, ps_o[:, h], bias(m, "f2_b2", h), x, ALU.add, ALU.add)\
                      .then_inc(sem.x3_sum, 1)

            def body(c, rep):
                if rep + 1 < NC:
                    copy_x(c + 1, rep + 1)
                if rep >= 1:
                    result(c - 1, rep - 1)
                for j in range(KF1):
                    dve.wait_ge(sem.h2a_act, c * KF1 + j + 1)
                    nc.vector.tensor_tensor(m.h2L_[:, j], m.h2F_[:, j % 4], m.h2H_[:, j].bitcast(F32), ALU.subtract)\
                      .then_inc(sem.h2a_low, 1)
                if rep + 1 < NC:
                    cond(c + 1, rep + 1)
            copy_x(0, 0)
            cond(0, 0)
            segments(dve, [0, 1, NC - 1, NC], body)
            result(NC - 1, NC - 1)
            dve.wait_ge(sem.x3_sum, 2 * NC)


HS = 512
KS = HS // P
NE = 8
PART = 64
TT_ = T // P


REGION = T + P
NSLOT = T * 2 // P + NE
SPARE = NE * REGION


def layer3_shared(nc, m, d, sem, z_rows):
    W = m.work
    for name, shape, at in (("c3w1H", [KD, FF1], 0), ("c3w1L", [KD, FF1], 8), ("w2H", [2, KF1, D], 16),
                            ("w2L", [2, KF1, D], 32),
                            ("x3H", [2, KD, CH], 52), ("x3L", [2, KD, CH], 60), ("h3aH", [KF1, CH], 76),
                            ("h3aL", [KF1, CH], 92), ("sw1H", [KD, HS], 112), ("sw1L", [KD, HS], 116),
                            ("sw2H", [KS, D], 120), ("sw2L", [KS, D], 124), ("zH", [KD, CH], 132), ("zL", [KD, CH], 136),
                            ("shH", [KS, CH], 140), ("shL", [KS, CH], 148)):
        place(nc, m, name, [P] + shape, F32R, W + at * KB)
    place(nc, m, "we", [P, 2, KF1, PART], F32, W + 48 * KB)
    place(nc, m, "h3aF", [P, 4, CH], F32, W + 68 * KB)
    place(nc, m, "ye", [SEQ, 2, 2, D], F32, W + 108 * KB)
    place(nc, m, "zF", [P, KD, CH], F32, W + 128 * KB)
    place(nc, m, "logits", [P, TT_, NE], F32, W + 160 * KB)
    place(nc, m, "rw", [P, KD, NE], F32, W + 161 * KB)
    place(nc, m, "rb", [P, NE], F32, W + 161 * KB + 512)
    place(nc, m, "hot_a", [P, TT_, NE], F32, W + 162 * KB)
    place(nc, m, "hot_b", [P, TT_, NE], F32, W + 163 * KB)
    place(nc, m, "zt", [P, PAIRS, D], F32, W + 164 * KB)
    place(nc, m, "before", [P, P], F32, W + 168 * KB)
    place(nc, m, "pos", [P, TT_, 2], I32, W + 168 * KB + 512)
    at = W + 168 * KB + 768
    for name, shape, dt in (("free_row", [NE], F32), ("rank8", [NE], F32), ("rank8i", [NE], I32), ("posc", [PAIRS, 2], I32),
                            ("posf", [PAIRS, 2], F32), ("lgc", [PAIRS, NE], F32), ("hac", [PAIRS, NE], F32),
                            ("hbc", [PAIRS, NE], F32), ("hsum", [PAIRS, NE], F32), ("rowc", [PAIRS, NE], F32),
                            ("rtmp", [PAIRS, NE], F32), ("rmax", [PAIRS, 1], F32), ("base_i", [NE], I32)):
        place(nc, m, name, [P] + shape, dt, at)
        at += max(32, 4 * shape[0] * (shape[1] if len(shape) > 1 else 1))
    place(nc, m, "pw", [P, TT_, 2], F32, at)
    at += 256
    assert at <= 207 * KB + 768
    place(nc, m, "st3a", [P, KD, FF1], F32, W + 76 * KB)
    place(nc, m, "st3b", [P, KF1, 192], F32, W + 84 * KB)
    place(nc, m, "st3c", [P, KD, HS], F32, W + 92 * KB)
    place(nc, m, "st3d", [P, KS, D], F32, W + 96 * KB)
    w1, w2, sw1, sw2 = (m.c3w1H, m.c3w1L), (m.w2H, m.w2L), (m.sw1H, m.sw1L), (m.sw2H, m.sw2L)
    SHARED = D - PART
    split_weights(nc, m, sem, ((m.st3a[:], d.c3_w1.rearrange("(k p) n -> p k n", p=P), *w1),
                               (m.st3b[:], d.c3_w2.rearrange("(k p) n -> p k n", p=P), *[w[:, 0, :, 0:SHARED] for w in w2]),
                               (m.st3b[:], None, *[w[:, 1, :, 0:SHARED] for w in w2]),
                               (m.st3c[:], d.sw1.rearrange("(k p) n -> p k n", p=P), *sw1),
                               (m.st3d[:], d.sw2.rearrange("(k p) n -> p k n", p=P), *sw2)),
                  sem.w3_loaded, sem.w3_high, sem.w3_low)

    CUTS = [0, 1, 2, NC - 1, NC, NC + 1]
    STEPS, RANKS_READ = 25, 20
    with nc.psum_tensor("l3_h", [P, 4, CH], F32) as ps_h, nc.psum_tensor("l3_o", [P, KD, CH], F32) as ps_o, \
            nc.psum_tensor("l3_e", [P, 2, CH], F32) as ps_e, \
            nc.Block() as block:

        @block.sync
        def _(sp):
            sp.dma_start(m.rw[:], d.rw.rearrange("(k p) n -> p k n", p=P)).then_inc(sem.r_loaded, 16)
            sp.dma_start(m.rb[:], d.rb.partition_broadcast(P)).then_inc(sem.r_loaded, 16)

            def body(c, rep):
                for b in range(BPC):
                    i = sp.value_load(m.ids0[0:1, ds(c * BPC + b, 1)], min_val=0, max_val=7)
                    if rep >= 1 or b >= 2:
                        sp.wait_ge(sem.we_low, c * BPC + b - 1)
                    i = apart(sp, i)
                    sp.dma_start(m.we[:, b % 2], d.we[ds(i, 1)].rearrange("e (k p) o -> p (e k) o", p=P))\
                      .then_inc(sem.we_loaded[b % 2], 16)
            segments(sp, [0, 1, NC], body)

        @block.tensor
        def _(pe):
            def body(c, rep):
                main, shared = rep < NC, rep >= 1
                if main:
                    pe.wait_ge(sem.x3_low, 2 * c + 2)
                    for j in range(KF1):
                        if j < 4:
                            if rep == 1:
                                pe.wait_ge(sem.h3a_act, KF1)
                            elif rep >= 2 and j < 2:
                                pe.wait_ge(sem.x4_sum, 2 * (c - 1))
                            elif rep >= 2:
                                pe.wait_ge(sem.sh_act, KS * (c - 1))
                        else:
                            pe.wait_ge(sem.h3a_act, c * KF1 + j - 3)
                        for k in range(KD):
                            last = products(nc, ps_h[:, j % 4], [w[:, k, ts(j, P)] for w in w1],
                                            [x[:, c % 2, k] for x in (m.x3H, m.x3L)], k == 0, k == KD - 1)
                        last.then_inc(sem.h3a_mm, 1)
                if shared:
                    pe.wait_ge(sem.z_low, 2 * c)
                    if not main:
                        pe.wait_ge(sem.x4_sum, 2 * (NC - 1))
                        pe.wait_ge(sem.sh_act, KS * (NC - 1))
                    for j in range(KS):
                        if main:
                            pe.wait_ge(sem.h3a_act, c * KF1 + j + 5)
                        for k in range(KD):
                            last = products(nc, ps_h[:, j], [w[:, k, ts(j, P)] for w in sw1],
                                            (m.zH[:, k], m.zL[:, k]), k == 0, k == KD - 1)
                        last.then_inc(sem.sh_mm, 1)
                    if rep == 1:
                        pe.wait_ge(sem.r_loaded, 32)
                        pe.wait_ge(sem.before_done, 2)
                    pe.wait_ge(sem.ye_act, PAIRS * c)
                    for q in range(PAIRS):
                        for k in range(KD):
                            last = nc.tensor.matmul(ps_e[:, 0, ts(q, NE)], m.zF[:, k, ts(q, P)], m.rw[:, k],
                                                    start=k == 0, stop=k == KD - 1)
                    last.then_inc(sem.r_mm, 1)
                    for g in range(2):
                        for q in range(2):
                            for h in range(KD):
                                last = nc.tensor.transpose(ps_o[:, g, ts(q * KD + h, P)], m.zF[:, h, ts(2 * g + q, P)], m.ident[:])
                        last.then_inc(sem.zt_mm, 1)
                if main:
                    if rep >= 1:
                        pe.wait_ge(sem.rt_step, (c - 1) * STEPS + 1)
                    batches(c, rep, 0)
                if shared:
                    pe.wait_ge(sem.hot_done, c)
                    nc.tensor.matmul(ps_e[:, 1, 0:32], m.before[:], m.hsum[:].rearrange("p q e -> p (q e)"), start=True, stop=True)
                    nc.tensor.matmul(ps_e[:, 1, 32:64], m.ones1[:], m.hsum[:].rearrange("p q e -> p (q e)"), start=True, stop=True)\
                      .then_inc(sem.rank_mm, 1)
                    second(c, main, 0)
                if main:
                    if not shared:
                        pe.wait_ge(sem.ye_act, 1)
                    turn(c, 0)
                    if shared:
                        pe.wait_ge(sem.rt_step, (c - 1) * STEPS + RANKS_READ)
                    batches(c, rep, 1)
                    batches(c, rep, 2)
                    turn(c, 1)
                    batches(c, rep, 3)
                    turn(c, 2)
                if shared:
                    second(c, main, 1)
                if main:
                    if not shared:
                        pe.wait_ge(sem.ye_act, PAIRS)
                    turn(c, 3)

            def batches(c, rep, q):
                if q >= 2:
                    pe.wait_ge(sem.ye_act, c * PAIRS + q - 1)
                for b in (2 * q, 2 * q + 1):
                    if b % 2 == 1 and q >= 2:
                        pe.wait_ge(sem.ye_act, c * PAIRS + q)
                    pe.wait_ge(sem.we_low, c * BPC + b + 1)
                    for k in range(KF1):
                        if b == 0:
                            pe.wait_ge(sem.h3a_low, c * KF1 + k + 1)
                        last = products(nc, ps_e[0:SEQ, q % 2, ts(b % 2, D)], [h[:, k, ts(b, SEQ)] for h in (m.h3aH, m.h3aL)],
                                        [w[:, b % 2, k] for w in w2], k == 0, k == KF1 - 1)
                    last.then_inc(sem.e_mm, 1)

            def second(c, main, h):
                for k in range(KS):
                    pe.wait_ge(sem.sh_low, KS * (c - 1) + k + 1)
                    if main and k == KS - 1:
                        if h == 0:
                            pe.wait_ge(sem.zt_act, 2 * c)
                        pe.wait_ge(sem.ye_act, c * PAIRS + 3 * h + 1)
                    last = products(nc, ps_h[:, h], [w[:, k, ts(h, P)] for w in sw2],
                                    (m.shH[:, k], m.shL[:, k]), k == 0, k == KS - 1)
                last.then_inc(sem.s2_mm, 1)

            def turn(c, q):
                for h in range(KD):
                    for b in range(2):
                        last = nc.tensor.transpose(ps_o[:, h, ts(2 * q + b, SEQ)], m.ye[:, q % 2, b, ts(h, P)], m.ident[0:SEQ, 0:SEQ])
                last.then_inc(sem.t3_mm, 1)
            segments(pe, CUTS, body)

        @block.scalar
        def _(act):
            def body(c, rep):
                main, shared = rep < NC, rep >= 1
                if main:
                    for j in range(KF1):
                        act.wait_ge(sem.h3a_mm, c * KF1 + j + 1)
                        if rep >= 1:
                            act.wait_ge(sem.e_mm, c * BPC)
                        if j >= 4:
                            act.wait_ge(sem.h3a_low, c * KF1 + j - 3)
                        elif rep >= 2:
                            act.wait_ge(sem.sh_low, KS * (c - 1))
                        elif rep == 1:
                            act.wait_ge(sem.h3a_low, KF1)
                        nc.scalar.activation(m.h3aH[:, j], ps_h[:, j % 4], ACT.Gelu, bias=bias(m, "c3_b1", j))
                        nc.scalar.activation(m.h3aF[:, j % 4], ps_h[:, j % 4], ACT.Gelu, bias=bias(m, "c3_b1", j))\
                          .then_inc(sem.h3a_act, 1)
                if shared:
                    for j in range(KS):
                        act.wait_ge(sem.sh_mm, KS * (c - 1) + j + 1)
                        if rep >= 2:
                            act.wait_ge(sem.s2_mm, 2 * (c - 1))
                        if main:
                            act.wait_ge(sem.h3a_low, c * KF1 + j + 5)
                        else:
                            act.wait_ge(sem.sh_low, KS * (NC - 1))
                        nc.scalar.activation(m.shH[:, j], ps_h[:, j], ACT.Gelu, bias=bias(m, "sb1", j))
                        nc.scalar.activation(m.h3aF[:, j], ps_h[:, j], ACT.Gelu, bias=bias(m, "sb1", j))\
                          .then_inc(sem.sh_act, 1)
                    for g in range(2):
                        act.wait_ge(sem.zt_mm, 2 * (c - 1) + g + 1)
                        if rep >= 2:
                            act.wait_ge(sem.scattered, 128 * (c - 1))
                        nc.scalar.copy(m.zt[:, 2 * g:2 * g + 2].rearrange("p q n -> p (q n)"), ps_o[:, g]).then_inc(sem.zt_act, 1)
                if main:
                    for q in range(PAIRS):
                        act.wait_ge(sem.e_mm, c * BPC + 2 * q + 2)
                        if rep >= 1 or q >= 2:
                            act.wait_ge(sem.t3_mm, c * PAIRS + q - 1)
                        nc.scalar.copy(m.ye[:, q % 2].rearrange("p b n -> p (b n)"), ps_e[0:SEQ, q % 2]).then_inc(sem.ye_act, 1)
            segments(act, CUTS, body)

        @block.vector
        def _(dve):
            def split_x(c, rep):
                if rep >= 2:
                    dve.wait_ge(sem.h3a_mm, (c - 1) * KF1)
                for h in range(KD):
                    nc.vector.tensor_copy(m.x3H[:, c % 2, h], m.X[:, h, ds(c * CH, CH)]).then_inc(sem.x3_high, 1)
                for h in range(KD):
                    dve.wait_ge(sem.x3_high, 2 * c + h + 1)
                    nc.vector.tensor_tensor(m.x3L[:, c % 2, h], m.X[:, h, ds(c * CH, CH)],
                                            m.x3H[:, c % 2, h].bitcast(F32), ALU.subtract).then_inc(sem.x3_low, 1)

            def split_we(c, rep, b):
                dve.wait_ge(sem.we_loaded[b % 2], 16 * (4 * c + b // 2 + 1))
                if rep >= 1 or b >= 2:
                    dve.wait_ge(sem.e_mm, c * BPC + b - 1)
                nc.vector.tensor_copy(m.w2H[:, b % 2, :, SHARED:D], m.we[:, b % 2]).then_inc(sem.we_high, 1)
                dve.wait_ge(sem.we_high, c * BPC + b + 1)
                nc.vector.tensor_tensor(m.w2L[:, b % 2, :, SHARED:D], m.we[:, b % 2], m.w2H[:, b % 2, :, SHARED:D].bitcast(F32),
                                        ALU.subtract).then_inc(sem.we_low, 1)

            def body(c, rep):
                main, shared = rep < NC, rep >= 1
                if main:
                    if rep + 1 < NC:
                        split_x(c + 1, rep + 1)
                    for j in range(KF1):
                        dve.wait_ge(sem.h3a_act, c * KF1 + j + 1)
                        nc.vector.tensor_tensor(m.h3aL[:, j], m.h3aF[:, j % 4], m.h3aH[:, j].bitcast(F32), ALU.subtract)\
                          .then_inc(sem.h3a_low, 1)
                        if j < 2:
                            split_we(c, rep, j)
                if shared:
                    for j in range(KS):
                        dve.wait_ge(sem.sh_act, KS * (c - 1) + j + 1)
                        nc.vector.tensor_tensor(m.shL[:, j], m.h3aF[:, j], m.shH[:, j].bitcast(F32), ALU.subtract)\
                          .then_inc(sem.sh_low, 1)
                    route_a(c - 1, rep - 1)
                if main:
                    split_we(c, rep, 2)
                    split_we(c, rep, 3)
                if shared:
                    route_b(c - 1, rep - 1)
                    result(c - 1, 0)
                if main:
                    for b in range(4, BPC):
                        split_we(c, rep, b)
                if shared:
                    result(c - 1, 1)
                if main:
                    dve.wait_ge(sem.t3_mm, PAIRS * (c + 1))
                    nc.vector.tensor_scalar(m.zF[:, 0], ps_o[:, 0], bias(m, "c3_b2"), None, ALU.add).then_inc(sem.z_done, 1)
                    nc.vector.tensor_tensor(by_batch(m.zF[:, 1]), by_batch(ps_o[:, 1]), per_batch(m.cond3[:, ds(c * BPC, BPC)]),
                                            ALU.add).then_inc(sem.z_done, 1)
                    for h in range(KD):
                        dve.wait_ge(sem.z_done, 2 * c + h + 1)
                        nc.vector.tensor_copy(m.zH[:, h], m.zF[:, h]).then_inc(sem.z_high, 1)
                    for h in range(KD):
                        dve.wait_ge(sem.z_high, 2 * c + h + 1)
                        nc.vector.tensor_tensor(m.zL[:, h], m.zF[:, h], m.zH[:, h].bitcast(F32), ALU.subtract)\
                          .then_inc(sem.z_low, 1)

            n = [0]

            def step(c, i):
                i.then_inc(sem.rt_step, 1)
                n[0] += 1
                dve.wait_ge(sem.rt_step, c * STEPS + n[0])

            def route_a(c, rep):
                n[0] = 0
                rank = m.rank8[:].unsqueeze(1).broadcast_to([P, PAIRS, NE])
                biggest = m.rmax[:].broadcast_to([P, PAIRS, NE])

                def first_of_max(hot, x):
                    step(c, nc.vector.tensor_reduce(m.rmax[:], x[:], AX.X, ALU.max))
                    step(c, nc.vector.tensor_tensor(m.rtmp[:], x[:], biggest, ALU.is_equal))
                    step(c, nc.vector.tensor_tensor(m.rtmp[:], m.rtmp[:], rank, ALU.mult))
                    step(c, nc.vector.tensor_reduce(m.rmax[:], m.rtmp[:], AX.X, ALU.max))
                    step(c, nc.vector.tensor_tensor(hot[:], rank, biggest, ALU.is_equal))
                dve.wait_ge(sem.r_mm, c + 1)
                step(c, nc.vector.tensor_tensor(m.lgc[:], ps_e[:, 0, 0:PAIRS * NE].rearrange("p (q e) -> p q e", e=NE),
                                             m.rb[:].unsqueeze(1).broadcast_to([P, PAIRS, NE]), ALU.add))
                first_of_max(m.hac, m.lgc)
                step(c, nc.vector.scalar_tensor_tensor(m.rowc[:], m.hac[:], -3e38, m.lgc[:], ALU.mult, ALU.add))
                first_of_max(m.hbc, m.rowc)
                nc.vector.tensor_tensor(m.hsum[:], m.hac[:], m.hbc[:], ALU.add).then_inc(sem.hot_done, 1)
                at = c * PAIRS
                nc.vector.tensor_copy(m.logits[:, ds(at, PAIRS)], m.lgc[:])
                nc.vector.tensor_copy(m.hot_a[:, ds(at, PAIRS)], m.hac[:])
                nc.vector.tensor_copy(m.hot_b[:, ds(at, PAIRS)], m.hbc[:])

            def route_b(c, rep):
                at = c * PAIRS
                dve.wait_ge(sem.rank_mm, c + 1)
                for q in range(PAIRS):
                    step(c, nc.vector.tensor_tensor(m.rowc[:, q], ps_e[:, 1, ds(q * NE, NE)], m.free_row[:], ALU.add))
                    step(c, nc.vector.tensor_tensor(m.free_row[:], ps_e[:, 1, ds(32 + q * NE, NE)], m.free_row[:], ALU.add))
                step(c, nc.vector.tensor_tensor(m.rtmp[:], m.rowc[:], m.hac[:], ALU.mult))
                step(c, nc.vector.tensor_reduce(m.posf[:, :, 0:1], m.rtmp[:], AX.X, ALU.add))
                step(c, nc.vector.tensor_tensor(m.rtmp[:], m.rowc[:], m.hbc[:], ALU.mult))
                step(c, nc.vector.tensor_reduce(m.posf[:, :, 1:2], m.rtmp[:], AX.X, ALU.add))
                if rep >= 1:
                    dve.wait_ge(sem.scattered, 128 * c)
                step(c, nc.vector.tensor_copy(m.posc[:], m.posf[:]))
                nc.vector.tensor_copy(m.pos[:, ds(at, PAIRS)], m.posc[:]).then_inc(sem.pos_done, 1)
                assert n[0] == STEPS, n[0]

            def result(c, h):
                dve.wait_ge(sem.s2_mm, 2 * c + h + 1)
                x = m.X[:, h, ds(c * CH, CH)]
                nc.vector.scalar_tensor_tensor(x, ps_h[:, h], bias(m, "sb2", h), x, ALU.add, ALU.add).then_inc(sem.x4_sum, 1)
            dve.wait_ge(sem.iota_done, 2)
            nc.vector.tensor_copy(m.rank8[:], m.rank8i[:]).then_inc(sem.rank_const, 1)
            nc.vector.tensor_copy(m.free_row[:], m.base_i[:]).then_inc(sem.rank_const, 1)
            dve.wait_ge(sem.r_loaded, 32)
            split_x(0, 0)
            dve.wait_ge(sem.rank_const, 2)
            segments(dve, CUTS, body)
            dve.wait_ge(sem.x4_sum, 2 * NC)

        @block.gpsimd
        def _(pool):
            pool.iota(m.rank8i[:], pattern=[[-1, NE]], base=NE, channel_multiplier=0).then_inc(sem.iota_done, 1)
            pool.iota(m.base_i[:], pattern=[[REGION, NE]], base=0, channel_multiplier=0).then_inc(sem.iota_done, 1)
            pool.memset(m.before[:], 1.0).then_inc(sem.before_done, 1)
            pool.wait_ge(sem.before_done, 1)
            pool.affine_select(out=m.before[:], in_=m.before[:], compare_op=ALU.is_gt, fill=0.0, base=0,
                               pattern=[[1, P]], channel_multiplier=-1).then_inc(sem.before_done, 1)

            def scatter(c):
                pool.wait_ge(sem.pos_done, c + 1)
                pool.wait_ge(sem.zt_act, 2 * (c + 1))
                for q in range(PAIRS):
                    for k in range(2):
                        pool.indirect_dma_start(z_rows, bass.IndirectOffsetOnAxis(ap=m.posc[:, q, k:k + 1], axis=0),
                                                m.zt[:, q], None).then_inc(sem.scattered, 16)

            for c in range(NC):
                scatter(c)
            pool.wait_ge(sem.scattered, 128 * NC)


N1, NW = KD * HS, KD * HS + KS * D


def expert_weights(nc, pool, m, d, sem, e):
    for half, src, k in ((0, d.ew1, KD), (1, d.ew2, KS)):
        i = 2 * e + half
        if i >= 1:
            pool.wait_ge(sem.ew_low, i)
        pool.dma_start(m.ew[:].rearrange("p (k n) -> p k n", k=k), src[e].rearrange("(k p) n -> p k n", p=P))\
            .then_inc(sem.ew_loaded, 16)
        hi, lo = (t[:, e, ts(half, N1)] for t in (m.ewH, m.ewL))
        pool.wait_ge(sem.ew_loaded, 16 * (i + 1))
        pool.tensor_copy(hi, m.ew[:]).then_inc(sem.ew_high, 1)
        pool.wait_ge(sem.ew_high, i + 1)
        pool.tensor_tensor(lo, m.ew[:], hi.bitcast(F32), ALU.subtract).then_inc(sem.ew_low, 1)


def layer3_tables(nc, m, d, sem, z_rows):
    W = m.work
    at = W + 136 * KB
    for name, shape, dt in (("prob", [TT_, NE], F32), ("rt2", [TT_, NE], F32), ("rt", [TT_, 1], F32), ("lanef", [1], F32),
                            ("lanei", [1], I32), ("tiles", [NE], F32), ("upto", [NE], F32), ("gap", [NE], F32), ("base_f", [NE], F32),
                            ("past", [NE], F32), ("sum1", [1], F32), ("shift", [NE], F32), ("posw", [TT_, 2], F32), ("tab", [2], F32), ("lane32", [1], F32), ("tabf", [2 * P], F32),
                            ("b1raw", [HS], F32), ("b2raw", [D], F32), ("b1all", [HS], F32R), ("b2all", [D], F32R)):
        place(nc, m, name, [P] + shape, dt, at)
        at += max(32, 4 * shape[0] * (shape[1] if len(shape) > 1 else 1))
    assert at <= W + 150 * KB
    place(nc, m, "zeros", [P, D], F32, W + 150 * KB)
    place(nc, m, "b1t", [40, HS], F32R, W + 155 * KB)
    place(nc, m, "sel", [40, 4, P], F32R, W + 157 * KB)
    place(nc, m, "b2t", [40, D], F32R, W + 159 * KB)
    place(nc, m, "hot_t", [40, P], F32, W + 160 * KB)
    place(nc, m, "pad_i", [1, NE], I32, W + 160 * KB + 512)
    place(nc, m, "tabi", [1, 2 * P], I32, W + 161 * KB)
    place(nc, m, "ewH", [P, NE, NW], F32R, W)
    place(nc, m, "ewL", [P, NE, NW], F32R, W + 64 * KB)
    place(nc, m, "ew", [P, 1024], F32, W + 151 * KB)

    def wide(t):
        return t[:].broadcast_to([P, TT_, NE])
    with nc.psum_tensor("l3_tab", [P, CH], F32) as ps, nc.Block() as block:
        @block.gpsimd
        def _(pool):
            pool.memset(m.zeros[:], 0.0).then_inc(sem.zeros_done, 1)
            pool.iota(m.lanei[:], pattern=[[0, 1]], base=0, channel_multiplier=1).then_inc(sem.tab_pool, 1)
            pool.memset(m.b1raw[0:40, :], 0.0).then_inc(sem.tab_pool, 1)
            pool.memset(m.b2raw[0:40, :], 0.0).then_inc(sem.tab_pool, 1)
            expert_weights(nc, pool, m, d, sem, 0)

        @block.scalar
        def _(act):
            act.wait_ge(sem.rt_dve, 2)
            nc.scalar.activation(m.prob[:], m.prob[:], ACT.Exp).then_inc(sem.rt_exp, 1)

        @block.tensor
        def _(pe):
            pe.wait_ge(sem.tab_done, 1)
            for i in range(2):
                last = nc.tensor.transpose(ps[0:1, ts(i, P)], m.tab[:, i:i + 1], m.ident[:])
            last.then_inc(sem.tab_mm, 1)
            pe.wait_ge(sem.tab_done, 2)
            nc.tensor.matmul(ps[0:40, 256:384], m.ones1[0:1, 0:40], m.tabf[0:1, 0:P], start=True, stop=True).then_inc(sem.tab_mm, 1)

        @block.vector
        def _(dve):
            n = [0]

            def step(i):
                i.then_inc(sem.rt_dve, 1)
                n[0] += 1
                dve.wait_ge(sem.rt_dve, n[0])
            step(nc.vector.tensor_reduce(m.rt[:], m.logits[:], AX.X, ALU.max))
            step(nc.vector.tensor_tensor(m.prob[:], m.logits[:], wide(m.rt), ALU.subtract))
            step(nc.vector.tensor_copy(m.base_f[:], m.base_i[:]))
            step(nc.vector.tensor_tensor(m.tiles[:], m.free_row[:], m.base_f[:], ALU.subtract))
            step(nc.vector.tensor_scalar(m.tiles[:], m.tiles[:], 1.0 / P, 0.5 - 0.5 / P, ALU.mult, ALU.add))
            step(nc.vector.tensor_scalar(m.tiles[:], m.tiles[:], MAGIC, None, ALU.add))
            step(nc.vector.tensor_scalar(m.tiles[:], m.tiles[:], MAGIC, None, ALU.subtract))
            step(nc.vector.tensor_copy(m.pad_i[:], m.free_row[0:1, :]))
            step(nc.vector.tensor_copy(m.upto[:], m.tiles[:]))
            for e in range(1, NE):
                step(nc.vector.tensor_tensor(m.upto[:, e:e + 1], m.upto[:, e:e + 1], m.upto[:, e - 1:e], ALU.add))
            step(nc.vector.tensor_scalar(m.gap[:], m.tiles[:], -float(P), float(REGION), ALU.mult, ALU.add))
            dve.wait_ge(sem.tab_pool, 3)
            step(nc.vector.tensor_copy(m.lanef[:], m.lanei[:]))
            step(nc.vector.tensor_scalar(m.past[:], m.upto[:], m.lanef[:], None, ALU.is_le))
            step(nc.vector.tensor_reduce(m.sum1[:], m.past[:], AX.X, ALU.add))
            step(nc.vector.tensor_scalar(m.tab[:, 0:1], m.sum1[:], float(NE - 1), None, ALU.min))
            step(nc.vector.tensor_tensor(m.past[:], m.past[:], m.gap[:], ALU.mult))
            step(nc.vector.tensor_reduce(m.sum1[:], m.past[:], AX.X, ALU.add))
            nc.vector.scalar_tensor_tensor(m.tab[:, 1:2], m.lanef[:], float(P), m.sum1[:], ALU.mult, ALU.add)\
              .then_inc(sem.tab_done, 1)
            dve.wait_ge(sem.tab_mm, 1)
            nc.vector.tensor_copy(m.tabi[:], ps[0:1, 0:2 * P])
            nc.vector.tensor_copy(m.tabf[0:1, :], ps[0:1, 0:2 * P]).then_inc(sem.tab_done, 1)
            step(nc.vector.tensor_copy(m.lane32[:], m.lanef[:]))
            step(nc.vector.tensor_scalar(m.lane32[32:64, :], m.lanef[32:64, :], 32.0, None, ALU.subtract))
            dve.wait_ge(sem.tab_mm, 2)
            step(nc.vector.tensor_scalar(m.hot_t[:], ps[0:40, 256:384], m.lane32[0:40, :], None, ALU.is_equal))
            dve.wait_ge(sem.rt_exp, 1)
            step(nc.vector.tensor_reduce(m.rt[:], m.prob[:], AX.X, ALU.add))
            step(nc.vector.reciprocal(m.rt[:], m.rt[:]))
            step(nc.vector.tensor_tensor(m.prob[:], m.prob[:], wide(m.rt), ALU.mult))
            for i, hot in enumerate((m.hot_a, m.hot_b)):
                step(nc.vector.tensor_tensor(m.rt2[:], m.prob[:], hot[:], ALU.mult))
                step(nc.vector.tensor_reduce(m.pw[:, :, i:i + 1], m.rt2[:], AX.X, ALU.add))
            step(nc.vector.tensor_tensor(m.shift[:], m.upto[:], m.tiles[:], ALU.subtract))
            step(nc.vector.scalar_tensor_tensor(m.shift[:], m.shift[:], float(P), m.base_f[:], ALU.mult, ALU.subtract))
            step(nc.vector.tensor_copy(m.posw[:], m.pos[:]))
            for i, hot in enumerate((m.hot_a, m.hot_b)):
                step(nc.vector.tensor_tensor(m.rt2[:], m.shift[:].unsqueeze(1).broadcast_to([P, TT_, NE]), hot[:], ALU.mult))
                step(nc.vector.tensor_reduce(m.rt[:], m.rt2[:], AX.X, ALU.add))
                step(nc.vector.tensor_tensor(m.posw[:, :, i:i + 1], m.posw[:, :, i:i + 1], m.rt[:], ALU.add))
            step(nc.vector.tensor_copy(m.pos[:], m.posw[:]))
            dve.wait_ge(sem.eb_loaded, 64)
            for raw, all_, t in ((m.b1raw, m.b1all, m.b1t), (m.b2raw, m.b2all, m.b2t)):
                step(nc.vector.tensor_copy(all_[0:40, :], raw[0:40, :]))
                step(nc.vector.tensor_copy(t[:], raw[0:40, :]))
                step(nc.vector.tensor_tensor(t[32:40, :], raw[32:40, :], all_[32:40, :].bitcast(F32), ALU.subtract))

        @block.sync
        def _(sp):
            sp.wait_ge(sem.tab_pool, 3)
            for raw, src in ((m.b1raw, d.eb1), (m.b2raw, d.eb2)):
                for at in (0, 32):
                    sp.dma_start(raw[at:at + NE, :], src).then_inc(sem.eb_loaded, 16)
            sp.wait_ge(sem.zeros_done, 1)
            for e in range(NE):
                sp.dma_start(z_rows[SPARE + e * P:SPARE + (e + 1) * P, :], m.zeros[:]).then_inc(sem.padded, 16)
            sp.wait_ge(sem.tab_done, 2)
            for e in range(NE):
                row = sp.value_load(m.pad_i[0:1, e:e + 1], min_val=e * REGION, max_val=e * REGION + T)
                sp.dma_start(z_rows[ds(row, P), :], m.zeros[:]).then_inc(sem.padded, 16)
            sp.wait_ge(sem.padded, 32 * NE)


def layer3_experts(nc, m, d, sem, z_rows, e_rows):
    W = m.work
    place(nc, m, "zr", [P, 4, D], F32, W + 128 * KB)
    place(nc, m, "zxH", [P, 2, KD, P], F32R, W + 132 * KB)
    place(nc, m, "zxL", [P, 2, KD, P], F32R, W + 134 * KB)
    place(nc, m, "ehF", [P, 2, HS], F32, W + 136 * KB)
    place(nc, m, "exH", [P, 2, KS, P], F32R, W + 140 * KB)
    place(nc, m, "exL", [P, 2, KS, P], F32R, W + 144 * KB)
    place(nc, m, "eo", [P, 2, D], F32, W + 148 * KB)
    FOURS = [0, 1, NSLOT // 4 - 1, NSLOT // 4, NSLOT // 4 + 1]

    def steps(eng, body):
        segments(eng, FOURS, lambda s, rep: [body(4 * s + u, 4 * rep + u, s) for u in range(4)])

    with nc.psum_tensor("ex_z", [P, CH], F32) as ps_z, nc.psum_tensor("ex_h", [P, 2, CH], F32) as ps_h, \
            nc.psum_tensor("ex_x", [P, 2, CH], F32) as ps_x, nc.psum_tensor("ex_o", [P, 2, CH], F32) as ps_o, \
            nc.Block() as block:

        @block.sync
        def _(sp):
            def rows(t, rep):
                row = sp.value_load(m.tabi[0:1, ds(t + P, 1)], min_val=0, max_val=SPARE + (NE - 1) * P)
                if rep >= 4:
                    sp.wait_ge(sem.zx_mm, t - 3)
                row = apart(sp, row)
                sp.dma_start(m.zr[:, rep % 4], z_rows[ds(row, P), :]).then_inc(sem.zr_loaded[rep % 4], 16)
            segments(sp, [0, 1, NSLOT // 4], lambda s, rep: [rows(4 * s + u, 4 * rep + u) for u in range(4)])

        @block.gpsimd
        def _(pool):
            for e in range(1, NE):
                expert_weights(nc, pool, m, d, sem, e)

        @block.tensor
        def _(pe):
            def turn_in(t, rep, turn):
                pe.wait_ge(sem.zr_loaded[rep % 4], 16 * (turn + 1))
                if rep >= 1:
                    pe.wait_ge(sem.zx_low, t)
                for k in range(KD):
                    last = nc.tensor.transpose(ps_z[:, ts(k, P)], m.zr[:, rep % 4, ts(k, P)], m.ident[:])
                last.then_inc(sem.zx_mm, 1)

            def first(t, rep):
                e = pe.value_load(m.tabi[0:1, ds(t, 1)], min_val=0, max_val=NE - 1)
                pe.wait_ge(sem.ew_low, e * 2 + 2)
                pe.wait_ge(sem.zx_low, t + 1)
                if rep >= 2:
                    pe.wait_ge(sem.eh_act, t - 1)
                nc.tensor.matmul(ps_h[:, rep % 2], m.sel[:, rep % 4], m.b1t[:], start=True, stop=False)
                for k in range(KD):
                    w = [t_[:, ds(e, 1), ts(k, HS)].rearrange("p o n -> p (o n)") for t_ in (m.ewH, m.ewL)]
                    last = products(nc, ps_h[:, rep % 2], [x[:, rep % 2, k] for x in (m.zxH, m.zxL)], w, False, k == KD - 1)
                last.then_inc(sem.eh_mm, 1)

            def turn_hidden(t, rep):
                pe.wait_ge(sem.eh_act, t + 1)
                if rep >= 2:
                    pe.wait_ge(sem.ex_low, t - 1)
                for k in range(KS):
                    last = nc.tensor.transpose(ps_x[:, rep % 2, ts(k, P)], m.ehF[:, rep % 2, ts(k, P)], m.ident[:])
                last.then_inc(sem.ex_mm, 1)

            def second(t, rep):
                e = pe.value_load(m.tabi[0:1, ds(t, 1)], min_val=0, max_val=NE - 1)
                pe.wait_ge(sem.ex_low, t + 1)
                if rep >= 2:
                    pe.wait_ge(sem.eo_out, t - 1)
                nc.tensor.matmul(ps_o[:, rep % 2, 0:D], m.sel[:, rep % 4], m.b2t[:], start=True, stop=False)
                for k in range(KS):
                    w = [t_[:, ds(e, 1), N1 + k * D:N1 + (k + 1) * D].rearrange("p o n -> p (o n)") for t_ in (m.ewH, m.ewL)]
                    last = products(nc, ps_o[:, rep % 2, 0:D], [x[:, rep % 2, k] for x in (m.exH, m.exL)], w, False, k == KS - 1)
                last.then_inc(sem.eo_mm, 1)

            def body(t, rep, turn):
                if rep + 1 < NSLOT:
                    turn_in(t + 1, rep + 1, turn + (rep % 4 + 1) // 4)
                if rep < NSLOT:
                    first(t, rep)
                if within(rep - 1, 0, NSLOT):
                    turn_hidden(t - 1, rep - 1)
                if within(rep - 2, 0, NSLOT):
                    second(t - 2, rep - 2)
            turn_in(0, 0, 0)
            steps(pe, body)

        @block.scalar
        def _(act):
            def store(t, rep):
                act.wait_ge(sem.eo_out, t + 1)
                t = apart(act, t)
                act.dma_start(e_rows[ds(t * P, P), :], m.eo[:, rep % 2]).then_inc(sem.eo_stored[rep % 2], 16)

            def body(t, rep, turn):
                if rep < NSLOT:
                    act.wait_ge(sem.eh_mm, t + 1)
                    if rep >= 2:
                        act.wait_ge(sem.ex_mm, t - 1)
                    nc.scalar.activation(m.ehF[:, rep % 2], ps_h[:, rep % 2], ACT.Gelu).then_inc(sem.eh_act, 1)
                if within(rep - 1, 0, NSLOT):
                    i = t - 1
                    act.wait_ge(sem.ex_mm, i + 1)
                    if rep - 1 >= 2:
                        act.wait_ge(sem.eo_mm, i - 1)
                    nc.scalar.copy(m.exH[:, (rep - 1) % 2].rearrange("p k n -> p (k n)"), ps_x[:, (rep - 1) % 2]).then_inc(sem.ex_high, 1)
                if within(rep - 3, 0, NSLOT):
                    store(t - 3, rep - 3)
            steps(act, body)
            for u in range(2):
                act.wait_ge(sem.eo_stored[u], 16 * (NSLOT // 2))

        @block.vector
        def _(dve):
            def turned(t, rep):
                dve.wait_ge(sem.zx_mm, t + 1)
                if rep >= 2:
                    dve.wait_ge(sem.eh_mm, t - 1)
                nc.vector.tensor_copy(m.zxH[:, rep % 2].rearrange("p k n -> p (k n)"), ps_z[:, 0:D]).then_inc(sem.zx_high, 1)
                if rep >= 4:
                    dve.wait_ge(sem.eo_mm, t - 3)
                c = apart(dve, t)
                nc.vector.tensor_copy(m.sel[:, rep % 4], m.hot_t[:, ds(c, 1)].broadcast_to([40, P]))
                dve.wait_ge(sem.zx_high, t + 1)
                nc.vector.tensor_tensor(m.zxL[:, rep % 2].rearrange("p k n -> p (k n)"), ps_z[:, 0:D],
                                        m.zxH[:, rep % 2].rearrange("p k n -> p (k n)").bitcast(F32), ALU.subtract)\
                  .then_inc(sem.zx_low, 1)

            def body(t, rep, turn):
                if rep + 1 < NSLOT:
                    turned(t + 1, rep + 1)
                if within(rep - 1, 0, NSLOT):
                    i, r = t - 1, (rep - 1) % 2
                    dve.wait_ge(sem.ex_high, i + 1)
                    nc.vector.tensor_tensor(m.exL[:, r].rearrange("p k n -> p (k n)"), ps_x[:, r],
                                            m.exH[:, r].rearrange("p k n -> p (k n)").bitcast(F32), ALU.subtract)\
                      .then_inc(sem.ex_low, 1)
                if within(rep - 2, 0, NSLOT):
                    i, r = t - 2, (rep - 2) % 2
                    dve.wait_ge(sem.eo_mm, i + 1)
                    if rep - 2 >= 2:
                        dve.wait_ge(sem.eo_stored[r], 16 * (2 * turn + (rep % 4 - 2) // 2))
                    nc.vector.tensor_copy(m.eo[:, r], ps_o[:, r, 0:D]).then_inc(sem.eo_out, 1)
            turned(0, 0)
            steps(dve, body)

def layer3_combine(nc, m, d, sem, e_rows, out):
    W = m.work
    place(nc, m, "ra", [P, 4, D], F32, W)
    place(nc, m, "rbb", [P, 4, D], F32, W + 4 * KB)
    place(nc, m, "xc", [P, 4, KD, P], F32, W + 8 * KB)
    place(nc, m, "res", [P, 4, D], F32, W + 12 * KB)

    def steps(eng, body):
        segments(eng, [0, 1, TT_ // 4], lambda s, rep: [body(4 * s + u, 4 * rep + u, s) for u in range(4)])

    with nc.psum_tensor("co_x", [P, 4, CH], F32) as ps, nc.Block() as block:
        @block.gpsimd
        def _(pool):
            for t in range(TT_):
                if t >= 4:
                    pool.wait_ge(sem.co_sum, 2 * (t - 3))
                for k, rows in enumerate((m.ra, m.rbb)):
                    pool.indirect_dma_start(rows[:, t % 4], None, e_rows, bass.IndirectOffsetOnAxis(ap=m.pos[:, t, k:k + 1], axis=0))\
                      .then_inc(sem.gathered[t % 4], 16)

        @block.scalar
        def _(act):
            def body(t, rep, turn):
                if rep >= 4:
                    act.wait_ge(sem.co_mm, t - 3)
                t = apart(act, t)
                nc.scalar.copy(m.xc[:, rep % 4], m.X[:, :, ds(t * P, P)]).then_inc(sem.co_copy, 1)
            steps(act, body)

        @block.tensor
        def _(pe):
            def body(t, rep, turn):
                pe.wait_ge(sem.co_copy, t + 1)
                if rep >= 4:
                    pe.wait_ge(sem.co_sum, 2 * (t - 3))
                for h in range(KD):
                    last = nc.tensor.transpose(ps[:, rep % 4, ts(h, P)], m.xc[:, rep % 4, h], m.ident[:])
                last.then_inc(sem.co_mm, 1)
            steps(pe, body)

        @block.vector
        def _(dve):
            def body(t, rep, turn):
                u = rep % 4
                if rep >= 4:
                    dve.wait_ge(sem.co_stored[u], 16 * turn)
                dve.wait_ge(sem.gathered[u], 32 * (turn + 1))
                dve.wait_ge(sem.co_mm, t + 1)
                c = apart(dve, t)
                nc.vector.scalar_tensor_tensor(m.res[:, u], m.ra[:, u], m.pw[:, ds(c, 1), 0:1].rearrange("p a b -> p (a b)"),
                                               ps[:, u, 0:D], ALU.mult, ALU.add).then_inc(sem.co_sum, 1)
                dve.wait_ge(sem.co_sum, 2 * t + 1)
                c = apart(dve, t)
                nc.vector.scalar_tensor_tensor(m.res[:, u], m.rbb[:, u], m.pw[:, ds(c, 1), 1:2].rearrange("p a b -> p (a b)"),
                                               m.res[:, u], ALU.mult, ALU.add).then_inc(sem.co_sum, 1)
            steps(dve, body)

        @block.sync
        def _(sp):
            def body(t, rep, turn):
                sp.wait_ge(sem.co_sum, 2 * t + 2)
                t = apart(sp, t)
                sp.dma_start(out[ds(t * P, P), :], m.res[:, rep % 4]).then_inc(sem.co_stored[rep % 4], 16)
            steps(sp, body)
            for u in range(4):
                sp.wait_ge(sem.co_stored[u], 16 * (TT_ // 4))


L0_SEMS = """rows_clear prep_pool prep_load prep_pe prep_hot prep_dve tok_mm tok_act turn_mm y_added yh_cond yl_cond yh_upd
yl_upd h1_act h1_mm h1_low h2_act h2_mm h2_low h3_act h3_mm h3_low th_act th_mm sums g_act g_mm coupl_b
cs_done t0_done t1_done y_upd""".split()
L1_SEMS = """x1_sum lap l1_const w1_loaded w1_rec w1_dve w1_scale w1_clip win_m wout_m win_q wout_q win_mm win_t lap_mm
du_a du_b du_c du_d du_done du_max q_done q_dve hid_mm hid_act hid_max g_round g_clip g_low_odd g_scaled
g_high g_low g_mm1 o1_act x2_sum""".split()
L2_SEMS = """w2_loaded w2_high w2_low xs_copied tok2_mm tok2_act turn2_mm y2_added y2_high y2_low h2a_mm h2a_act h2a_low
o2_mm x3_sum""".split()
L3_SEMS = """w3_loaded w3_high w3_low r_loaded we_low x3_low h3a_act x4_sum sh_act h3a_mm z_low sh_mm ye_act r_mm z_done
h3a_low zt_act hot_done rank_mm rt_step e_mm sh_low s2_mm zt_mm t3_mm scattered x3_high we_high
z_high pos_done iota_done rank_const before_done ew_low ew_loaded ew_high zeros_done tab_pool rt_dve rt_exp
tab_done tab_mm eb_loaded padded zx_mm zx_low eh_act eh_mm ex_low ex_mm eo_out eo_mm ex_high zx_high
co_sum co_mm co_copy""".split()


INPUTS = {
    "xT": "x", "ids0": "itok_B_0_7", "ids2": "itok_B_0_30", "zX": "condB_zX", "zY": "condB_zY", "zR": "condB_zR",
    "c0_wT": "L0_cond_weight", "c0_b": "L0_cond_bias",
    "cn_w1": "L0_ffn_cn_w1", "cn_b1": "L0_ffn_cn_b1", "cn_w2": "L0_ffn_cn_w2", "cn_b2": "L0_ffn_cn_b2",
    "cn_w3": "L0_ffn_cn_w3", "cn_b3": "L0_ffn_cn_b3", "cn_w4": "L0_ffn_cn_w4", "cn_b4": "L0_ffn_cn_b4",
    "gc_w1": "L0_ffn_gc_w1", "gc_b1": "L0_ffn_gc_b1", "gc_w2": "L0_ffn_gc_w2", "gc_b2": "L0_ffn_gc_b2",
    "gc_w3": "L0_ffn_gc_w3", "gc_b3": "L0_ffn_gc_b3", "ar": "L0_ffn_adaptive_range",
    "w_inT": "L1_ffn_W_in", "b_in": "L1_ffn_b_in", "w_out": "L1_ffn_W_out", "b_out": "L1_ffn_b_out",
    "c2_w": "L2_cond_W", "c2_b": "L2_cond_b", "f2_w1": "L2_ffn_w1", "f2_b1": "L2_ffn_b1",
    "f2_w2": "L2_ffn_w2", "f2_b2": "L2_ffn_b2", "c3_w1": "L3_cond_W1", "c3_b1": "L3_cond_b1",
    "c3_w2": "L3_cond_W2", "c3_b2": "L3_cond_b2", "we": "L3_cond_We", "be": "L3_cond_be",
    "rw": "L3_ffn_router_w", "rb": "L3_ffn_router_b", "sw1": "L3_ffn_sw1", "sb1": "L3_ffn_sb1",
    "sw2": "L3_ffn_sw2", "sb2": "L3_ffn_sb2", "ew1": "L3_ffn_rw1", "eb1": "L3_ffn_rb1",
    "ew2": "L3_ffn_rw2", "eb2": "L3_ffn_rb2",
}


def acquire(nc, sem, names, groups=()):
    for name in names:
        sem[name] = nc.alloc_semaphore(name)
    for name, n in groups:
        sem[name] = [nc.alloc_semaphore(f"{name}{i}") for i in range(n)]


def retire(nc, sem):
    for s in list(sem.values()):
        nc.clear_and_free_semaphores(s if isinstance(s, list) else [s])
    sem.clear()
    nc.all_engine_barrier()


def build(nc, d, out):
    sem, m = Names(), Names()
    common_memory(nc, m)
    acquire(nc, sem, L0_SEMS, (("x_loaded", 5), ("cw_loaded", SLOTS)))
    prepare(nc, m, d, sem)
    layer0(nc, m, d, sem)
    retire(nc, sem)
    acquire(nc, sem, L1_SEMS, (("red_mm", 2), ("red_v", 2)))
    layer1(nc, m, d, sem)
    retire(nc, sem)
    acquire(nc, sem, L2_SEMS, (("cw2_loaded", BPC),))
    layer2(nc, m, d, sem)
    retire(nc, sem)
    acquire(nc, sem, L3_SEMS, (("we_loaded", 2), ("zr_loaded", 4), ("gathered", 4), ("eo_stored", 2), ("co_stored", 4)))
    z_rows = nc.dram_tensor("z_rows", (SPARE + NE * P, D), F32).ap()
    e_rows = nc.dram_tensor("e_rows", (NSLOT * P, D), F32).ap()
    layer3_shared(nc, m, d, sem, z_rows)
    layer3_tables(nc, m, d, sem, z_rows)
    layer3_experts(nc, m, d, sem, z_rows, e_rows)
    layer3_combine(nc, m, d, sem, e_rows, out)


def lay_out(program_name, a):
    if program_name == "xT":
        return a.reshape(T, D).T
    if program_name == "c0_wT":
        return a.transpose(0, 2, 1)
    if program_name == "w_inT":
        return a.T
    return a


def kernel(**inputs):
    import numpy as np
    import concourse.bacc as bacc
    from concourse.bass_utils import run_bass_kernel_spmd

    nc = bacc.Bacc("TRN2", target_bir_lowering=False, num_devices=1)
    arrays, aps = {}, {}
    for name, source in INPUTS.items():
        a = np.ascontiguousarray(lay_out(name, np.asarray(inputs[source])))
        arrays["in_" + name] = a
        aps[name] = nc.dram_tensor("in_" + name, a.shape, mybir.dt.from_np(a.dtype), kind="ExternalInput").ap()
    out = nc.dram_tensor("out_0", (T, D), F32, kind="ExternalOutput").ap()
    build(nc, Names(aps), out)
    result = run_bass_kernel_spmd(nc, [arrays], core_ids=[0])
    return result.results[0]["out_0"].reshape(BATCH, SEQ, D)
```

```python
import concourse.bass as bass
from concourse import mybir

ALU = mybir.AluOpType
ACT = mybir.ActivationFunctionType
F32 = mybir.dt.float32
F32R = mybir.dt.float32r
BF16 = mybir.dt.bfloat16
I32 = mybir.dt.int32
AX = mybir.AxisListType
ds, ts = bass.ds, bass.ts


class Names(dict):
    def __getattr__(self, name):
        return self[name]


P = 128
BATCH, SEQ, D = 64, 64, 256
T = BATCH * SEQ
KD = D // P
CH = 512
NC = T // CH
BPC = CH // SEQ
PAIRS = CH // P
SLOTS = 6
NCYCLE = 3
NITEM = NCYCLE * NC
KB = 1024
MAGIC = 1.5 * 2.0 ** 23
PARTS = ((0, 0), (0, 1), (1, 0))


def segments(eng, cuts, body):
    for lo, hi in zip(cuts, cuts[1:]):
        if hi - lo == 1:
            body(lo, lo)
        else:
            with eng.Fori(lo, hi) as step:
                body(step, lo)


def apart(eng, x):
    return x if isinstance(x, int) else eng.snap(x)


def within(x, lo, hi):
    return lo <= x < hi


def per_batch(ap, n=BPC):
    return ap.unsqueeze(2).broadcast_to([P, n, SEQ])


def by_batch(ap):
    return ap.rearrange("p (b s) -> p b s", s=SEQ)


def products(nc, out, weights, data, start, stop):
    for n, (a, b) in enumerate(PARTS):
        last = nc.tensor.matmul(out, weights[a], data[b], start=start and n == 0,
                                stop=stop and n == len(PARTS) - 1)
    return last



def place(nc, m, name, shape, dt, at):
    m[name] = nc.alloc_sbuf_tensor_at(name, shape, dt, offset=m.base + at)


BIASES = (("cn_b1", 256), ("cn_b2", 128), ("cn_b3", 64), ("gc_b1", 128), ("gc_b2", 64), ("b_in", 1024), ("b_out", 256),
          ("f2_b1", 1024), ("f2_b2", 256), ("c3_b1", 1024), ("c3_b2", 192), ("sb1", 512), ("sb2", 256))
NROWS = 48


def first_rows():
    out, r = {}, 0
    for name, n in BIASES:
        out[name] = r
        r += (n + P - 1) // P
    assert r <= NROWS
    return out


ROWS = first_rows()


def common_memory(nc, m):
    m.base = (nc.sbuf_base + 31) // 32 * 32
    place(nc, m, "X", [P, KD, T], F32, 0)
    c = 32 * KB

    def const(name, cols, dt=F32):
        nonlocal c
        place(nc, m, name, [P, cols], dt, c)
        c += (cols * 4 + 31) // 32 * 32

    const("ident", P)
    const("biases", 48)
    const("cond0", KD * BATCH)
    const("coupl_b", BATCH)
    const("zxyz", 3 * BATCH)
    const("zk", BATCH)
    const("cond2", KD * BATCH)
    const("cond3", BATCH)
    const("scal", 16)
    const("magic", 1)
    const("nmagic", 1)
    const("ones1", P)
    const("ids0", BATCH, I32)
    const("ids2", BATCH, I32)
    m.work = 36 * KB + 512
    assert c <= m.work

    m.AR, m.CN_B4, m.GC_B3, m.SIGN, m.AMUL, m.GMUL, m.TENTH, m.CNB4, m.GCB3 = range(9)


def sc(m, col, rows=P):
    return m.scal[0:rows, col:col + 1]



def load_cw(sp, m, d, sem, b):
    i = sp.value_load(m.ids0[0:1, b:b + 1], min_val=0, max_val=7)
    if b >= SLOTS:
        sp.wait_ge(sem.tok_mm, (b - SLOTS) // 2 + 1)
    sp.dma_start(m.cw[:, b % SLOTS], d.c0_wT[ds(i, 1)].rearrange("e (k p) o -> p (e k) o", p=P))\
      .then_inc(sem.cw_loaded[b % SLOTS], 16)


def load_x(sp, m, d, sem, c):
    sp.dma_start(m.X[:, :, ts(c, CH)], d.xT.rearrange("(k p) t -> p k t", p=P)[:, :, ts(c, CH)]).then_inc(sem.x_loaded[c], 16)


def prepare(nc, m, d, sem):
    W = m.work
    place(nc, m, "cw", [P, SLOTS, KD, D], F32, W + 98 * KB)
    w = W + 98 * KB + 16 * KB
    for name, rows, cols in (("cnw1", P, KD * 256), ("cnw2", P, KD * 128), ("cnw3", P, 64), ("cnw4", 64, 128)):
        for part in "HL":
            place(nc, m, name + part, [rows, cols], F32R, w)
            w += cols * 4
    for name, rows, cols in (("gcw1", P, KD * 128), ("gcw2", P, 64), ("gcw3", 64, 128)):
        place(nc, m, name, [rows, cols], F32, w)
        w += cols * 4
    m.l0_work = w
    s = w
    stage = {}
    for name, rows, cols in (("cnw1", P, KD * 256), ("cnw2", P, KD * 128), ("cnw3", P, 64), ("cnw4", 64, 128)):
        place(nc, m, "stage_" + name, [rows, cols], F32, s)
        stage[name] = m["stage_" + name]
        s += cols * 4
    for name, rows, cols, dt in (("rows", NROWS, P, F32), ("lastcols", 64, 2, F32),
                                 ("b0tab", 8, 256, F32), ("b2tab", 32, 256, F32), ("betab", 8, 64, F32),
                                 ("idsB0", 32, BATCH, I32), ("idsB2", 32, BATCH, I32),
                                 ("hot0", 32, BATCH, F32), ("hot2", 32, BATCH, F32),
                                 ("lane", P, 1, F32), ("laneI", P, 1, I32), ("ones", 64, P, F32)):
        place(nc, m, "t_" + name, [rows, cols], dt, s)
        s += max(32, cols * 4)
    with nc.psum_tensor("prep_psum", [P, 5, 512], F32) as ps:
        with nc.Block() as block:
            @block.gpsimd
            def _(pool):
                pool.memset(m.ident[:], 1.0).then_inc(sem.prep_pool, 1)
                pool.memset(m.t_ones[:], 1.0)
                pool.memset(m.magic[:], MAGIC)
                pool.memset(m.nmagic[:], -MAGIC).then_inc(sem.prep_pool, 1)
                pool.iota(m.t_laneI[:], pattern=[[0, 1]], base=0, channel_multiplier=1).then_inc(sem.prep_pool, 1)
                pool.memset(m.scal[:], 0.0).then_inc(sem.prep_pool, 1)
                pool.wait_ge(sem.prep_pool, 4)
                pool.affine_select(out=m.ident[:], in_=m.ident[:], compare_op=ALU.is_equal, fill=0.0, base=0,
                                   pattern=[[1, P]], channel_multiplier=-1).then_inc(sem.prep_pool, 1)
                pool.wait_ge(sem.prep_pool, 5)

            @block.sync
            def _(sp):
                sp.dma_start(m.ids0[0:1, :], d.ids0.unsqueeze(0)).then_inc(sem.ids_loaded, 16)
                load_x(sp, m, d, sem, 0)
                for dst, src in ((m.ids2[0:1, :], d.ids2.unsqueeze(0)),
                                 (stage["cnw1"].rearrange("p (k n) -> p k n", k=KD), d.cn_w1.rearrange("(k p) n -> p k n", p=P)),
                                 (stage["cnw2"].rearrange("p (k n) -> p k n", k=KD), d.cn_w2.rearrange("(k p) n -> p k n", p=P)),
                                 (stage["cnw3"][:], d.cn_w3),
                                 (m.t_lastcols[:], d.lastcols),
                                 (m.gcw1.rearrange("p (k n) -> p k n", k=KD), d.gc_w1.rearrange("(k p) n -> p k n", p=P)),
                                 (m.gcw2[:], d.gc_w2)):
                    sp.dma_start(dst, src).then_inc(sem.prep_load, 16)

            @block.scalar
            def _(act):
                act.wait_ge(sem.prep_pool, 4)
                for dst, src in ((m.t_rows[:], d.rows), (m.t_b0tab[:], d.c0_b), (m.t_idsB0[:], d.ids0.partition_broadcast(32)),
                                 (m.scal[:, m.AR:m.GC_B3 + 1], d.scalars.partition_broadcast(P)),
                                 (m.zxyz[:], d.zs.partition_broadcast(P)),
                                 (m.t_b2tab[:], d.c2_b), (m.t_betab[:], d.be), (m.t_idsB2[:], d.ids2.partition_broadcast(32))):
                    act.dma_start(dst, src).then_inc(sem.prep_load, 16)

        n_loads = 7 + 8
        with nc.Block() as block:
            @block.sync
            def _(sp):
                sp.wait_ge(sem.ids_loaded, 16)
                for b in range(SLOTS):
                    load_cw(sp, m, d, sem, b)
                load_x(sp, m, d, sem, 1)

            @block.tensor
            def _(pe):
                pe.wait_ge(sem.prep_load, 16 * n_loads)
                nc.tensor.transpose(ps[:, 0, 0:48], m.t_rows[:], m.ident[0:48, 0:48]).then_inc(sem.prep_pe, 1)
                pe.wait_ge(sem.prep_hot, 2)
                for k in range(KD):
                    nc.tensor.matmul(ps[:, 1, ts(k, BATCH)], m.t_b0tab[:, ts(k, P)], m.t_hot0[0:8, :], start=True, stop=True)
                    nc.tensor.matmul(ps[:, 2, ts(k, BATCH)], m.t_b2tab[:, ts(k, P)], m.t_hot2[:], start=True, stop=True)
                nc.tensor.matmul(ps[64:128, 3, 0:BATCH], m.t_betab[:], m.t_hot0[0:8, :], start=True, stop=True)\
                  .then_inc(sem.prep_pe, 1)

            @block.vector
            def _(dve):
                own = sem.prep_dve
                n = [0]

                def mark(i):
                    i.then_inc(own, 1)
                    n[0] += 1
                    return n[0]
                dve.wait_ge(sem.prep_load, 16 * n_loads)
                mark(nc.vector.tensor_copy(m.t_lane[:], m.t_laneI[:]))
                mark(nc.vector.tensor_copy(m.t_hot0[:], m.t_idsB0[:]))
                dve.wait_ge(own, mark(nc.vector.tensor_copy(m.t_hot2[:], m.t_idsB2[:])))
                for t in (m.t_hot0, m.t_hot2):
                    nc.vector.tensor_scalar(t[:], t[:], m.t_lane[0:32, :], None, ALU.is_equal).then_inc(sem.prep_hot, 1)
                mark(nc.vector.memset(m.scal[0:64, m.SIGN:m.SIGN + 1], 1.0))
                mark(nc.vector.memset(m.scal[64:128, m.SIGN:m.SIGN + 1], -1.0))
                mark(nc.vector.tensor_scalar(m.stage_cnw4[:], m.t_ones[:], m.t_lastcols[:, 0:1], None, ALU.mult))
                mark(nc.vector.tensor_scalar(m.gcw3[:], m.t_ones[:], m.t_lastcols[:, 1:2], None, ALU.mult))
                mark(nc.vector.tensor_scalar(sc(m, m.CNB4), sc(m, m.CN_B4), 0.5, None, ALU.mult))
                mark(nc.vector.tensor_scalar(sc(m, m.GCB3), sc(m, m.GC_B3), 0.5, None, ALU.mult))
                for name in ("cnw1", "cnw2", "cnw3"):
                    mark(nc.vector.tensor_copy(m[name + "H"][:], stage[name][:]))
                dve.wait_ge(own, n[0])
                mark(nc.vector.tensor_copy(m.cnw4H[:], m.stage_cnw4[:]))
                mark(nc.vector.tensor_scalar(sc(m, m.AMUL), sc(m, m.AR), sc(m, m.SIGN), 0.3, ALU.mult, ALU.mult))
                mark(nc.vector.tensor_scalar(sc(m, m.GMUL), sc(m, m.AR), sc(m, m.SIGN), 0.7, ALU.mult, ALU.mult))
                mark(nc.vector.tensor_scalar(sc(m, m.TENTH), sc(m, m.SIGN), 0.1, None, ALU.mult))
                mark(nc.vector.scalar_tensor_tensor(m.zk[:], m.zxyz[:, 64:128], -2.0, m.zxyz[:, 128:192],
                                                    ALU.mult, ALU.add))
                dve.wait_ge(own, n[0])
                for name in ("cnw1", "cnw2", "cnw3", "cnw4"):
                    nc.vector.tensor_tensor(m[name + "L"][:], stage[name][:],
                                            m[name + "H"][:].bitcast(F32), ALU.subtract)
                dve.wait_ge(sem.prep_pe, 1)
                mark(nc.vector.tensor_copy(m.biases[:], ps[:, 0, 0:48]))
                dve.wait_ge(sem.prep_pe, 2)
                mark(nc.vector.tensor_copy(m.cond0[:], ps[:, 1, 0:KD * BATCH]))
                mark(nc.vector.tensor_copy(m.cond2[:], ps[:, 2, 0:KD * BATCH]))
                mark(nc.vector.tensor_copy(m.cond3[64:128, :], ps[64:128, 3, 0:BATCH]))
                dve.wait_ge(own, n[0])
                mark(nc.vector.memset(m.cond3[0:64, :], 0.0))
                dve.wait_ge(own, n[0])
                r = ROWS["c3_b2"] + 1
                mark(nc.vector.tensor_scalar(m.cond3[0:64, :], m.cond3[0:64, :], m.biases[0:64, r:r + 1], None, ALU.add))
                dve.wait_ge(own, n[0])


def bias(m, name, k=0, rows=P):
    r = ROWS[name] + k
    return m.biases[0:rows, r:r + 1]



def layer0(nc, m, d, sem):
    W = m.work
    place(nc, m, "Y", [P, KD, T], F32, W)
    place(nc, m, "YH", [P, KD, T], F32R, W + 32 * KB)
    place(nc, m, "YL", [P, KD, T], F32R, W + 64 * KB)
    place(nc, m, "yt", [P, PAIRS, D], F32, W + 110 * KB)
    place(nc, m, "l0_small", [P, 72], F32, W + 96 * KB)
    a = m.l0_work
    for name, rows, shape, dt in (("h1F", P, [KD, CH], F32), ("h1H", P, [2, KD, CH], F32R), ("h1L", P, [2, KD, CH], F32R),
                                  ("h2F", P, [CH], F32), ("h2H", P, [2, CH], F32R), ("h2L", P, [2, CH], F32R),
                                  ("h3F", 64, [CH], F32), ("h3H", 64, [2, CH], F32R), ("h3L", 64, [2, CH], F32R),
                                  ("th", P, [CH], F32), ("cs", P, [CH], F32), ("t0", P, [CH], F32), ("t1", P, [CH], F32)):
        place(nc, m, name, [rows] + shape, dt, a)
        size = 4
        for x in shape:
            size *= x
        a += size
    gsum = m.l0_small[:, 40:72].rearrange("p (s n) -> p s n", s=2)
    g1 = m.l0_small[:, 16:24]
    g2 = m.l0_small[0:64, 24:32]
    tg = m.l0_small[:, 32:40]
    cnw1 = [x.rearrange("p (k n) -> p k n", k=KD) for x in (m.cnw1H, m.cnw1L)]
    cnw2 = [x.rearrange("p (k n) -> p k n", k=KD) for x in (m.cnw2H, m.cnw2L)]
    gcw1 = m.gcw1.rearrange("p (k n) -> p k n", k=KD)
    LAST_SPLIT = NITEM - NC

    CUTS = [*range(NC + 5), LAST_SPLIT + 4, *range(NITEM, NITEM + 5)]

    with nc.psum_tensor("l0_tok", [P, CH], F32) as ps_tok, nc.psum_tensor("l0_turn", [P, CH], F32) as ps_turn, \
            nc.psum_tensor("l0_h1", [P, KD, CH], F32) as ps_h1, \
            nc.psum_tensor("l0_h2", [P, CH], F32) as ps_h2, nc.psum_tensor("l0_h3", [P, CH], F32) as ps_h3, \
            nc.psum_tensor("l0_th", [P, CH], F32) as ps_th, nc.psum_tensor("l0_g", [P, CH], F32) as ps_g, \
            nc.Block() as block:

        @block.sync
        def _(sp):
            for b in range(SLOTS, BATCH):
                if b % BPC == 4 or b == SLOTS:
                    c = 2 if b == SLOTS else b // BPC + 2
                    if c < NC:
                        load_x(sp, m, d, sem, c)
                load_cw(sp, m, d, sem, b)

        @block.tensor
        def _(pe):
            def pair(c, rep, q):
                if q == 0:
                    pe.wait_ge(sem.x_loaded[c], 16)
                if c >= 1 or q >= 1:
                    pe.wait_ge(sem.tok_act, c * PAIRS + q)
                for b in (c * BPC + 2 * q, c * BPC + 2 * q + 1):
                    pe.wait_ge(sem.cw_loaded[b % SLOTS], 16 * (b // SLOTS + 1))
                    for k in range(KD):
                        last = nc.tensor.matmul(ps_tok[ts(b % 2, SEQ), 0:D], m.X[:, k, ts(b, SEQ)], m.cw[:, b % SLOTS, k],
                                                start=k == 0, stop=k == KD - 1)
                last.then_inc(sem.tok_mm, 1)

            def turn(c, rep, h):
                pe.wait_ge(sem.tok_act, (c + 1) * PAIRS)
                if rep >= 1 or h >= 1:
                    pe.wait_ge(sem.y_added, 2 * c + h)
                for q in range(PAIRS):
                    last = nc.tensor.transpose(ps_turn[:, ts(q, P)], m.yt[:, q, ts(h, P)], m.ident[:])
                last.then_inc(sem.turn_mm, 1)

            def body(j, rep):
                cond = rep + 2 < NC
                if cond:
                    pair(j + 2, rep + 2, 0)
                if rep < NITEM:
                    c = j % NC
                    if rep < NC:
                        pe.wait_ge(sem.yh_cond, 2 * j + 2)
                        pe.wait_ge(sem.yl_cond, 2 * j + 2)
                    else:
                        pe.wait_ge(sem.yh_upd, 2 * (j - NC) + 2)
                        pe.wait_ge(sem.yl_upd, 2 * (j - NC) + 2)
                    for h in range(KD):
                        if rep >= 1:
                            pe.wait_ge(sem.h1_act, 2 * j - 1 + h)
                        for k in range(KD):
                            last = products(nc, ps_h1[:, h], [w[:, k, ts(h, P)] for w in cnw1],
                                            [y[:, k, ds(c * CH, CH)] for y in (m.YH, m.YL)], k == 0, k == KD - 1)
                        last.then_inc(sem.h1_mm, 1)
                        if cond and h == 0:
                            pair(j + 2, rep + 2, 1)
                if rep < NC + 2:
                    if rep >= 1:
                        pe.wait_ge(sem.g_act, j)
                    if rep < NC:
                        pe.wait_ge(sem.sums, j + 1)
                        for k in range(KD):
                            last = nc.tensor.matmul(ps_g[:, 0:BPC], gcw1[:, k], gsum[:, j % 2, ts(k, BPC)], start=k == 0, stop=k == KD - 1)
                    if within(rep - 1, 0, NC):
                        last = nc.tensor.matmul(ps_g[0:64, 8:16], m.gcw2[:], g1, start=True, stop=True)
                    if within(rep - 2, 0, NC):
                        last = nc.tensor.matmul(ps_g[:, 16:24], m.gcw3[:], g2, start=True, stop=True)
                    last.then_inc(sem.g_mm, 1)
                if cond:
                    pair(j + 2, rep + 2, 2)
                if within(rep - 1, 0, NITEM):
                    i = j - 1
                    pe.wait_ge(sem.h1_act, 2 * i + 2)
                    pe.wait_ge(sem.h1_low, 2 * i + 2)
                    if rep - 1 >= 1:
                        pe.wait_ge(sem.h2_act, i)
                    for k in range(KD):
                        last = products(nc, ps_h2[:], [w[:, k] for w in cnw2],
                                        [x[:, i % 2, k] for x in (m.h1H, m.h1L)], k == 0, k == KD - 1)
                    last.then_inc(sem.h2_mm, 1)
                if cond:
                    pair(j + 2, rep + 2, 3)
                if within(rep - 2, 0, NITEM):
                    i = j - 2
                    pe.wait_ge(sem.h2_act, i + 1)
                    pe.wait_ge(sem.h2_low, i + 1)
                    if rep - 2 >= 1:
                        pe.wait_ge(sem.h3_act, i)
                    products(nc, ps_h3[0:64, :], (m.cnw3H[:], m.cnw3L[:]),
                             [x[:, i % 2] for x in (m.h2H, m.h2L)], True, True).then_inc(sem.h3_mm, 1)
                if cond:
                    turn(j + 2, rep + 2, 0)
                if within(rep - 3, 0, NITEM):
                    i = j - 3
                    pe.wait_ge(sem.h3_act, i + 1)
                    pe.wait_ge(sem.h3_low, i + 1)
                    if rep - 3 >= 1:
                        pe.wait_ge(sem.th_act, i)
                    products(nc, ps_th[:], (m.cnw4H[:], m.cnw4L[:]),
                             [x[:, i % 2] for x in (m.h3H, m.h3L)], True, True).then_inc(sem.th_mm, 1)
                if cond:
                    turn(j + 2, rep + 2, 1)

            for c in range(2):
                for q in range(PAIRS):
                    pair(c, c, q)
                for h in range(KD):
                    turn(c, c, h)
            segments(pe, CUTS, body)

        @block.scalar
        def _(act):
            def pair(c, rep, q):
                act.wait_ge(sem.tok_mm, c * PAIRS + q + 1)
                if rep >= 1:
                    act.wait_ge(sem.turn_mm, 2 * c)
                nc.scalar.copy(m.yt[:, q], ps_tok[:, 0:D]).then_inc(sem.tok_act, 1)

            def body(j, rep):
                cond = rep + 2 < NC
                if cond:
                    pair(j + 2, rep + 2, 0)
                if rep < NITEM:
                    for h in range(KD):
                        act.wait_ge(sem.h1_mm, 2 * j + h + 1)
                        if rep >= 1:
                            act.wait_ge(sem.h1_low, 2 * j - 1 + h)
                        if rep >= 2:
                            act.wait_ge(sem.h2_mm, j - 1)
                        nc.scalar.activation(m.h1H[:, j % 2, h], ps_h1[:, h], ACT.Gelu, bias=bias(m, "cn_b1", h))
                        nc.scalar.activation(m.h1F[:, h], ps_h1[:, h], ACT.Gelu, bias=bias(m, "cn_b1", h))\
                          .then_inc(sem.h1_act, 1)
                        if cond and h == 0:
                            pair(j + 2, rep + 2, 1)
                if rep < NC + 2:
                    act.wait_ge(sem.g_mm, j + 1)
                    if within(rep - 2, 0, NC):
                        if rep - 2 >= 1:
                            act.wait_ge(sem.coupl_b, j - 2)
                        last = nc.scalar.activation(tg, ps_g[:, 16:24], ACT.Tanh, bias=sc(m, m.GCB3), scale=0.5)
                    if within(rep - 1, 0, NC):
                        last = nc.scalar.activation(g2, ps_g[0:64, 8:16], ACT.Gelu, bias=bias(m, "gc_b2", rows=64))
                    if rep < NC:
                        last = nc.scalar.activation(g1, ps_g[:, 0:BPC], ACT.Gelu, bias=bias(m, "gc_b1"), scale=1.0 / SEQ)
                    last.then_inc(sem.g_act, 1)
                if cond:
                    pair(j + 2, rep + 2, 2)
                if within(rep - 1, 0, NITEM):
                    i = j - 1
                    act.wait_ge(sem.h2_mm, i + 1)
                    if rep - 1 >= 1:
                        act.wait_ge(sem.h2_low, i)
                    if rep - 1 >= 2:
                        act.wait_ge(sem.h3_mm, i - 1)
                    nc.scalar.activation(m.h2H[:, i % 2], ps_h2[:], ACT.Gelu, bias=bias(m, "cn_b2"))
                    nc.scalar.activation(m.h2F[:], ps_h2[:], ACT.Gelu, bias=bias(m, "cn_b2")).then_inc(sem.h2_act, 1)
                if cond:
                    pair(j + 2, rep + 2, 3)
                if within(rep - 2, 0, NITEM):
                    i = j - 2
                    act.wait_ge(sem.h3_mm, i + 1)
                    if rep - 2 >= 1:
                        act.wait_ge(sem.h3_low, i)
                    if rep - 2 >= 2:
                        act.wait_ge(sem.th_mm, i - 1)
                    nc.scalar.activation(m.h3H[:, i % 2], ps_h3[0:64, :], ACT.Gelu, bias=bias(m, "cn_b3", rows=64))
                    nc.scalar.activation(m.h3F[:], ps_h3[0:64, :], ACT.Gelu, bias=bias(m, "cn_b3", rows=64))\
                      .then_inc(sem.h3_act, 1)
                if within(rep - 3, 0, NITEM):
                    i = j - 3
                    act.wait_ge(sem.th_mm, i + 1)
                    if rep - 3 >= 1:
                        act.wait_ge(sem.cs_done, i)
                    nc.scalar.activation(m.th[:], ps_th[:], ACT.Tanh, bias=sc(m, m.CNB4), scale=0.5)\
                      .then_inc(sem.th_act, 1)
            for c in range(2):
                for q in range(PAIRS):
                    pair(c, c, q)
            segments(act, CUTS, body)

        @block.vector
        def _(dve):
            def cond_bias(c, rep):
                for h in range(KD):
                    dve.wait_ge(sem.turn_mm, KD * c + h + 1)
                    nc.vector.tensor_tensor(by_batch(m.Y[:, h, ds(c * CH, CH)]), by_batch(ps_turn[:]),
                                            per_batch(m.cond0[:, ds(h * BATCH + c * BPC, BPC)]), ALU.add)\
                      .then_inc(sem.y_added, 1)

            def cond(c, rep):
                if rep >= 2:
                    dve.wait_ge(sem.g_mm, c - 1)
                for h in range(KD):
                    dve.wait_ge(sem.y_added, 2 * c + 1 + h)
                    nc.vector.tensor_copy(m.YH[:, h, ds(c * CH, CH)], m.Y[:, h, ds(c * CH, CH)]).then_inc(sem.yh_cond, 1)
                for h in range(KD):
                    last = nc.vector.tensor_reduce(gsum[:, c % 2, ts(h, BPC)], by_batch(m.Y[:, h, ds(c * CH, CH)]), AX.X, ALU.add)
                last.then_inc(sem.sums, 1)

            def body(j, rep):
                upd = within(rep - 4, 0, NITEM)
                u = j - 4
                if rep < NITEM:
                    for h in range(KD):
                        dve.wait_ge(sem.h1_act, 2 * j + h + 1)
                        if rep >= 2:
                            dve.wait_ge(sem.h2_mm, j - 1)
                        nc.vector.tensor_tensor(m.h1L[:, j % 2, h], m.h1F[:, h], m.h1H[:, j % 2, h].bitcast(F32),
                                                ALU.subtract).then_inc(sem.h1_low, 1)
                if upd:
                    uc = u % NC
                    dve.wait_ge(sem.th_act, u + 1)
                    if rep - 4 < NC:
                        dve.wait_ge(sem.coupl_b, u + 1)
                    if rep - 4 >= 1:
                        dve.wait_ge(sem.t1_done, u)
                    nc.vector.scalar_tensor_tensor(by_batch(m.cs[:]), by_batch(m.th[:]), sc(m, m.AMUL),
                                                   per_batch(m.coupl_b[:, ds(uc * BPC, BPC)]), ALU.mult, ALU.add)\
                      .then_inc(sem.cs_done, 1)
                    dve.wait_ge(sem.cs_done, u + 1)
                    nc.vector.tensor_tensor(m.t0[:], m.cs[:], m.Y[:, 1, ds(uc * CH, CH)], ALU.mult).then_inc(sem.t0_done, 1)
                if within(rep - 1, 0, NITEM):
                    i = j - 1
                    dve.wait_ge(sem.h2_act, i + 1)
                    if rep - 1 >= 2:
                        dve.wait_ge(sem.h3_mm, i - 1)
                    nc.vector.tensor_tensor(m.h2L[:, i % 2], m.h2F[:], m.h2H[:, i % 2].bitcast(F32), ALU.subtract)\
                      .then_inc(sem.h2_low, 1)
                if rep + 2 < NC:
                    cond_bias(j + 2, rep + 2)
                if within(rep - 2, 0, NC):
                    i = j - 2
                    dve.wait_ge(sem.g_act, j + 1)
                    nc.vector.tensor_scalar(m.coupl_b[:, ds(i * BPC, BPC)], tg, sc(m, m.GMUL), sc(m, m.TENTH),
                                            ALU.mult, ALU.add).then_inc(sem.coupl_b, 1)
                if rep + 2 < NC:
                    cond(j + 2, rep + 2)
                if upd:
                    dve.wait_ge(sem.t0_done, u + 1)
                    dve.wait_ge(sem.t1_done, u + 1)
                    nc.vector.tensor_tensor(m.Y[:, 0, ds(uc * CH, CH)], m.Y[:, 0, ds(uc * CH, CH)], m.t0[:], ALU.add)\
                      .then_inc(sem.y_upd, 1)
                    nc.vector.tensor_tensor(m.Y[:, 1, ds(uc * CH, CH)], m.Y[:, 1, ds(uc * CH, CH)], m.t1[:], ALU.subtract)\
                      .then_inc(sem.y_upd, 1)
                    if rep - 4 < LAST_SPLIT:
                        for h in range(KD):
                            dve.wait_ge(sem.y_upd, 2 * u + 1 + h)
                            nc.vector.tensor_copy(m.YH[:, h, ds(uc * CH, CH)], m.Y[:, h, ds(uc * CH, CH)])\
                              .then_inc(sem.yh_upd, 1)
            for c in range(2):
                cond_bias(c, c)
                cond(c, c)
            segments(dve, CUTS, body)

        @block.gpsimd
        def _(pool):
            def low(c, done, made, at):
                for h in range(KD):
                    pool.wait_ge(made, 2 * at + h + 1)
                    pool.tensor_tensor(m.YL[:, h, ds(c * CH, CH)], m.Y[:, h, ds(c * CH, CH)],
                                       m.YH[:, h, ds(c * CH, CH)].bitcast(F32), ALU.subtract).then_inc(done, 1)

            def body(j, rep):
                upd = within(rep - 4, 0, NITEM)
                u = j - 4
                if upd:
                    uc = u % NC
                    pool.wait_ge(sem.cs_done, u + 1)
                    if rep - 4 >= 1:
                        pool.wait_ge(sem.y_upd, 2 * u)
                    pool.tensor_tensor(m.t1[:], m.cs[:], m.Y[:, 0, ds(uc * CH, CH)], ALU.mult).then_inc(sem.t1_done, 1)
                if within(rep - 2, 0, NITEM):
                    i = j - 2
                    pool.wait_ge(sem.h3_act, i + 1)
                    if rep - 2 >= 2:
                        pool.wait_ge(sem.th_mm, i - 1)
                    slot = apart(pool, i) % 2
                    pool.tensor_tensor(m.h3L[:, slot], m.h3F[:], m.h3H[:, slot].bitcast(F32), ALU.subtract)\
                        .then_inc(sem.h3_low, 1)
                if rep + 2 < NC:
                    low(j + 2, sem.yl_cond, sem.yh_cond, j + 2)
                if upd and rep - 4 < LAST_SPLIT:
                    low(uc, sem.yl_upd, sem.yh_upd, u)
                if upd and rep - 4 >= LAST_SPLIT:
                    for h in range(KD):
                        pool.wait_ge(sem.y_upd, 2 * u + h + 1)
                        x = m.X[:, h, ds(uc * CH, CH)]
                        pool.tensor_tensor(x, x, m.Y[:, h, ds(uc * CH, CH)], ALU.add).then_inc(sem.x1_sum, 1)
            low(0, sem.yl_cond, sem.yh_cond, 0)
            low(1, sem.yl_cond, sem.yh_cond, 1)
            segments(pool, CUTS, body)
            pool.wait_ge(sem.x1_sum, KD * NC)



FF1 = 1024
KF1 = FF1 // P
HS = 512
KS = HS // P


def layer1(nc, m, d, sem):
    W = m.work
    NT = NC * KF1
    place(nc, m, "hid", [P, NT, CH], F32, W)
    place(nc, m, "du", [P, NC, KD, CH], F32, W + 96 * KB)
    w = W + 128 * KB
    place(nc, m, "w_in", [P, KD, FF1], BF16, w)
    place(nc, m, "w_out", [P, KF1, D], F32R, w + 4 * KB)
    place(nc, m, "s1", [P, 64], F32, w + 12 * KB)
    w += 13 * KB
    place(nc, m, "lap", [P, KD, D], F32, W + 32 * KB)
    place(nc, m, "st", [P, KF1, D], F32, W + 34 * KB)
    place(nc, m, "st2", [P, KF1, D], F32, W + 42 * KB)
    place(nc, m, "stq", [P, KF1, D], BF16, W + 50 * KB)
    for i, name in enumerate(("ub", "cb", "db", "ab", "us")):
        place(nc, m, name, [P, 2, CH], F32, W + (54 + 4 * i) * KB)
    place(nc, m, "identb", [P, P], BF16, W + 74 * KB)
    place(nc, m, "mx1", [P, 2 * NC], F32, W + 75 * KB)
    place(nc, m, "nzR", [P, BATCH], F32, W + 76 * KB)
    place(nc, m, "qt", [P, 2, KD, CH], F32, w)
    place(nc, m, "qH", [P, 2, KD, CH], BF16, w + 8 * KB)
    place(nc, m, "qL", [P, 2, KD, CH], BF16, w + 12 * KB)
    place(nc, m, "mx2", [P, NT], F32, w + 16 * KB)
    place(nc, m, "raw_w1", [P, KD, FF1], F32, W)
    place(nc, m, "raw_w2", [P, KF1, D], F32, W + 8 * KB)
    GS = 4
    place(nc, m, "gH", [P, GS, CH], F32R, w)
    place(nc, m, "gL", [P, GS, CH], F32R, w + 8 * KB)
    place(nc, m, "o1", [P, 2, KD, CH], F32, w + 18 * KB)
    s1 = m.s1
    WIN_A, WIN_S, WOUT_A, WOUT_S, DEQ = (slice(8 * i, 8 * i + 8) for i in range(5))
    MX, AMAX, SX, ISX, SH, ISH = (slice(48 + i, 49 + i) for i in range(6))

    def reduce_part(block, ps, mx, scale, inverse, stage):
        mm, v = sem.red_mm[stage - 1], sem.red_v[stage - 1]

        @block.tensor
        def _(pe):
            pe.wait_ge(v, 1)
            nc.tensor.transpose(ps[0:1, 0:P], s1[:, MX], m.ident[:]).then_inc(mm, 1)
            pe.wait_ge(v, 2)
            nc.tensor.matmul(ps[:, P:P + 1], m.ones1[0:1, :], s1[0:1, AMAX], start=True, stop=True).then_inc(mm, 1)

        @block.vector
        def _(dve):
            nc.vector.tensor_reduce(s1[:, MX], mx, AX.X, ALU.max).then_inc(v, 1)
            dve.wait_ge(mm, 1)
            nc.vector.tensor_reduce(s1[0:1, AMAX], ps[0:1, 0:P], AX.X, ALU.max).then_inc(v, 1)
            dve.wait_ge(mm, 2)
            nc.vector.tensor_scalar(s1[:, MX], ps[:, P:P + 1], 1e-8, None, ALU.max).then_inc(v, 1)
            dve.wait_ge(v, 3)
            nc.vector.reciprocal(s1[:, AMAX], s1[:, MX]).then_inc(v, 1)
            dve.wait_ge(v, 4)
            nc.vector.tensor_scalar(s1[:, scale], s1[:, AMAX], 32767.0, None, ALU.mult).then_inc(v, 1)
            dve.wait_ge(v, 5)
            nc.vector.reciprocal(s1[:, inverse], s1[:, scale]).then_inc(v, 1)
            dve.wait_ge(v, 6)
            if stage == 1:
                nc.vector.tensor_scalar(s1[:, DEQ], s1[:, WIN_A], s1[:, inverse], None, ALU.mult).then_inc(v, 1)
                dve.wait_ge(v, 7)

    with nc.Block() as block:
        @block.sync
        def _(sp):
            sp.dma_start(m.st[:], d.w_inT.rearrange("(j p) k -> p j k", p=P)).then_inc(sem.w1_loaded, 16)
            sp.dma_start(m.st2[:], d.w_out.rearrange("(j p) k -> p j k", p=P)).then_inc(sem.w1_loaded, 16)

        @block.vector
        def _(dve):
            nc.vector.tensor_scalar(m.nzR[:], m.zxyz[:, 128:192], -1.0, None, ALU.mult)
            nc.vector.tensor_copy(m.identb[:], m.ident[:])
            nc.vector.memset(m.ones1[:], 1.0).then_inc(sem.l1_const, 1)
            dve.wait_ge(sem.l1_const, 1)

        @block.gpsimd
        def _(pool):
            n = [0]

            def step(i):
                i.then_inc(sem.lap, 1)
                n[0] += 1
                pool.wait_ge(sem.lap, n[0])
            step(pool.memset(m.lap[:], 0.0))
            for k in range(KD):
                for off, v in ((0, -2.0), (1, 1.0), (-1, 1.0)):
                    step(pool.affine_select(out=m.lap[:, k], in_=m.lap[:, k], compare_op=ALU.not_equal, fill=v,
                                            base=k * P - off, pattern=[[-1, D]], channel_multiplier=1))
            step(pool.affine_select(out=m.lap[:, 0, 0:1], in_=m.lap[:, 0, 0:1], compare_op=ALU.not_equal, fill=2.0,
                                    base=-1, pattern=[[0, 1]], channel_multiplier=1))
            step(pool.affine_select(out=m.lap[:, 1, D - 1:D], in_=m.lap[:, 1, D - 1:D], compare_op=ALU.not_equal, fill=2.0,
                                    base=-(P - 2), pattern=[[0, 1]], channel_multiplier=1))

    zX, zY, zR = (m.zxyz[:, ts(i, BATCH)] for i in range(3))

    with nc.psum_tensor("l1_lap", [P, 2, CH], F32) as ps_lap, \
            nc.psum_tensor("l1_wt", [P, 2, 1024], BF16) as ps_w, nc.Block() as block:

        @block.tensor
        def _(pe):
            def body(c, rep):
                for h in range(KD):
                    if rep >= 1:
                        pe.wait_ge(sem.du_a, 2 * c - 1 + h)
                    for k in range(KD):
                        last = nc.tensor.matmul(ps_lap[:, h], m.lap[:, k, ts(h, P)], m.X[:, k, ds(c * CH, CH)],
                                                start=k == 0, stop=k == KD - 1)
                    last.then_inc(sem.lap_mm, 1)
            body(0, 0)
            body(1, 1)
            body(2, 2)
            pe.wait_ge(sem.win_q, 1)
            for g in range(4):
                if g >= 2:
                    pe.wait_ge(sem.win_t, g - 1)
                for i in range(4):
                    j, k = (4 * g + i) // KD, (4 * g + i) % KD
                    last = nc.tensor.transpose(ps_w[:, g % 2, ts(i, P)], m.stq[:, j, ts(k, P)], m.identb[:])
                last.then_inc(sem.win_mm, 1)
            segments(pe, [3, NC], body)

        ACT_BATCHES = (BPC, BPC // 2)

        @block.scalar
        def _(act):
            def body(c, rep):
                for h in range(KD):
                    i = 2 * c + h
                    if rep >= 1:
                        act.wait_ge(sem.du_u, i - 1)
                    at = apart(act, c * CH)
                    nc.scalar.activation(by_batch(m.us[:, h])[:, :, 0:64:63], by_batch(m.X[:, h, ds(at, CH)])[:, :, 1:63:61],
                                         ACT.Identity, scale=2.0).then_inc(sem.us_edge, 1)
                    if rep >= 1:
                        act.wait_ge(sem.du_d, i - 1)
                    at = apart(act, c * BPC)
                    for b in range(ACT_BATCHES[h]):
                        last = nc.scalar.activation(m.cb[:, h, ts(b, SEQ)], m.X[:, h, ds((at + b) * SEQ, SEQ)], ACT.Identity,
                                                    bias=m.zk[:, ds(at + b, 1)], scale=m.nzR[:, ds(at + b, 1)])
                    last.then_inc(sem.du_c, 1)

            def magic(t, s, ready, done):
                act.wait_ge(sem.w1_scale, ready)
                for j in range(KF1):
                    last = nc.scalar.activation(t[:, j], t[:, j], ACT.Identity, bias=m.magic[:], scale=s1[:, s][:, j:j + 1])
                last.then_inc(done, 1)
            body(0, 0)
            magic(m.st, WIN_S, 1, sem.win_m)
            body(1, 1)
            magic(m.st2, WOUT_S, 2, sem.wout_m)
            body(2, 2)
            act.wait_ge(sem.w1_clip, 1)
            nc.scalar.activation(m.stq[:], m.st[:], ACT.Identity, bias=m.nmagic[:]).then_inc(sem.win_q, 1)
            body(3, 3)
            for g in range(4):
                act.wait_ge(sem.win_mm, g + 1)
                for i in range(4):
                    j, k = (4 * g + i) // KD, (4 * g + i) % KD
                    last = nc.scalar.copy(m.w_in[:, k, ts(j, P)], ps_w[:, g % 2, ts(i, P)])
                last.then_inc(sem.win_t, 1)
            body(4, 4)
            act.wait_ge(sem.w1_clip, 2)
            nc.scalar.activation(m.w_out[:], m.st2[:], ACT.Identity, bias=m.nmagic[:]).then_inc(sem.wout_q, 1)
            segments(act, [5, NC], body)
            act.wait_ge(sem.wout_q, 1)

        @block.vector
        def _(dve):
            def weights_scale(n, t, a, s):
                dve.wait_ge(sem.w1_loaded, 32)
                nc.vector.tensor_reduce(s1[:, a], t[:], AX.X, ALU.max, apply_absolute_value=True).then_inc(sem.w1_dve, 1)
                dve.wait_ge(sem.w1_dve, 3 * n + 1)
                nc.vector.tensor_scalar(s1[:, a], s1[:, a], 1e-8, None, ALU.max).then_inc(sem.w1_dve, 1)
                dve.wait_ge(sem.w1_dve, 3 * n + 2)
                nc.vector.reciprocal(s1[:, s], s1[:, a]).then_inc(sem.w1_rec, 1)
                dve.wait_ge(sem.w1_rec, n + 1)
                nc.vector.tensor_scalar(s1[:, s], s1[:, s], 127.0, None, ALU.mult).then_inc(sem.w1_scale, 1)
                dve.wait_ge(sem.w1_scale, n + 1)
                nc.vector.reciprocal(s1[:, a], s1[:, s]).then_inc(sem.w1_dve, 1)

            def clip(done, t):
                dve.wait_ge(done, 1)
                nc.vector.tensor_scalar(t[:], t[:], MAGIC + 127.0, MAGIC - 128.0, ALU.min, ALU.max).then_inc(sem.w1_clip, 1)

            def body(c, rep):
                for h in range(KD):
                    i = 2 * c + h
                    dve.wait_ge(sem.us_mid, i + 1)
                    dve.wait_ge(sem.us_edge, i + 1)
                    nc.vector.tensor_tensor(by_batch(m.ub[:, h]), by_batch(m.us[:, h]), per_batch(zY[:, ds(c * BPC, BPC)]), ALU.mult)\
                      .then_inc(sem.du_u, 1)
                    dve.wait_ge(sem.lap_mm, i + 1)
                    nc.vector.tensor_tensor(by_batch(m.ab[:, h]), by_batch(ps_lap[:, h]), per_batch(zX[:, ds(c * BPC, BPC)]), ALU.mult)\
                      .then_inc(sem.du_a, 1)
                for h in range(KD):
                    i = 2 * c + h
                    dve.wait_ge(sem.du_u, i + 1)
                    dve.wait_ge(sem.du_a, i + 1)
                    nc.vector.tensor_tensor(m.ab[:, h], m.ab[:, h], m.ub[:, h], ALU.add).then_inc(sem.du_b, 1)
                for h in range(KD):
                    i = 2 * c + h
                    dve.wait_ge(sem.du_d, i + 1)
                    dve.wait_ge(sem.du_b, i + 1)
                    nc.vector.tensor_tensor(m.du[:, c, h], m.ab[:, h], m.db[:, h], ALU.add).then_inc(sem.du_done, 1)
                for h in range(KD):
                    i = 2 * c + h
                    dve.wait_ge(sem.du_done, i + 1)
                    i2 = apart(dve, i)
                    nc.vector.tensor_reduce(m.mx1[:, ds(i2, 1)], m.du[:, c, h], AX.X, ALU.max, apply_absolute_value=True)\
                      .then_inc(sem.du_max, 1)
            weights_scale(0, m.st, WIN_A, WIN_S)
            body(0, 0)
            weights_scale(1, m.st2, WOUT_A, WOUT_S)
            body(1, 1)
            clip(sem.win_m, m.st)
            body(2, 2)
            clip(sem.wout_m, m.st2)
            segments(dve, [3, NC], body)
            dve.wait_ge(sem.w1_dve, 6)

        @block.gpsimd
        def _(pool):
            def body(c, rep):
                for h in range(KD):
                    i = 2 * c + h
                    if rep >= 1:
                        pool.wait_ge(sem.du_u, i - 1)
                    at = apart(pool, c * CH)
                    x = by_batch(m.X[:, h, ds(at, CH)])
                    pool.tensor_tensor(by_batch(m.us[:, h])[:, :, 1:63], x[:, :, 0:62], x[:, :, 2:64], ALU.add).then_inc(sem.us_mid, 1)
                b0 = ACT_BATCHES[1]
                own = slice(b0 * SEQ, CH)
                batches = ds(c * BPC + b0, BPC - b0)
                if rep >= 1:
                    pool.wait_ge(sem.du_d, 2 * c)
                pool.tensor_tensor(by_batch(m.cb[:, 1, own]), by_batch(m.X[:, 1, ds(c * CH + b0 * SEQ, CH - b0 * SEQ)]),
                                   per_batch(m.nzR[:, batches], BPC - b0), ALU.mult).then_inc(sem.du_c_pool, 1)
                pool.wait_ge(sem.du_c_pool, 2 * c + 1)
                pool.tensor_tensor(by_batch(m.cb[:, 1, own]), by_batch(m.cb[:, 1, own]), per_batch(m.zk[:, batches], BPC - b0),
                                   ALU.add).then_inc(sem.du_c_pool, 1)
                for h in range(KD):
                    i = 2 * c + h
                    if rep >= 1:
                        pool.wait_ge(sem.du_done, i - 1)
                    pool.wait_ge(sem.du_c, i + 1)
                    if h == 1:
                        pool.wait_ge(sem.du_c_pool, 2 * c + 2)
                    pool.tensor_tensor(m.db[:, h], m.cb[:, h], m.X[:, h, ds(c * CH, CH)], ALU.mult).then_inc(sem.du_d, 1)
            segments(pool, range(NC + 1), body)

    with nc.psum_tensor("l1_red", [P, CH], F32) as ps, nc.Block() as block:
        reduce_part(block, ps, m.mx1[:], SX, ISX, 1)

    with nc.psum_tensor("l1_h", [P, KF1, CH], F32) as ps_h, nc.Block() as block:

        @block.tensor
        def _(pe):
            def body(c, rep):
                pe.wait_ge(sem.q_done, 2 * c + 2)
                for j in range(KF1):
                    t = c * KF1 + j
                    if rep >= 1:
                        pe.wait_ge(sem.hid_act, t - KF1 + 1)
                    for k in range(KD):
                        for n, q in enumerate((m.qH, m.qL)):
                            last = nc.tensor.matmul(ps_h[:, j], m.w_in[:, k, ts(j, P)], q[:, c % 2, k],
                                                    start=k == 0 and n == 0, stop=k == KD - 1 and n == 1)
                    last.then_inc(sem.hid_mm, 1)
            segments(pe, [0, 1, NC], body)

        @block.scalar
        def _(act):
            def high(c, rep):
                for h in range(KD):
                    act.wait_ge(sem.q_int, 2 * c + h + 1)
                    if rep >= 2:
                        act.wait_ge(sem.hid_mm, (c - 1) * KF1)
                    nc.scalar.copy(m.qH[:, c % 2, h], m.qt[:, c % 2, h]).then_inc(sem.q_high, 1)

            def body(c, rep):
                for j in range(KF1):
                    t = c * KF1 + j
                    if j == 3 and rep + 1 < NC:
                        high(c + 1, rep + 1)
                    act.wait_ge(sem.hid_mm, t + 1)
                    t = apart(act, t)
                    nc.scalar.activation(m.hid[:, t], ps_h[:, j], ACT.Gelu, bias=bias(m, "b_in", j),
                                         scale=s1[:, DEQ][:, j:j + 1]).then_inc(sem.hid_act, 1)
            high(0, 0)
            segments(act, range(NC + 1), body)

        @block.gpsimd
        def _(pool):
            def body(c, rep):
                for h in range(KD):
                    i = 2 * c + h
                    pool.wait_ge(sem.q_high, i + 1)
                    pool.tensor_tensor(m.qL[:, c % 2, h], m.qt[:, c % 2, h], m.qH[:, c % 2, h], ALU.subtract).then_inc(sem.q_done, 1)
            segments(pool, [0, NC], body)

        @block.vector
        def _(dve):
            def quantize(c, rep):
                for h in range(KD):
                    i = 2 * c + h
                    if rep >= 2:
                        dve.wait_ge(sem.q_done, i - 3)
                    nc.vector.tensor_scalar(m.qt[:, c % 2, h], m.du[:, c, h], s1[:, SX], MAGIC, ALU.mult, ALU.add).then_inc(sem.q_dve, 1)
                for h in range(KD):
                    i = 2 * c + h
                    t = m.qt[:, c % 2, h]
                    dve.wait_ge(sem.q_dve, 4 * c + h + 1)
                    nc.vector.tensor_scalar(t, t, MAGIC + 32767.0, MAGIC - 32768.0, ALU.min, ALU.max).then_inc(sem.q_dve, 1)
                for h in range(KD):
                    i = 2 * c + h
                    t = m.qt[:, c % 2, h]
                    dve.wait_ge(sem.q_dve, 4 * c + h + 3)
                    nc.vector.tensor_scalar(t, t, MAGIC, None, ALU.subtract).then_inc(sem.q_int, 1)

            def body(c, rep):
                if rep + 1 < NC:
                    quantize(c + 1, rep + 1)
                for j in range(KF1):
                    t = c * KF1 + j
                    dve.wait_ge(sem.hid_act, t + 1)
                    t = apart(dve, t)
                    nc.vector.tensor_reduce(m.mx2[:, ds(t, 1)], m.hid[:, t], AX.X, ALU.max, apply_absolute_value=True)\
                      .then_inc(sem.hid_max, 1)
            quantize(0, 0)
            segments(dve, [0, 1, NC - 1, NC], body)
            dve.wait_ge(sem.hid_max, NT)

    with nc.psum_tensor("l1_red2", [P, CH], F32) as ps, nc.Block() as block:
        reduce_part(block, ps, m.mx2[:], SH, ISH, 2)

    with nc.psum_tensor("l1_o", [P, 2, KD, CH], F32) as ps_o, nc.Block() as block:
        AHEAD = 4

        @block.sync
        def _(sp):
            sp.wait_ge(sem.g_mm1, KF1)
            sp.dma_start(m.raw_w1[:], d.f2_w1.rearrange("(k p) n -> p k n", p=P)).then_inc(sem.raw_loaded, 16)
            sp.dma_start(m.raw_w2[:], d.f2_w2.rearrange("(k p) n -> p k n", p=P)).then_inc(sem.raw_loaded, 16)
            sp.wait_ge(sem.raw_loaded, 32)

        @block.scalar
        def _(act):
            def magic(t):
                nc.scalar.activation(m.hid[:, t], m.hid[:, t], ACT.Identity, bias=m.magic[:], scale=s1[:, SH])\
                  .then_inc(sem.g_round, 1)

            def result(c, rep):
                act.wait_ge(sem.g_mm1, KF1 * (c + 1))
                for h in range(KD):
                    if rep >= 2:
                        act.wait_ge(sem.x2_sum, 2 * c - 3 + h)
                    nc.scalar.activation(m.o1[:, c % 2, h], ps_o[:, c % 2, h], ACT.Identity, bias=bias(m, "b_out", h),
                                         scale=s1[:, ISH]).then_inc(sem.o1_act, 1)

            def body(c, rep):
                for k in range(KF1):
                    t = c * KF1 + k
                    if k % 2 == 0 and (rep < NC - 1 or k + AHEAD < KF1):
                        magic(t + AHEAD)
                    if rep >= 1 or k >= GS:
                        act.wait_ge(sem.g_mm1, t - GS + 1)
                    act.wait_ge(sem.g_scaled, t + 1)
                    t = apart(act, t)
                    nc.scalar.activation(m.gH[:, k % GS], m.hid[:, t], ACT.Identity).then_inc(sem.g_high, 1)
                    if rep >= 1 and k == 2:
                        result(c - 1, rep - 1)
            for t in range(0, AHEAD, 2):
                magic(t)
            segments(act, range(NC + 1), body)
            result(NC - 1, NC - 1)

        POOL_LOWS, DVE_LOWS = (0, 1, 3, 5, 7), (2, 4, 6)

        def low(eng, t, k, used, done):
            eng.wait_ge(sem.g_high, t + 1)
            if used:
                eng.wait_ge(sem.g_mm1, t - GS + 1)
            t = apart(eng, t)
            eng.tensor_tensor(m.gL[:, k % GS], m.hid[:, t], m.gH[:, k % GS].bitcast(F32), ALU.subtract).then_inc(done, 1)

        @block.gpsimd
        def _(pool):
            def result(c, rep):
                for h in range(KD):
                    pool.wait_ge(sem.o1_act, 2 * c + h + 1)
                    at = apart(pool, c * CH)
                    x = m.X[:, h, ds(at, CH)]
                    pool.tensor_tensor(x, x, m.o1[:, c % 2, h], ALU.add).then_inc(sem.x2_sum, 1)

            def body(c, rep):
                for k in POOL_LOWS:
                    low(pool, c * KF1 + k, k, rep >= 1 or k >= GS, sem.g_low_pool)
                    if rep >= 1 and k == 3:
                        result(c - 1, rep - 1)
            segments(pool, [0, 1, NC], body)
            result(NC - 1, NC - 1)

        @block.vector
        def _(dve):
            def odd(c, k):
                t = c * KF1 + k
                nc.vector.tensor_scalar(m.hid[:, t], m.hid[:, t], s1[:, SH], MAGIC, ALU.mult, ALU.add).then_inc(sem.g_round_odd, 1)

            def clip(c, k):
                t = c * KF1 + k
                if k % 2:
                    dve.wait_ge(sem.g_round_odd, c * (KF1 // 2) + k // 2 + 1)
                else:
                    dve.wait_ge(sem.g_round, c * (KF1 // 2) + k // 2 + 1)
                nc.vector.tensor_scalar(m.hid[:, t], m.hid[:, t], MAGIC + 32767.0, MAGIC - 32768.0, ALU.min, ALU.max)\
                  .then_inc(sem.g_clip, 1)

            def body(c, rep):
                for k in range(KF1):
                    t = c * KF1 + k
                    if k % 2 == 1 and (rep < NC - 1 or k + 2 < KF1):
                        odd(c + (k + 2) // KF1, (k + 2) % KF1)
                    if rep < NC - 1 or k < KF1 - 1:
                        clip(c + (k + 1) // KF1, (k + 1) % KF1)
                    dve.wait_ge(sem.g_clip, t + 1)
                    nc.vector.tensor_scalar(m.hid[:, t], m.hid[:, t], MAGIC, s1[:, WOUT_A][:, k:k + 1], ALU.subtract, ALU.mult)\
                      .then_inc(sem.g_scaled, 1)
                    if k - 1 in DVE_LOWS:
                        low(dve, t - 1, k - 1, rep >= 1 or k - 1 >= GS, sem.g_low)
            odd(0, 1)
            clip(0, 0)
            segments(dve, [0, 1, NC - 1, NC], body)

        @block.tensor
        def _(pe):
            def body(c, rep):
                if rep >= 2:
                    pe.wait_ge(sem.o1_act, 2 * c - 2)
                for k in range(KF1):
                    t = c * KF1 + k
                    if k in POOL_LOWS:
                        pe.wait_ge(sem.g_low_pool, c * len(POOL_LOWS) + POOL_LOWS.index(k) + 1)
                    else:
                        pe.wait_ge(sem.g_low, c * len(DVE_LOWS) + DVE_LOWS.index(k) + 1)
                    for h in range(KD):
                        for n, g in enumerate((m.gH, m.gL)):
                            last = nc.tensor.matmul(ps_o[:, c % 2, h], m.w_out[:, k, ts(h, P)], g[:, k % GS],
                                                    start=k == 0 and n == 0, stop=k == KF1 - 1 and n == 1)
                    last.then_inc(sem.g_mm1, 1)
            segments(pe, [0, 1, 2, NC], body)


def layer2(nc, m, d, sem):
    W = m.work
    for i, name in enumerate(("f2w1H", "f2w1L")):
        place(nc, m, name, [P, KD, FF1], F32R, W + (16 + 8 * i) * KB)
    for i, name in enumerate(("f2w2H", "f2w2L")):
        place(nc, m, name, [P, KF1, D], F32R, W + (32 + 8 * i) * KB)
    for name, shape, at in (("c3w1H", [KD, FF1], 48), ("c3w1L", [KD, FF1], 56), ("sw1H", [KD, HS], 64), ("sw1L", [KD, HS], 68),
                            ("sw2H", [KS, D], 72), ("sw2L", [KS, D], 76)):
        place(nc, m, name, [P] + shape, F32R, W + at * KB)
    place(nc, m, "wstage", [P, 2, 1024], F32, W)
    place(nc, m, "cw2", [P, BPC, KD, D], F32, W + 80 * KB)
    place(nc, m, "xs", [P, KD, CH], F32, W + 96 * KB)
    place(nc, m, "y2t", [P, PAIRS, D], F32, W + 100 * KB)
    place(nc, m, "y2F", [P, KD, CH], F32, W + 104 * KB)
    place(nc, m, "y2H", [P, 2, KD, CH], F32R, W + 108 * KB)
    place(nc, m, "y2L", [P, 2, KD, CH], F32R, W + 116 * KB)
    place(nc, m, "f2hF", [P, 4, CH], F32, W + 124 * KB)
    place(nc, m, "f2hH", [P, KF1, CH], F32R, W + 132 * KB)
    place(nc, m, "f2hL", [P, KF1, CH], F32R, W + 148 * KB)
    w1, w2 = (m.f2w1H, m.f2w1L), (m.f2w2H, m.f2w2L)

    with nc.psum_tensor("l2_tok", [P, CH], F32) as ps_tok, nc.psum_tensor("l2_turn", [P, CH], F32) as ps_turn, \
            nc.psum_tensor("l2_h", [P, 4, CH], F32) as ps_h, nc.psum_tensor("l2_o", [P, KD, CH], F32) as ps_o, \
            nc.Block() as block:

        @block.sync
        def _(sp):
            def body(c, rep):
                for b in range(BPC):
                    i = sp.value_load(m.ids2[0:1, ds(c * BPC + b, 1)], min_val=0, max_val=31)
                    if rep >= 1:
                        sp.wait_ge(sem.tok2_mm, (c - 1) * PAIRS + b // 2 + 1)
                    i = apart(sp, i)
                    sp.dma_start(m.cw2[:, b], d.c2_w[ds(i, 1)].rearrange("e (k p) o -> p (e k) o", p=P))\
                      .then_inc(sem.cw2_loaded[b], 16)
            segments(sp, [0, 1, NC], body)

        @block.tensor
        def _(pe):
            def cond(c, rep):
                pe.wait_ge(sem.xs_copied, c + 1)
                banks = (ps_tok[:], ps_o[:, 0], ps_o[:, 1], ps_tok[:])
                if rep >= 1:
                    pe.wait_ge(sem.y2_added, 2 * c)
                for q in range(PAIRS):
                    if rep >= 2 and q == 1:
                        pe.wait_ge(sem.x3_sum, 2 * (c - 1))
                    if q == 3:
                        pe.wait_ge(sem.tok2_act, c * PAIRS + 1)
                    for b in (2 * q, 2 * q + 1):
                        pe.wait_ge(sem.cw2_loaded[b], 16 * (c + 1))
                        for k in range(KD):
                            last = nc.tensor.matmul(banks[q][ts(b % 2, SEQ), 0:D], m.xs[:, k, ts(b, SEQ)], m.cw2[:, b, k],
                                                    start=k == 0, stop=k == KD - 1)
                    last.then_inc(sem.tok2_mm, 1)
                pe.wait_ge(sem.tok2_act, (c + 1) * PAIRS)
                for h in range(KD):
                    for q in range(PAIRS):
                        last = nc.tensor.transpose((ps_turn, ps_tok)[h][:, ts(q, P)], m.y2t[:, q, ts(h, P)], m.ident[:])
                    last.then_inc(sem.turn2_mm, 1)

            def body(c, rep):
                pe.wait_ge(sem.y2_low, 2 * c + 2)
                for j in range(KF1):
                    if rep >= 1 or j >= 4:
                        pe.wait_ge(sem.h2a_act, c * KF1 + j - 3)
                    for k in range(KD):
                        last = products(nc, ps_h[:, j % 4], [w[:, k, ts(j, P)] for w in w1],
                                        [y[:, c % 2, k] for y in (m.y2H, m.y2L)], k == 0, k == KD - 1)
                    last.then_inc(sem.h2a_mm, 1)
                if rep + 1 < NC:
                    cond(c + 1, rep + 1)
                if rep == 0:
                    pe.wait_ge(sem.w2_low_pool, 1)
                if rep >= 1:
                    pe.wait_ge(sem.x3_sum, 2 * c)
                for k in range(KF1):
                    pe.wait_ge(sem.h2a_low, c * KF1 + k + 1)
                    for h in range(KD):
                        last = products(nc, ps_o[:, h], [w[:, k, ts(h, P)] for w in w2],
                                        (m.f2hH[:, k], m.f2hL[:, k]), k == 0, k == KF1 - 1)
                    last.then_inc(sem.o2_mm, 1)
            cond(0, 0)
            pe.wait_ge(sem.w2_low, 1)
            segments(pe, [0, 1, NC - 1, NC], body)

        @block.scalar
        def _(act):
            def cond(c, rep):
                for q in range(PAIRS):
                    act.wait_ge(sem.tok2_mm, c * PAIRS + q + 1)
                    if rep >= 1:
                        act.wait_ge(sem.turn2_mm, 2 * c)
                    nc.scalar.copy(m.y2t[:, q], (ps_tok[:, 0:D], ps_o[:, 0, 0:D], ps_o[:, 1, 0:D], ps_tok[:, 0:D])[q]).then_inc(sem.tok2_act, 1)

            def body(c, rep):
                for j in range(KF1):
                    act.wait_ge(sem.h2a_mm, c * KF1 + j + 1)
                    if rep >= 1:
                        act.wait_ge(sem.o2_mm, (c - 1) * KF1 + j + 1)
                    if rep >= 1 or j >= 4:
                        act.wait_ge(sem.h2a_low, c * KF1 + j - 3)
                    nc.scalar.activation(m.f2hH[:, j], ps_h[:, j % 4], ACT.Relu, bias=bias(m, "f2_b1", j))
                    nc.scalar.activation(m.f2hF[:, j % 4], ps_h[:, j % 4], ACT.Relu, bias=bias(m, "f2_b1", j))\
                      .then_inc(sem.h2a_act, 1)
                if rep + 1 < NC:
                    cond(c + 1, rep + 1)
            nc.scalar.copy(m.f2w1H[:], m.raw_w1[:]).then_inc(sem.w2_high, 1)
            cond(0, 0)
            segments(act, [0, 1, NC - 1, NC], body)

        @block.vector
        def _(dve):
            def copy_x(c, rep):
                if rep >= 1:
                    dve.wait_ge(sem.tok2_mm, c * PAIRS)
                c = apart(dve, c)
                nc.vector.tensor_copy(m.xs[:], m.X[:, :, ds(c * CH, CH)]).then_inc(sem.xs_copied, 1)

            def cond(c, rep):
                for h in range(KD):
                    i = 2 * c + h
                    dve.wait_ge(sem.turn2_mm, i + 1)
                    if rep >= 1:
                        dve.wait_ge(sem.y2_low, i - 1)
                    if rep >= 2:
                        dve.wait_ge(sem.h2a_mm, (c - 1) * KF1)
                    nc.vector.tensor_tensor(by_batch(m.y2F[:, h]), by_batch((ps_turn, ps_tok)[h][:]),
                                            per_batch(m.cond2[:, ds(h * BATCH + c * BPC, BPC)]), ALU.add)\
                      .then_inc(sem.y2_added, 1)
                for h in range(KD):
                    dve.wait_ge(sem.y2_added, 2 * c + h + 1)
                    nc.vector.tensor_copy(m.y2H[:, c % 2, h], m.y2F[:, h]).then_inc(sem.y2_high, 1)
                for h in range(KD):
                    dve.wait_ge(sem.y2_high, 2 * c + h + 1)
                    nc.vector.tensor_tensor(m.y2L[:, c % 2, h], m.y2F[:, h], m.y2H[:, c % 2, h].bitcast(F32), ALU.subtract)\
                      .then_inc(sem.y2_low, 1)

            def result(c, rep):
                dve.wait_ge(sem.o2_mm, KF1 * (c + 1))
                for h in range(KD):
                    x = m.X[:, h, ds(c * CH, CH)]
                    nc.vector.scalar_tensor_tensor(x, ps_o[:, h], bias(m, "f2_b2", h), x, ALU.add, ALU.add)\
                      .then_inc(sem.x3_sum, 1)

            def body(c, rep):
                if rep + 1 < NC:
                    copy_x(c + 1, rep + 1)
                if rep >= 1:
                    result(c - 1, rep - 1)
                for j in range(KF1):
                    dve.wait_ge(sem.h2a_act, c * KF1 + j + 1)
                    nc.vector.tensor_tensor(m.f2hL[:, j], m.f2hF[:, j % 4], m.f2hH[:, j].bitcast(F32), ALU.subtract)\
                      .then_inc(sem.h2a_low, 1)
                if rep + 1 < NC:
                    cond(c + 1, rep + 1)
            copy_x(0, 0)
            dve.wait_ge(sem.w2_high, 1)
            nc.vector.tensor_tensor(m.f2w1L[:], m.raw_w1[:], m.f2w1H[:].bitcast(F32), ALU.subtract).then_inc(sem.w2_low, 1)
            cond(0, 0)
            segments(dve, [0, 1, NC - 1, NC], body)
            result(NC - 1, NC - 1)
            dve.wait_ge(sem.x3_sum, 2 * NC)

        @block.gpsimd
        def _(pool):
            pool.tensor_copy(m.f2w2H[:], m.raw_w2[:]).then_inc(sem.w2_high_pool, 1)
            pool.wait_ge(sem.w2_high_pool, 1)
            pool.tensor_tensor(m.f2w2L[:], m.raw_w2[:], m.f2w2H[:].bitcast(F32), ALU.subtract).then_inc(sem.w2_low_pool, 1)
            pool.wait_ge(sem.w2_low, 1)
            first = d.c3_w1.rearrange("(k p) n -> p k n", p=P)
            pieces = [(first[:, k], m.c3w1H[:, k], m.c3w1L[:, k], None) for k in range(KD)]
            pieces.append((d.sw1.rearrange("(k p) n -> p k n", p=P), m.sw1H[:], m.sw1L[:], KD))
            pieces.append((d.sw2.rearrange("(k p) n -> p k n", p=P), m.sw2H[:], m.sw2L[:], KS))

            def stage(i):
                k = pieces[i][3]
                return m.wstage[:, i % 2] if k is None else m.wstage[:, i % 2].rearrange("p (k n) -> p k n", k=k)

            def load(i):
                if i >= 2:
                    pool.wait_ge(sem.w3_low, i - 1)
                pool.dma_start(stage(i), pieces[i][0]).then_inc(sem.w3_loaded[i % 2], 16)
            load(0)
            for i, (src, high, low, _) in enumerate(pieces):
                if i + 1 < len(pieces):
                    load(i + 1)
                pool.wait_ge(sem.w3_loaded[i % 2], 16 * (i // 2 + 1))
                pool.tensor_copy(high, stage(i)).then_inc(sem.w3_high, 1)
                pool.wait_ge(sem.w3_high, i + 1)
                pool.tensor_tensor(low, stage(i), high.bitcast(F32), ALU.subtract).then_inc(sem.w3_low, 1)
            pool.wait_ge(sem.w3_low, len(pieces))


NE = 8
PART = 64
NTILE = T // P


N1, NW = KD * HS, KD * HS + KS * D
REGION = T + P
NSLOT = T * 2 // P + NE
SPARE = NE * REGION


def scatter(nc, pool, m, sem, z_rows, c):
    pool.wait_ge(sem.pos_done, c + 1)
    pool.wait_ge(sem.zt_act, 2 * (c + 1))
    for q in range(PAIRS):
        for k in range(2):
            pool.indirect_dma_start(z_rows, bass.IndirectOffsetOnAxis(ap=m.posc[:, q, k:k + 1], axis=0),
                                    m.zt[:, q], None).then_inc(sem.scattered, 16)


def layer3_shared(nc, m, d, sem, z_rows):
    W = m.work
    for name, shape, at in (("w2H", [2, KF1, D], 0), ("w2L", [2, KF1, D], 16), ("h3aH", [KF1, CH], 80),
                            ("h3aL", [KF1, CH], 96), ("x3H", [2, KD, CH], 112), ("x3L", [2, KD, CH], 120),
                            ("zH", [KD, CH], 132), ("zL", [KD, CH], 136), ("shH", [KS, CH], 140), ("shL", [KS, CH], 148)):
        place(nc, m, name, [P] + shape, F32R, W + at * KB)
    place(nc, m, "we", [P, 2, KF1, PART], F32, W + 32 * KB)
    place(nc, m, "h3aF", [P, 4, CH], F32, W + 36 * KB)
    place(nc, m, "ye", [SEQ, 2, 2, D], F32, W + 44 * KB)
    place(nc, m, "zF", [P, KD, CH], F32, W + 128 * KB)
    place(nc, m, "raw3", [P, KF1, D - PART], F32, W + 140 * KB)
    place(nc, m, "ew0", [P, NW], F32, W + 112 * KB)
    place(nc, m, "logits", [P, NTILE, NE], F32, W + 160 * KB)
    place(nc, m, "rw", [P, KD, NE], F32, W + 161 * KB)
    place(nc, m, "rb", [P, NE], F32, W + 161 * KB + 512)
    place(nc, m, "hot_a", [P, NTILE, NE], F32, W + 162 * KB)
    place(nc, m, "hot_b", [P, NTILE, NE], F32, W + 163 * KB)
    place(nc, m, "zt", [P, PAIRS, D], F32, W + 164 * KB)
    place(nc, m, "before", [P, P], F32, W + 168 * KB)
    place(nc, m, "pos", [P, NTILE, 2], I32, W + 168 * KB + 512)
    at = W + 168 * KB + 768
    for name, shape, dt in (("free_row", [NE], F32), ("rank8", [NE], F32), ("rank8i", [NE], I32), ("posc", [PAIRS, 2], I32),
                            ("posf", [PAIRS, 2], F32), ("lgc", [PAIRS, NE], F32), ("hac", [PAIRS, NE], F32),
                            ("hbc", [PAIRS, NE], F32), ("hsum", [PAIRS, NE], F32), ("rowc", [PAIRS, NE], F32),
                            ("rtmp", [PAIRS, NE], F32), ("rmax", [PAIRS, 1], F32), ("base_i", [NE], I32)):
        place(nc, m, name, [P] + shape, dt, at)
        at += max(32, 4 * shape[0] * (shape[1] if len(shape) > 1 else 1))
    place(nc, m, "pw", [P, NTILE, 2], F32, at)
    at += 256
    assert at <= 207 * KB + 768
    w1, w2, sw1, sw2 = (m.c3w1H, m.c3w1L), (m.w2H, m.w2L), (m.sw1H, m.sw1L), (m.sw2H, m.sw2L)
    SHARED = D - PART
    CUTS = [0, 1, 2, NC - 1, NC, NC + 1]
    STEPS, RANKS_READ = 25, 20
    with nc.psum_tensor("l3_h", [P, 4, CH], F32) as ps_h, nc.psum_tensor("l3_o", [P, KD, CH], F32) as ps_o, \
            nc.psum_tensor("l3_e", [P, 2, CH], F32) as ps_e, \
            nc.Block() as block:

        @block.sync
        def _(sp):
            sp.dma_start(m.raw3[:], d.c3_w2.rearrange("(k p) n -> p k n", p=P)).then_inc(sem.raw3_loaded, 16)
            sp.dma_start(m.rw[:], d.rw.rearrange("(k p) n -> p k n", p=P)).then_inc(sem.r_loaded, 16)
            sp.dma_start(m.rb[:], d.rb.partition_broadcast(P)).then_inc(sem.r_loaded, 16)

            def body(c, rep):
                for b in range(BPC):
                    i = sp.value_load(m.ids0[0:1, ds(c * BPC + b, 1)], min_val=0, max_val=7)
                    if rep >= 1 or b >= 2:
                        sp.wait_ge(sem.we_low, c * BPC + b - 1)
                    i = apart(sp, i)
                    sp.dma_start(m.we[:, b % 2], d.we[ds(i, 1)].rearrange("e (k p) o -> p (e k) o", p=P))\
                      .then_inc(sem.we_loaded[b % 2], 16)
            segments(sp, [0, 1, NC], body)
            sp.wait_ge(sem.h3a_mm, NC * KF1)
            sp.dma_start(m.ew0[:, 0:N1].rearrange("p (k n) -> p k n", k=KD), d.ew1[0].rearrange("(k p) n -> p k n", p=P))\
              .then_inc(sem.ew0_loaded, 16)
            sp.dma_start(m.ew0[:, N1:NW].rearrange("p (k n) -> p k n", k=KS), d.ew2[0].rearrange("(k p) n -> p k n", p=P))\
              .then_inc(sem.ew0_loaded, 16)

        @block.tensor
        def _(pe):
            def body(c, rep):
                main, shared = rep < NC, rep >= 1
                if main:
                    pe.wait_ge(sem.x3_low, 2 * c + 2)
                    for j in range(KF1):
                        if j < 4:
                            if rep == 1:
                                pe.wait_ge(sem.h3a_act, KF1)
                            elif rep >= 2 and j < 2:
                                pe.wait_ge(sem.x4_sum, 2 * (c - 1))
                            elif rep >= 2:
                                pe.wait_ge(sem.sh_act, KS * (c - 1))
                        else:
                            pe.wait_ge(sem.h3a_act, c * KF1 + j - 3)
                        for k in range(KD):
                            last = products(nc, ps_h[:, j % 4], [w[:, k, ts(j, P)] for w in w1],
                                            [x[:, c % 2, k] for x in (m.x3H, m.x3L)], k == 0, k == KD - 1)
                        last.then_inc(sem.h3a_mm, 1)
                if shared:
                    pe.wait_ge(sem.z_low, 2 * c)
                    if not main:
                        pe.wait_ge(sem.x4_sum, 2 * (NC - 1))
                        pe.wait_ge(sem.sh_act, KS * (NC - 1))
                    for j in range(KS):
                        if main:
                            pe.wait_ge(sem.h3a_act, c * KF1 + j + 5)
                        for k in range(KD):
                            last = products(nc, ps_h[:, j], [w[:, k, ts(j, P)] for w in sw1],
                                            (m.zH[:, k], m.zL[:, k]), k == 0, k == KD - 1)
                        last.then_inc(sem.sh_mm, 1)
                    if rep == 1:
                        pe.wait_ge(sem.r_loaded, 32)
                        pe.wait_ge(sem.before_done, 2)
                    pe.wait_ge(sem.ye_act, PAIRS * c)
                    for q in range(PAIRS):
                        for k in range(KD):
                            last = nc.tensor.matmul(ps_e[:, 0, ts(q, NE)], m.zF[:, k, ts(q, P)], m.rw[:, k],
                                                    start=k == 0, stop=k == KD - 1)
                    last.then_inc(sem.r_mm, 1)
                    for g in range(2):
                        for q in range(2):
                            for h in range(KD):
                                last = nc.tensor.transpose(ps_o[:, g, ts(q * KD + h, P)], m.zF[:, h, ts(2 * g + q, P)], m.ident[:])
                        last.then_inc(sem.zt_mm, 1)
                if main:
                    if rep >= 1:
                        pe.wait_ge(sem.rt_step, (c - 1) * STEPS + 1)
                    batches(c, rep, 0)
                if shared:
                    pe.wait_ge(sem.hot_done, c)
                    nc.tensor.matmul(ps_e[:, 1, 0:32], m.before[:], m.hsum[:].rearrange("p q e -> p (q e)"), start=True, stop=True)
                    nc.tensor.matmul(ps_e[:, 1, 32:64], m.ones1[:], m.hsum[:].rearrange("p q e -> p (q e)"), start=True, stop=True)\
                      .then_inc(sem.rank_mm, 1)
                    second(c, main, 0)
                if main:
                    if not shared:
                        pe.wait_ge(sem.ye_act, 1)
                    turn(c, 0)
                    if shared:
                        pe.wait_ge(sem.rt_step, (c - 1) * STEPS + RANKS_READ)
                    batches(c, rep, 1)
                    batches(c, rep, 2)
                    turn(c, 1)
                    batches(c, rep, 3)
                    turn(c, 2)
                if shared:
                    second(c, main, 1)
                if main:
                    if not shared:
                        pe.wait_ge(sem.ye_act, PAIRS)
                    turn(c, 3)

            def batches(c, rep, q):
                if q >= 2:
                    pe.wait_ge(sem.ye_act, c * PAIRS + q - 1)
                for b in (2 * q, 2 * q + 1):
                    if b % 2 == 1 and q >= 2:
                        pe.wait_ge(sem.ye_act, c * PAIRS + q)
                    if rep == 0 and b < 2:
                        pe.wait_ge(sem.raw_low, b + 1)
                    pe.wait_ge(sem.we_low, c * BPC + b + 1)
                    for k in range(KF1):
                        if b == 0:
                            pe.wait_ge(sem.h3a_low, c * KF1 + k + 1)
                        last = products(nc, ps_e[0:SEQ, q % 2, ts(b % 2, D)], [h[:, k, ts(b, SEQ)] for h in (m.h3aH, m.h3aL)],
                                        [w[:, b % 2, k] for w in w2], k == 0, k == KF1 - 1)
                    last.then_inc(sem.e_mm, 1)

            def second(c, main, h):
                for k in range(KS):
                    pe.wait_ge(sem.sh_low, KS * (c - 1) + k + 1)
                    if main and k == KS - 1:
                        if h == 0:
                            pe.wait_ge(sem.zt_act, 2 * c)
                        pe.wait_ge(sem.ye_act, c * PAIRS + 3 * h + 1)
                    last = products(nc, ps_h[:, h], [w[:, k, ts(h, P)] for w in sw2],
                                    (m.shH[:, k], m.shL[:, k]), k == 0, k == KS - 1)
                last.then_inc(sem.s2_mm, 1)

            def turn(c, q):
                for h in range(KD):
                    for b in range(2):
                        last = nc.tensor.transpose(ps_o[:, h, ts(2 * q + b, SEQ)], m.ye[:, q % 2, b, ts(h, P)], m.ident[0:SEQ, 0:SEQ])
                last.then_inc(sem.t3_mm, 1)
            segments(pe, CUTS, body)

        @block.scalar
        def _(act):
            def body(c, rep):
                main, shared = rep < NC, rep >= 1
                if main:
                    for j in range(KF1):
                        act.wait_ge(sem.h3a_mm, c * KF1 + j + 1)
                        if rep >= 1:
                            act.wait_ge(sem.e_mm, c * BPC)
                        if j >= 4:
                            act.wait_ge(sem.h3a_low, c * KF1 + j - 3)
                        elif rep >= 2:
                            act.wait_ge(sem.sh_low, KS * (c - 1))
                        elif rep == 1:
                            act.wait_ge(sem.h3a_low, KF1)
                        nc.scalar.activation(m.h3aH[:, j], ps_h[:, j % 4], ACT.Gelu, bias=bias(m, "c3_b1", j))
                        nc.scalar.activation(m.h3aF[:, j % 4], ps_h[:, j % 4], ACT.Gelu, bias=bias(m, "c3_b1", j))\
                          .then_inc(sem.h3a_act, 1)
                if shared:
                    for j in range(KS):
                        act.wait_ge(sem.sh_mm, KS * (c - 1) + j + 1)
                        if rep >= 2:
                            act.wait_ge(sem.s2_mm, 2 * (c - 1))
                        if main:
                            act.wait_ge(sem.h3a_low, c * KF1 + j + 5)
                        else:
                            act.wait_ge(sem.sh_low, KS * (NC - 1))
                        nc.scalar.activation(m.shH[:, j], ps_h[:, j], ACT.Gelu, bias=bias(m, "sb1", j))
                        nc.scalar.activation(m.h3aF[:, j], ps_h[:, j], ACT.Gelu, bias=bias(m, "sb1", j))\
                          .then_inc(sem.sh_act, 1)
                    for g in range(2):
                        act.wait_ge(sem.zt_mm, 2 * (c - 1) + g + 1)
                        if rep >= 2:
                            act.wait_ge(sem.scattered, 128 * (c - 1))
                        nc.scalar.copy(m.zt[:, 2 * g:2 * g + 2].rearrange("p q n -> p (q n)"), ps_o[:, g]).then_inc(sem.zt_act, 1)
                if main:
                    for q in range(PAIRS):
                        act.wait_ge(sem.e_mm, c * BPC + 2 * q + 2)
                        if rep >= 1 or q >= 2:
                            act.wait_ge(sem.t3_mm, c * PAIRS + q - 1)
                        nc.scalar.copy(m.ye[:, q % 2].rearrange("p b n -> p (b n)"), ps_e[0:SEQ, q % 2]).then_inc(sem.ye_act, 1)
            act.wait_ge(sem.raw3_loaded, 16)
            for slot in range(2):
                nc.scalar.copy(m.w2H[:, slot, :, 0:SHARED], m.raw3[:]).then_inc(sem.raw_high, 1)
            segments(act, CUTS, body)

        @block.vector
        def _(dve):
            def split_x(c, rep):
                if rep >= 2:
                    dve.wait_ge(sem.h3a_mm, (c - 1) * KF1)
                for h in range(KD):
                    nc.vector.tensor_copy(m.x3H[:, c % 2, h], m.X[:, h, ds(c * CH, CH)]).then_inc(sem.x3_high, 1)
                for h in range(KD):
                    dve.wait_ge(sem.x3_high, 2 * c + h + 1)
                    nc.vector.tensor_tensor(m.x3L[:, c % 2, h], m.X[:, h, ds(c * CH, CH)],
                                            m.x3H[:, c % 2, h].bitcast(F32), ALU.subtract).then_inc(sem.x3_low, 1)

            def split_we(c, rep, b):
                dve.wait_ge(sem.we_loaded[b % 2], 16 * (4 * c + b // 2 + 1))
                if rep >= 1 or b >= 2:
                    dve.wait_ge(sem.e_mm, c * BPC + b - 1)
                nc.vector.tensor_copy(m.w2H[:, b % 2, :, SHARED:D], m.we[:, b % 2]).then_inc(sem.we_high, 1)
                dve.wait_ge(sem.we_high, c * BPC + b + 1)
                nc.vector.tensor_tensor(m.w2L[:, b % 2, :, SHARED:D], m.we[:, b % 2], m.w2H[:, b % 2, :, SHARED:D].bitcast(F32),
                                        ALU.subtract).then_inc(sem.we_low, 1)

            def body(c, rep):
                main, shared = rep < NC, rep >= 1
                if main:
                    if rep + 1 < NC:
                        split_x(c + 1, rep + 1)
                    for j in range(KF1):
                        dve.wait_ge(sem.h3a_act, c * KF1 + j + 1)
                        nc.vector.tensor_tensor(m.h3aL[:, j], m.h3aF[:, j % 4], m.h3aH[:, j].bitcast(F32), ALU.subtract)\
                          .then_inc(sem.h3a_low, 1)
                        if j < 2:
                            split_we(c, rep, j)
                if shared:
                    for j in range(KS):
                        dve.wait_ge(sem.sh_act, KS * (c - 1) + j + 1)
                        nc.vector.tensor_tensor(m.shL[:, j], m.h3aF[:, j], m.shH[:, j].bitcast(F32), ALU.subtract)\
                          .then_inc(sem.sh_low, 1)
                    route_a(c - 1, rep - 1)
                if main:
                    split_we(c, rep, 2)
                    split_we(c, rep, 3)
                if shared:
                    route_b(c - 1, rep - 1)
                    result(c - 1, 0)
                if main:
                    for b in range(4, BPC):
                        split_we(c, rep, b)
                if shared:
                    result(c - 1, 1)
                if main:
                    dve.wait_ge(sem.t3_mm, PAIRS * (c + 1))
                    nc.vector.tensor_scalar(m.zF[:, 0], ps_o[:, 0], bias(m, "c3_b2"), None, ALU.add).then_inc(sem.z_done, 1)
                    nc.vector.tensor_tensor(by_batch(m.zF[:, 1]), by_batch(ps_o[:, 1]), per_batch(m.cond3[:, ds(c * BPC, BPC)]),
                                            ALU.add).then_inc(sem.z_done, 1)
                    for h in range(KD):
                        dve.wait_ge(sem.z_done, 2 * c + h + 1)
                        nc.vector.tensor_copy(m.zH[:, h], m.zF[:, h]).then_inc(sem.z_high, 1)
                    for h in range(KD):
                        dve.wait_ge(sem.z_high, 2 * c + h + 1)
                        nc.vector.tensor_tensor(m.zL[:, h], m.zF[:, h], m.zH[:, h].bitcast(F32), ALU.subtract)\
                          .then_inc(sem.z_low, 1)

            n = [0]

            def step(c, i):
                i.then_inc(sem.rt_step, 1)
                n[0] += 1
                dve.wait_ge(sem.rt_step, c * STEPS + n[0])

            def route_a(c, rep):
                n[0] = 0
                rank = m.rank8[:].unsqueeze(1).broadcast_to([P, PAIRS, NE])
                biggest = m.rmax[:].broadcast_to([P, PAIRS, NE])

                def first_of_max(hot, x):
                    step(c, nc.vector.tensor_reduce(m.rmax[:], x[:], AX.X, ALU.max))
                    step(c, nc.vector.tensor_tensor(m.rtmp[:], x[:], biggest, ALU.is_equal))
                    step(c, nc.vector.tensor_tensor(m.rtmp[:], m.rtmp[:], rank, ALU.mult))
                    step(c, nc.vector.tensor_reduce(m.rmax[:], m.rtmp[:], AX.X, ALU.max))
                    step(c, nc.vector.tensor_tensor(hot[:], rank, biggest, ALU.is_equal))
                dve.wait_ge(sem.r_mm, c + 1)
                step(c, nc.vector.tensor_tensor(m.lgc[:], ps_e[:, 0, 0:PAIRS * NE].rearrange("p (q e) -> p q e", e=NE),
                                             m.rb[:].unsqueeze(1).broadcast_to([P, PAIRS, NE]), ALU.add))
                first_of_max(m.hac, m.lgc)
                step(c, nc.vector.scalar_tensor_tensor(m.rowc[:], m.hac[:], -3e38, m.lgc[:], ALU.mult, ALU.add))
                first_of_max(m.hbc, m.rowc)
                nc.vector.tensor_tensor(m.hsum[:], m.hac[:], m.hbc[:], ALU.add).then_inc(sem.hot_done, 1)
                at = c * PAIRS
                nc.vector.tensor_copy(m.logits[:, ds(at, PAIRS)], m.lgc[:])
                nc.vector.tensor_copy(m.hot_a[:, ds(at, PAIRS)], m.hac[:])
                nc.vector.tensor_copy(m.hot_b[:, ds(at, PAIRS)], m.hbc[:])

            def route_b(c, rep):
                at = c * PAIRS
                dve.wait_ge(sem.rank_mm, c + 1)
                for q in range(PAIRS):
                    step(c, nc.vector.tensor_tensor(m.rowc[:, q], ps_e[:, 1, ds(q * NE, NE)], m.free_row[:], ALU.add))
                    step(c, nc.vector.tensor_tensor(m.free_row[:], ps_e[:, 1, ds(32 + q * NE, NE)], m.free_row[:], ALU.add))
                step(c, nc.vector.tensor_tensor(m.rtmp[:], m.rowc[:], m.hac[:], ALU.mult))
                step(c, nc.vector.tensor_reduce(m.posf[:, :, 0:1], m.rtmp[:], AX.X, ALU.add))
                step(c, nc.vector.tensor_tensor(m.rtmp[:], m.rowc[:], m.hbc[:], ALU.mult))
                step(c, nc.vector.tensor_reduce(m.posf[:, :, 1:2], m.rtmp[:], AX.X, ALU.add))
                if rep >= 1:
                    dve.wait_ge(sem.scattered, 128 * c)
                step(c, nc.vector.tensor_copy(m.posc[:], m.posf[:]))
                nc.vector.tensor_copy(m.pos[:, ds(at, PAIRS)], m.posc[:]).then_inc(sem.pos_done, 1)
                assert n[0] == STEPS, n[0]

            def result(c, h):
                dve.wait_ge(sem.s2_mm, 2 * c + h + 1)
                x = m.X[:, h, ds(c * CH, CH)]
                nc.vector.scalar_tensor_tensor(x, ps_h[:, h], bias(m, "sb2", h), x, ALU.add, ALU.add).then_inc(sem.x4_sum, 1)
            dve.wait_ge(sem.iota_done, 2)
            nc.vector.tensor_copy(m.rank8[:], m.rank8i[:]).then_inc(sem.rank_const, 1)
            nc.vector.tensor_copy(m.free_row[:], m.base_i[:]).then_inc(sem.rank_const, 1)
            split_x(0, 0)
            dve.wait_ge(sem.r_loaded, 32)
            dve.wait_ge(sem.rank_const, 2)
            segments(dve, CUTS, body)
            dve.wait_ge(sem.x4_sum, 2 * NC)

        @block.gpsimd
        def _(pool):
            pool.iota(m.rank8i[:], pattern=[[-1, NE]], base=NE, channel_multiplier=0).then_inc(sem.iota_done, 1)
            pool.iota(m.base_i[:], pattern=[[REGION, NE]], base=0, channel_multiplier=0).then_inc(sem.iota_done, 1)
            for slot in range(2):
                pool.wait_ge(sem.raw_high, slot + 1)
                pool.tensor_tensor(m.w2L[:, slot, :, 0:SHARED], m.raw3[:], m.w2H[:, slot, :, 0:SHARED].bitcast(F32), ALU.subtract)\
                    .then_inc(sem.raw_low, 1)
            pool.memset(m.before[:], 1.0).then_inc(sem.before_done, 1)
            pool.wait_ge(sem.before_done, 1)
            pool.affine_select(out=m.before[:], in_=m.before[:], compare_op=ALU.is_gt, fill=0.0, base=0,
                               pattern=[[1, P]], channel_multiplier=-1).then_inc(sem.before_done, 1)

            for c in range(NC - 1):
                scatter(nc, pool, m, sem, z_rows, c)
            pool.wait_ge(sem.scattered, 128 * (NC - 1))


def expert_weights(nc, pool, m, d, sem, e):
    for half, src, k in ((0, d.ew1, KD), (1, d.ew2, KS)):
        i = 2 * e + half
        if i >= 3:
            pool.wait_ge(sem.ew_low, i)
        pool.dma_start(m.ew[:].rearrange("p (k n) -> p k n", k=k), src[e].rearrange("(k p) n -> p k n", p=P))\
            .then_inc(sem.ew_loaded, 16)
        hi, lo = (t[:, e, ts(half, N1)] for t in (m.ewH, m.ewL))
        pool.wait_ge(sem.ew_loaded, 16 * (i - 1))
        pool.tensor_copy(hi, m.ew[:]).then_inc(sem.ew_high, 1)
        pool.wait_ge(sem.ew_high, i + 1)
        pool.tensor_tensor(lo, m.ew[:], hi.bitcast(F32), ALU.subtract).then_inc(sem.ew_low, 1)


def layer3_tables(nc, m, d, sem, z_rows):
    W = m.work
    at = W + 136 * KB
    for name, shape, dt in (("lanef", [1], F32), ("lanei", [1], I32), ("gap", [NE], F32), ("past", [NE], F32),
                            ("sum1", [1], F32), ("tab", [2], F32), ("lane32", [1], F32), ("tabf", [2 * P], F32),
                            ("b1raw", [HS], F32), ("b2raw", [D], F32), ("b1all", [HS], F32R), ("b2all", [D], F32R)):
        place(nc, m, name, [P] + shape, dt, at)
        at += max(32, 4 * shape[0] * (shape[1] if len(shape) > 1 else 1))
    assert at <= W + 150 * KB
    at = W + 120 * KB
    for name, shape, dt in (("prob", [NTILE, NE], F32), ("rt2", [NTILE, NE], F32), ("rt", [NTILE, 1], F32), ("tiles", [NE], F32),
                            ("upto", [NE], F32), ("base_f", [NE], F32), ("shift", [NE], F32), ("posw", [NTILE, 2], F32)):
        place(nc, m, name, [P] + shape, dt, at)
        at += 4 * shape[0] * (shape[1] if len(shape) > 1 else 1)
    place(nc, m, "zeros", [P, D], F32, W + 150 * KB)
    place(nc, m, "b1t", [40, HS], F32R, W + 155 * KB)
    place(nc, m, "sel", [40, 4, P], F32R, W + 157 * KB)
    place(nc, m, "b2t", [40, D], F32R, W + 159 * KB)
    place(nc, m, "hot_t", [40, P], F32, W + 160 * KB)
    place(nc, m, "pad_i", [1, NE], I32, W + 160 * KB + 512)
    place(nc, m, "tabi", [1, 2 * P], I32, W + 161 * KB)
    place(nc, m, "ewH", [P, NE, NW], F32R, W)
    place(nc, m, "ewL", [P, NE, NW], F32R, W + 64 * KB)
    place(nc, m, "ew", [P, 1024], F32, W + 151 * KB)

    def wide(t):
        return t[:].broadcast_to([P, NTILE, NE])

    def pads(eng, experts):
        for e in experts:
            row = eng.value_load(m.pad_i[0:1, e:e + 1], min_val=e * REGION, max_val=e * REGION + T)
            eng.dma_start(z_rows[ds(row, P), :], m.zeros[:]).then_inc(sem.padded, 16)

    with nc.psum_tensor("l3_tab", [P, CH], F32) as ps, nc.Block() as block:
        @block.gpsimd
        def _(pool):
            pool.memset(m.zeros[:], 0.0).then_inc(sem.zeros_done, 1)
            pool.iota(m.lanei[:], pattern=[[0, 1]], base=0, channel_multiplier=1).then_inc(sem.tab_pool, 1)
            pool.memset(m.b1raw[0:40, :], 0.0).then_inc(sem.tab_pool, 1)
            pool.memset(m.b2raw[0:40, :], 0.0).then_inc(sem.tab_pool, 1)
            scatter(nc, pool, m, sem, z_rows, NC - 1)
            pool.wait_ge(sem.scattered, 128 * NC)

        @block.scalar
        def _(act):
            act.wait_ge(sem.ew0_loaded, 32)
            nc.scalar.copy(m.ewH[:, 0], m.ew0[:]).then_inc(sem.ew_high, 2)
            act.wait_ge(sem.rt_dve, 2)
            nc.scalar.activation(m.prob[:], m.prob[:], ACT.Exp).then_inc(sem.rt_exp, 1)
            act.wait_ge(sem.zeros_done, 1)
            act.wait_ge(sem.tab_done, 2)
            pads(act, range(1, NE, 2))

        @block.tensor
        def _(pe):
            pe.wait_ge(sem.tab_done, 1)
            for i in range(2):
                last = nc.tensor.transpose(ps[0:1, ts(i, P)], m.tab[:, i:i + 1], m.ident[:])
            last.then_inc(sem.tab_mm, 1)
            pe.wait_ge(sem.tab_done, 2)
            nc.tensor.matmul(ps[0:40, 256:384], m.ones1[0:1, 0:40], m.tabf[0:1, 0:P], start=True, stop=True).then_inc(sem.tab_mm, 1)

        @block.vector
        def _(dve):
            n = [0]

            def step(i):
                i.then_inc(sem.rt_dve, 1)
                n[0] += 1
                dve.wait_ge(sem.rt_dve, n[0])
            step(nc.vector.tensor_reduce(m.rt[:], m.logits[:], AX.X, ALU.max))
            step(nc.vector.tensor_tensor(m.prob[:], m.logits[:], wide(m.rt), ALU.subtract))
            step(nc.vector.tensor_copy(m.base_f[:], m.base_i[:]))
            step(nc.vector.tensor_tensor(m.tiles[:], m.free_row[:], m.base_f[:], ALU.subtract))
            step(nc.vector.tensor_scalar(m.tiles[:], m.tiles[:], 1.0 / P, 0.5 - 0.5 / P, ALU.mult, ALU.add))
            step(nc.vector.tensor_scalar(m.tiles[:], m.tiles[:], MAGIC, None, ALU.add))
            step(nc.vector.tensor_scalar(m.tiles[:], m.tiles[:], MAGIC, None, ALU.subtract))
            step(nc.vector.tensor_copy(m.pad_i[:], m.free_row[0:1, :]))
            step(nc.vector.tensor_copy(m.upto[:], m.tiles[:]))
            for e in range(1, NE):
                step(nc.vector.tensor_tensor(m.upto[:, e:e + 1], m.upto[:, e:e + 1], m.upto[:, e - 1:e], ALU.add))
            step(nc.vector.tensor_scalar(m.gap[:], m.tiles[:], -float(P), float(REGION), ALU.mult, ALU.add))
            dve.wait_ge(sem.tab_pool, 3)
            step(nc.vector.tensor_copy(m.lanef[:], m.lanei[:]))
            step(nc.vector.tensor_scalar(m.past[:], m.upto[:], m.lanef[:], None, ALU.is_le))
            step(nc.vector.tensor_reduce(m.sum1[:], m.past[:], AX.X, ALU.add))
            step(nc.vector.tensor_scalar(m.tab[:, 0:1], m.sum1[:], float(NE - 1), None, ALU.min))
            step(nc.vector.tensor_tensor(m.past[:], m.past[:], m.gap[:], ALU.mult))
            step(nc.vector.tensor_reduce(m.sum1[:], m.past[:], AX.X, ALU.add))
            nc.vector.scalar_tensor_tensor(m.tab[:, 1:2], m.lanef[:], float(P), m.sum1[:], ALU.mult, ALU.add)\
              .then_inc(sem.tab_done, 1)
            dve.wait_ge(sem.tab_mm, 1)
            nc.vector.tensor_copy(m.tabi[:], ps[0:1, 0:2 * P])
            nc.vector.tensor_copy(m.tabf[0:1, :], ps[0:1, 0:2 * P]).then_inc(sem.tab_done, 1)
            step(nc.vector.tensor_copy(m.lane32[:], m.lanef[:]))
            step(nc.vector.tensor_scalar(m.lane32[32:64, :], m.lanef[32:64, :], 32.0, None, ALU.subtract))
            dve.wait_ge(sem.tab_mm, 2)
            step(nc.vector.tensor_scalar(m.hot_t[:], ps[0:40, 256:384], m.lane32[0:40, :], None, ALU.is_equal))
            dve.wait_ge(sem.ew_high, 2)
            nc.vector.tensor_tensor(m.ewL[:, 0], m.ew0[:], m.ewH[:, 0].bitcast(F32), ALU.subtract).then_inc(sem.ew_low, 2)
            dve.wait_ge(sem.eb_loaded, 64)
            for raw, all_, t in ((m.b1raw, m.b1all, m.b1t), (m.b2raw, m.b2all, m.b2t)):
                step(nc.vector.tensor_copy(all_[0:40, :], raw[0:40, :]))
                step(nc.vector.tensor_copy(t[:], raw[0:40, :]))
                step(nc.vector.tensor_tensor(t[32:40, :], raw[32:40, :], all_[32:40, :].bitcast(F32), ALU.subtract))

        @block.sync
        def _(sp):
            sp.wait_ge(sem.tab_pool, 3)
            for raw, src in ((m.b1raw, d.eb1), (m.b2raw, d.eb2)):
                for at in (0, 32):
                    sp.dma_start(raw[at:at + NE, :], src).then_inc(sem.eb_loaded, 16)
            sp.wait_ge(sem.zeros_done, 1)
            sp.dma_start(z_rows[SPARE:SPARE + NE * P, :].rearrange("(e p) n -> p e n", p=P),
                         m.zeros[:].unsqueeze(1).broadcast_to([P, NE, D])).then_inc(sem.padded, 16)
            sp.wait_ge(sem.tab_done, 2)
            pads(sp, range(0, NE, 2))
            sp.wait_ge(sem.padded, 16 * (NE + 1))


LATE = (0, 7, 17)


def weights_by_token(nc, dve, m, sem, part):
    wide = m.rt[:].broadcast_to([P, NTILE, NE])
    n = [LATE[part]]

    def step(i):
        i.then_inc(sem.late_dve, 1)
        n[0] += 1
        dve.wait_ge(sem.late_dve, n[0])
    if part == 0:
        step(nc.vector.tensor_reduce(m.rt[:], m.prob[:], AX.X, ALU.add))
        step(nc.vector.reciprocal(m.rt[:], m.rt[:]))
        step(nc.vector.tensor_tensor(m.prob[:], m.prob[:], wide, ALU.mult))
        for i, hot in enumerate((m.hot_a, m.hot_b)):
            step(nc.vector.tensor_tensor(m.rt2[:], m.prob[:], hot[:], ALU.mult))
            step(nc.vector.tensor_reduce(m.pw[:, :, i:i + 1], m.rt2[:], AX.X, ALU.add))
    else:
        step(nc.vector.tensor_tensor(m.shift[:], m.upto[:], m.tiles[:], ALU.subtract))
        step(nc.vector.scalar_tensor_tensor(m.shift[:], m.shift[:], float(P), m.base_f[:], ALU.mult, ALU.subtract))
        step(nc.vector.tensor_copy(m.posw[:], m.pos[:]))
        for i, hot in enumerate((m.hot_a, m.hot_b)):
            step(nc.vector.tensor_tensor(m.rt2[:], m.shift[:].unsqueeze(1).broadcast_to([P, NTILE, NE]), hot[:], ALU.mult))
            step(nc.vector.tensor_reduce(m.rt[:], m.rt2[:], AX.X, ALU.add))
            step(nc.vector.tensor_tensor(m.posw[:, :, i:i + 1], m.posw[:, :, i:i + 1], m.rt[:], ALU.add))
        step(nc.vector.tensor_copy(m.pos[:], m.posw[:]))
    assert n[0] == LATE[part + 1]


def layer3_experts(nc, m, d, sem, z_rows, e_rows):
    W = m.work
    place(nc, m, "zr", [P, 4, D], F32, W + 128 * KB)
    place(nc, m, "zxH", [P, 2, KD, P], F32R, W + 132 * KB)
    place(nc, m, "zxL", [P, 2, KD, P], F32R, W + 134 * KB)
    place(nc, m, "ehF", [P, 2, HS], F32, W + 136 * KB)
    place(nc, m, "exH", [P, 2, KS, P], F32R, W + 140 * KB)
    place(nc, m, "exL", [P, 2, KS, P], F32R, W + 144 * KB)
    place(nc, m, "eo", [P, 2, D], F32, W + 148 * KB)
    FOURS = [0, 1, 2, NSLOT // 4 - 1, NSLOT // 4, NSLOT // 4 + 1]

    def steps(eng, body, cuts=FOURS):
        segments(eng, cuts, lambda s, rep: [body(4 * s + u, 4 * rep + u, s) for u in range(4)])

    with nc.psum_tensor("ex_z", [P, CH], F32) as ps_z, nc.psum_tensor("ex_h", [P, 2, CH], F32) as ps_h, \
            nc.psum_tensor("ex_x", [P, 2, CH], F32) as ps_x, nc.psum_tensor("ex_o", [P, 2, CH], F32) as ps_o, \
            nc.Block() as block:

        @block.sync
        def _(sp):
            def rows(t, rep):
                row = sp.value_load(m.tabi[0:1, ds(t + P, 1)], min_val=0, max_val=SPARE + (NE - 1) * P)
                if rep >= 4:
                    sp.wait_ge(sem.zx_mm, t - 3)
                row = apart(sp, row)
                sp.dma_start(m.zr[:, rep % 4], z_rows[ds(row, P), :]).then_inc(sem.zr_loaded[rep % 4], 16)
            segments(sp, [0, 1, NSLOT // 4], lambda s, rep: [rows(4 * s + u, 4 * rep + u) for u in range(4)])

        @block.gpsimd
        def _(pool):
            for e in range(1, NE):
                if e == NE - 2:
                    pool.wait_ge(sem.ew_low, 2)
                    pool.wait_ge(sem.late_dve, LATE[2])
                expert_weights(nc, pool, m, d, sem, e)

        @block.tensor
        def _(pe):
            def turn_in(t, rep, turn):
                pe.wait_ge(sem.zr_loaded[rep % 4], 16 * (turn + 1))
                if rep >= 1:
                    pe.wait_ge(sem.zx_low, t)
                for k in range(KD):
                    last = nc.tensor.transpose(ps_z[:, ts(k, P)], m.zr[:, rep % 4, ts(k, P)], m.ident[:])
                last.then_inc(sem.zx_mm, 1)

            def first(t, rep):
                e = pe.value_load(m.tabi[0:1, ds(t, 1)], min_val=0, max_val=NE - 1)
                pe.wait_ge(sem.ew_low, e * 2 + 2)
                pe.wait_ge(sem.zx_low, t + 1)
                if rep >= 2:
                    pe.wait_ge(sem.eh_act, t - 1)
                nc.tensor.matmul(ps_h[:, rep % 2], m.sel[:, rep % 4], m.b1t[:], start=True, stop=False)
                for k in range(KD):
                    w = [t_[:, ds(e, 1), ts(k, HS)].rearrange("p o n -> p (o n)") for t_ in (m.ewH, m.ewL)]
                    last = products(nc, ps_h[:, rep % 2], [x[:, rep % 2, k] for x in (m.zxH, m.zxL)], w, False, k == KD - 1)
                last.then_inc(sem.eh_mm, 1)

            def turn_hidden(t, rep):
                pe.wait_ge(sem.eh_act, t + 1)
                if rep >= 2:
                    pe.wait_ge(sem.ex_low, t - 1)
                for k in range(KS):
                    last = nc.tensor.transpose(ps_x[:, rep % 2, ts(k, P)], m.ehF[:, rep % 2, ts(k, P)], m.ident[:])
                last.then_inc(sem.ex_mm, 1)

            def second(t, rep):
                e = pe.value_load(m.tabi[0:1, ds(t, 1)], min_val=0, max_val=NE - 1)
                pe.wait_ge(sem.ex_low, t + 1)
                if rep >= 2:
                    pe.wait_ge(sem.eo_out, t - 1)
                nc.tensor.matmul(ps_o[:, rep % 2, 0:D], m.sel[:, rep % 4], m.b2t[:], start=True, stop=False)
                for k in range(KS):
                    w = [t_[:, ds(e, 1), N1 + k * D:N1 + (k + 1) * D].rearrange("p o n -> p (o n)") for t_ in (m.ewH, m.ewL)]
                    last = products(nc, ps_o[:, rep % 2, 0:D], [x[:, rep % 2, k] for x in (m.exH, m.exL)], w, False, k == KS - 1)
                last.then_inc(sem.eo_mm, 1)

            def body(t, rep, turn):
                if rep + 1 < NSLOT:
                    turn_in(t + 1, rep + 1, turn + (rep % 4 + 1) // 4)
                if rep < NSLOT:
                    first(t, rep)
                if within(rep - 1, 0, NSLOT):
                    turn_hidden(t - 1, rep - 1)
                if within(rep - 2, 0, NSLOT):
                    second(t - 2, rep - 2)
            turn_in(0, 0, 0)
            steps(pe, body)

        @block.scalar
        def _(act):
            def store(t, rep):
                act.wait_ge(sem.eo_out, t + 1)
                t = apart(act, t)
                act.dma_start(e_rows[ds(t * P, P), :], m.eo[:, rep % 2]).then_inc(sem.eo_stored[rep % 2], 16)

            def body(t, rep, turn):
                if rep < NSLOT:
                    act.wait_ge(sem.eh_mm, t + 1)
                    if rep >= 2:
                        act.wait_ge(sem.ex_mm, t - 1)
                    nc.scalar.activation(m.ehF[:, rep % 2], ps_h[:, rep % 2], ACT.Gelu).then_inc(sem.eh_act, 1)
                if within(rep - 1, 0, NSLOT):
                    i = t - 1
                    act.wait_ge(sem.ex_mm, i + 1)
                    if rep - 1 >= 2:
                        act.wait_ge(sem.eo_mm, i - 1)
                    nc.scalar.copy(m.exH[:, (rep - 1) % 2].rearrange("p k n -> p (k n)"), ps_x[:, (rep - 1) % 2]).then_inc(sem.ex_high, 1)
                if within(rep - 3, 0, NSLOT):
                    store(t - 3, rep - 3)
            steps(act, body)
            for u in range(2):
                act.wait_ge(sem.eo_stored[u], 16 * (NSLOT // 2))

        @block.vector
        def _(dve):
            def turned(t, rep):
                dve.wait_ge(sem.zx_mm, t + 1)
                if rep >= 2:
                    dve.wait_ge(sem.eh_mm, t - 1)
                nc.vector.tensor_copy(m.zxH[:, rep % 2].rearrange("p k n -> p (k n)"), ps_z[:, 0:D]).then_inc(sem.zx_high, 1)
                if rep >= 4:
                    dve.wait_ge(sem.eo_mm, t - 3)
                c = apart(dve, t)
                nc.vector.tensor_copy(m.sel[:, rep % 4], m.hot_t[:, ds(c, 1)].broadcast_to([40, P]))
                dve.wait_ge(sem.zx_high, t + 1)
                nc.vector.tensor_tensor(m.zxL[:, rep % 2].rearrange("p k n -> p (k n)"), ps_z[:, 0:D],
                                        m.zxH[:, rep % 2].rearrange("p k n -> p (k n)").bitcast(F32), ALU.subtract)\
                  .then_inc(sem.zx_low, 1)

            def body(t, rep, turn):
                if rep + 1 < NSLOT:
                    turned(t + 1, rep + 1)
                if within(rep - 1, 0, NSLOT):
                    i, r = t - 1, (rep - 1) % 2
                    dve.wait_ge(sem.ex_high, i + 1)
                    nc.vector.tensor_tensor(m.exL[:, r].rearrange("p k n -> p (k n)"), ps_x[:, r],
                                            m.exH[:, r].rearrange("p k n -> p (k n)").bitcast(F32), ALU.subtract)\
                      .then_inc(sem.ex_low, 1)
                if within(rep - 2, 0, NSLOT):
                    i, r = t - 2, (rep - 2) % 2
                    dve.wait_ge(sem.eo_mm, i + 1)
                    if rep - 2 >= 2:
                        dve.wait_ge(sem.eo_stored[r], 16 * (2 * turn + (rep % 4 - 2) // 2))
                    nc.vector.tensor_copy(m.eo[:, r], ps_o[:, r, 0:D]).then_inc(sem.eo_out, 1)
            turned(0, 0)
            steps(dve, body, FOURS[:2])
            weights_by_token(nc, dve, m, sem, 0)
            steps(dve, body, FOURS[1:3])
            weights_by_token(nc, dve, m, sem, 1)
            steps(dve, body, FOURS[2:])

def layer3_combine(nc, m, d, sem, e_rows, out):
    W = m.work
    place(nc, m, "ra_rows", [P, 4, D], F32, W)
    place(nc, m, "rb_rows", [P, 4, D], F32, W + 4 * KB)
    place(nc, m, "xc", [P, 4, KD, P], F32, W + 8 * KB)
    place(nc, m, "res", [P, 4, D], F32, W + 12 * KB)

    def steps(eng, body):
        segments(eng, [0, 1, NTILE // 4], lambda s, rep: [body(4 * s + u, 4 * rep + u, s) for u in range(4)])

    with nc.psum_tensor("co_x", [P, 4, CH], F32) as ps, nc.Block() as block:
        @block.gpsimd
        def _(pool):
            for t in range(NTILE):
                if t >= 4:
                    pool.wait_ge(sem.co_sum, 2 * (t - 3))
                for k, rows in enumerate((m.ra_rows, m.rb_rows)):
                    pool.indirect_dma_start(rows[:, t % 4], None, e_rows, bass.IndirectOffsetOnAxis(ap=m.pos[:, t, k:k + 1], axis=0))\
                      .then_inc(sem.gathered[t % 4], 16)

        @block.scalar
        def _(act):
            def body(t, rep, turn):
                if rep >= 4:
                    act.wait_ge(sem.co_mm, t - 3)
                t = apart(act, t)
                nc.scalar.copy(m.xc[:, rep % 4], m.X[:, :, ds(t * P, P)]).then_inc(sem.co_copy, 1)
            steps(act, body)

        @block.tensor
        def _(pe):
            def body(t, rep, turn):
                pe.wait_ge(sem.co_copy, t + 1)
                if rep >= 4:
                    pe.wait_ge(sem.co_sum, 2 * (t - 3))
                for h in range(KD):
                    last = nc.tensor.transpose(ps[:, rep % 4, ts(h, P)], m.xc[:, rep % 4, h], m.ident[:])
                last.then_inc(sem.co_mm, 1)
            steps(pe, body)

        @block.vector
        def _(dve):
            def body(t, rep, turn):
                u = rep % 4
                if rep >= 4:
                    dve.wait_ge(sem.co_stored[u], 16 * turn)
                dve.wait_ge(sem.gathered[u], 32 * (turn + 1))
                dve.wait_ge(sem.co_mm, t + 1)
                c = apart(dve, t)
                nc.vector.scalar_tensor_tensor(m.res[:, u], m.ra_rows[:, u], m.pw[:, ds(c, 1), 0:1].rearrange("p a b -> p (a b)"),
                                               ps[:, u, 0:D], ALU.mult, ALU.add).then_inc(sem.co_sum, 1)
                dve.wait_ge(sem.co_sum, 2 * t + 1)
                c = apart(dve, t)
                nc.vector.scalar_tensor_tensor(m.res[:, u], m.rb_rows[:, u], m.pw[:, ds(c, 1), 1:2].rearrange("p a b -> p (a b)"),
                                               m.res[:, u], ALU.mult, ALU.add).then_inc(sem.co_sum, 1)
            steps(dve, body)

        @block.sync
        def _(sp):
            def body(t, rep, turn):
                sp.wait_ge(sem.co_sum, 2 * t + 2)
                t = apart(sp, t)
                sp.dma_start(out[ds(t * P, P), :], m.res[:, rep % 4]).then_inc(sem.co_stored[rep % 4], 16)
            steps(sp, body)
            for u in range(4):
                sp.wait_ge(sem.co_stored[u], 16 * (NTILE // 4))


L0_SEMS = """ids_loaded prep_pool prep_load prep_pe prep_hot prep_dve tok_mm tok_act y_added turn_mm yh_cond yl_cond yh_upd
yl_upd h1_act h1_mm g_act sums g_mm h1_low h2_act h2_mm h2_low h3_act h3_mm h3_low th_act th_mm coupl_b
cs_done t1_done t0_done y_upd x1_sum""".split()
L1_SEMS = """raw_loaded du_c_pool w1_loaded l1_const lap du_a lap_mm win_q win_t win_m win_mm du_u us_edge du_d du_c w1_scale wout_m w1_clip
wout_q w1_dve w1_rec us_mid du_b du_done du_max q_done hid_act hid_mm q_int q_high q_dve hid_max g_round g_mm1
x2_sum o1_act g_scaled g_high g_low g_low_pool g_round_odd g_clip""".split()
L2_SEMS = """tok2_mm xs_copied tok2_act y2_added turn2_mm y2_low h2a_act h2a_mm w2_low w2_low_pool x3_sum h2a_low o2_mm
w2_high y2_high w2_high_pool w3_low w3_high""".split()
L3_SEMS = """pos_done zt_act scattered raw3_loaded r_loaded we_low h3a_mm ew0_loaded x3_low h3a_act x4_sum sh_act z_low
sh_mm before_done ye_act r_mm zt_mm rt_step hot_done rank_mm raw_low h3a_low e_mm sh_low s2_mm t3_mm raw_high
x3_high we_high z_done z_high iota_done rank_const ew_low ew_loaded ew_high zeros_done tab_pool rt_dve rt_exp
tab_done tab_mm eb_loaded padded late_dve zx_mm zx_low eh_act eh_mm ex_low ex_mm eo_out eo_mm ex_high zx_high
co_sum co_mm co_copy""".split()


INPUTS = {
    "xT": "x", "ids0": "itok_B_0_7", "ids2": "itok_B_0_30", "zs": ("condB_zX", "condB_zY", "condB_zR"),
    "scalars": ("L0_ffn_adaptive_range", "L0_ffn_cn_b4", "L0_ffn_gc_b3"), "lastcols": ("L0_ffn_cn_w4", "L0_ffn_gc_w3"),
    "rows": ("L0_ffn_cn_b1", "L0_ffn_cn_b2", "L0_ffn_cn_b3", "L0_ffn_gc_b1", "L0_ffn_gc_b2", "L1_ffn_b_in", "L1_ffn_b_out",
             "L2_ffn_b1", "L2_ffn_b2", "L3_cond_b1", "L3_cond_b2", "L3_ffn_sb1", "L3_ffn_sb2"),
    "c0_wT": "L0_cond_weight", "c0_b": "L0_cond_bias", "cn_w1": "L0_ffn_cn_w1", "cn_w2": "L0_ffn_cn_w2",
    "cn_w3": "L0_ffn_cn_w3", "gc_w1": "L0_ffn_gc_w1", "gc_w2": "L0_ffn_gc_w2",
    "w_inT": "L1_ffn_W_in", "w_out": "L1_ffn_W_out", "c2_w": "L2_cond_W", "c2_b": "L2_cond_b",
    "f2_w1": "L2_ffn_w1", "f2_w2": "L2_ffn_w2", "c3_w1": "L3_cond_W1", "c3_w2": "L3_cond_W2",
    "we": "L3_cond_We", "be": "L3_cond_be", "rw": "L3_ffn_router_w", "rb": "L3_ffn_router_b",
    "sw1": "L3_ffn_sw1", "sw2": "L3_ffn_sw2", "ew1": "L3_ffn_rw1", "eb1": "L3_ffn_rb1", "ew2": "L3_ffn_rw2", "eb2": "L3_ffn_rb2",
}


def acquire(nc, sem, names, groups=()):
    for name in names:
        sem[name] = nc.alloc_semaphore(name)
    for name, n in groups:
        sem[name] = [nc.alloc_semaphore(f"{name}{i}") for i in range(n)]


def retire(nc, sem):
    for s in list(sem.values()):
        nc.clear_and_free_semaphores(s if isinstance(s, list) else [s])
    sem.clear()
    nc.all_engine_barrier()


def build(nc, d, out):
    sem, m = Names(), Names()
    common_memory(nc, m)
    acquire(nc, sem, L0_SEMS + L1_SEMS, (("x_loaded", NC), ("cw_loaded", SLOTS), ("red_mm", 2), ("red_v", 2)))
    prepare(nc, m, d, sem)
    layer0(nc, m, d, sem)
    layer1(nc, m, d, sem)
    retire(nc, sem)
    acquire(nc, sem, L2_SEMS + L3_SEMS, (("cw2_loaded", BPC), ("w3_loaded", 2), ("we_loaded", 2), ("zr_loaded", 4), ("gathered", 4),
                                         ("eo_stored", 2), ("co_stored", 4)))
    layer2(nc, m, d, sem)
    z_rows = nc.dram_tensor("z_rows", (SPARE + NE * P, D), F32).ap()
    e_rows = nc.dram_tensor("e_rows", (NSLOT * P, D), F32).ap()
    layer3_shared(nc, m, d, sem, z_rows)
    layer3_tables(nc, m, d, sem, z_rows)
    layer3_experts(nc, m, d, sem, z_rows, e_rows)
    layer3_combine(nc, m, d, sem, e_rows, out)


def lay_out(name, inputs):
    import numpy as np
    source = INPUTS[name]
    if name == "rows":
        rows = np.zeros((NROWS, P), np.float32)
        for (bias_name, n), x in zip(BIASES, source):
            at = ROWS[bias_name] * P
            rows.reshape(-1)[at:at + n] = np.asarray(inputs[x])
        return rows
    if name == "lastcols":
        return np.concatenate([np.asarray(inputs[x]) for x in source], axis=1)
    if not isinstance(source, str):
        return np.concatenate([np.asarray(inputs[x]) for x in source])
    a = np.asarray(inputs[source])
    if name == "xT":
        a = a.reshape(T, D).T
    if name == "c0_wT":
        a = a.transpose(0, 2, 1)
    if name == "w_inT":
        a = a.T
    return np.ascontiguousarray(a)


def kernel(**inputs):
    import numpy as np
    import concourse.bacc as bacc
    from concourse.bass_utils import run_bass_kernel_spmd

    nc = bacc.Bacc("TRN2", target_bir_lowering=False, num_devices=1)
    arrays, aps = {}, {}
    for name in INPUTS:
        a = lay_out(name, inputs)
        arrays["in_" + name] = a
        aps[name] = nc.dram_tensor("in_" + name, a.shape, mybir.dt.from_np(a.dtype), kind="ExternalInput").ap()
    out = nc.dram_tensor("out_0", (T, D), F32, kind="ExternalOutput").ap()
    build(nc, Names(aps), out)
    result = run_bass_kernel_spmd(nc, [arrays], core_ids=[0])
    return result.results[0]["out_0"].reshape(BATCH, SEQ, D)
```
